# Optimizing a Trainium2 kernel written in Bass

```python
import numpy as np
import jax
import jax.numpy as jnp

def _softmax(x, axis=-1):
    return jax.nn.softmax(x, axis=axis)

def _gelu(x):
    return jax.nn.gelu(x, approximate=True)

def _silu(x):
    return jax.nn.silu(x)

def _sigmoid(x):
    return jax.nn.sigmoid(x)

def _layernorm(x, axis=-1, eps=1e-05):
    m = jnp.mean(x, axis=axis, keepdims=True)
    v = jnp.var(x, axis=axis, keepdims=True)
    return (x - m) / jnp.sqrt(v + eps)

def _scatter_add(tgt, idx, src, axis=0):
    return tgt.at[idx].add(src)

def _segment_sum(src, seg, n):
    return jax.ops.segment_sum(src, seg, n)
kernel_name = 'mk_recurrent_d2_jaxref_r8_9bb7ad'

def setup_inputs(seed: int=0):
    np.random.seed(seed)
    _w = jnp.asarray

    def _L0_attn_setup():
        import jax, jax.numpy as jnp
        import numpy as np
        D_MODEL = 128
        D_STATE = 32
        EXPAND = 2
        D_INNER = D_MODEL * EXPAND
        B_SZ = 2
        SEQ = 64

        def _forward(x, W_in, A_log, W_B, W_C, W_dt, b_dt, dt_bias, rope_freq, ln_w, ln_b, W_out):
            B, L, _ = x.shape
            half = D_STATE // 2
            offset = 0
            xz = jnp.einsum('bld,ed->ble', x, W_in)
            x_inner = xz[..., :D_INNER]
            z = jax.nn.silu(xz[..., D_INNER:])
            A = -jnp.exp(A_log)
            Bm = jnp.einsum('bld,nd->bln', x, W_B)
            Cm = jnp.einsum('bld,nd->bln', x, W_C)
            dt = jax.nn.softplus(jnp.einsum('bld,ed->ble', x, W_dt) + b_dt + dt_bias)
            dtA = dt[..., None] * A
            denom = 1.0 - dtA / 2.0
            A_bar = (1.0 + dtA / 2.0) / denom
            B_bar = dt[..., None] / denom
            t_idx = jnp.arange(L, dtype=jnp.float32) + offset
            ang = t_idx[:, None] * rope_freq
            cos_a = jnp.cos(ang)
            sin_a = jnp.sin(ang)

            def step(state, inp):
                A_t, Bb_t, B_t, x_t, C_t, c_t, s_t = inp
                state = A_t * state + Bb_t * B_t[:, None, :] * x_t[:, :, None]
                real = state[..., :half]
                imag = state[..., half:]
                state = jnp.concatenate([real * c_t - imag * s_t, real * s_t + imag * c_t], axis=-1)
                y_t = jnp.einsum('bds,bs->bd', state, C_t)
                return (state, y_t)
            state0 = jnp.zeros((B, D_INNER, D_STATE), dtype=x.dtype)
            xs = (jnp.swapaxes(A_bar, 0, 1), jnp.swapaxes(B_bar, 0, 1), jnp.swapaxes(Bm, 0, 1), jnp.swapaxes(x_inner, 0, 1), jnp.swapaxes(Cm, 0, 1), cos_a, sin_a)
            final_state, ys = jax.lax.scan(step, state0, xs)
            out = jnp.swapaxes(ys, 0, 1) * z
            mu = jnp.mean(out, axis=-1, keepdims=True)
            var = jnp.mean((out - mu) ** 2, axis=-1, keepdims=True)
            out = (out - mu) * jax.lax.rsqrt(var + 1e-05) * ln_w + ln_b
            out = jnp.einsum('ble,de->bld', out, W_out)
            return (out, final_state)

        def _reference_tuple_inner(x, W_in, A_log, W_B, W_C, W_dt, b_dt, dt_bias, rope_freq, ln_w, ln_b, W_out):
            return _forward(x, W_in, A_log, W_B, W_C, W_dt, b_dt, dt_bias, rope_freq, ln_w, ln_b, W_out)
        key = jax.random.key(seed)
        ks = jax.random.split(key, 10)
        x = jax.random.normal(ks[0], (B_SZ, SEQ, D_MODEL), dtype=jnp.float32)
        W_in = jax.random.normal(ks[1], (2 * D_INNER, D_MODEL), dtype=jnp.float32) * 0.02
        A_log = jax.random.uniform(ks[2], (D_INNER, D_STATE), minval=-4.0, maxval=-1.0, dtype=jnp.float32)
        W_B = jax.random.normal(ks[3], (D_STATE, D_MODEL), dtype=jnp.float32) * 0.02
        W_C = jax.random.normal(ks[4], (D_STATE, D_MODEL), dtype=jnp.float32) * 0.02
        W_dt = jax.random.normal(ks[5], (D_INNER, D_MODEL), dtype=jnp.float32) * 0.02
        b_dt = jnp.zeros((D_INNER,), dtype=jnp.float32)
        dt_bias = jnp.zeros((D_INNER,), dtype=jnp.float32) - 4.0
        rope_freq = jax.random.normal(ks[6], (D_STATE // 2,), dtype=jnp.float32) * 0.01
        ln_w = jnp.ones((D_INNER,), dtype=jnp.float32)
        ln_b = jnp.zeros((D_INNER,), dtype=jnp.float32)
        W_out = jax.random.normal(ks[7], (D_MODEL, D_INNER), dtype=jnp.float32) * 0.02
        return {'x': x, 'W_in': W_in, 'A_log': A_log, 'W_B': W_B, 'W_C': W_C, 'W_dt': W_dt, 'b_dt': b_dt, 'dt_bias': dt_bias, 'rope_freq': rope_freq, 'ln_w': ln_w, 'ln_b': ln_b, 'W_out': W_out}
    _L0_attn_in = _L0_attn_setup()

    def _L0_ffn_setup():
        import jax, jax.numpy as jnp
        import numpy as np
        NUM_GROUPS = 2
        EXPERT_CAPACITY = 80
        NUM_SELECTED = 2
        key = jax.random.key(seed)
        k1, k2, k3, k4 = jax.random.split(key, 4)
        B, S, H, E, F = (4, 256, 128, 8, 512)
        return {'input_emb': jax.random.normal(k1, (B, S, H), dtype=jnp.float32), 'w_router': jax.random.normal(k2, (H, E), dtype=jnp.float32) * 0.02, 'wi': jax.random.normal(k3, (E, H, F), dtype=jnp.float32) * 0.02, 'wo': jax.random.normal(k4, (E, F, H), dtype=jnp.float32) * 0.02}
    _L0_ffn_in = _L0_ffn_setup()

    def _L1_attn_setup():
        import jax, jax.numpy as jnp
        import numpy as np
        D_MODEL = 128
        NUM_HEADS = 16
        D_K = D_MODEL // NUM_HEADS
        ROPE_THETA = 10000.0
        MAX_SEQ_LEN = 256

        def _rope_tables():
            dim_index = jnp.arange(D_K // 2, dtype=jnp.float32)
            pos = jnp.arange(MAX_SEQ_LEN, dtype=jnp.float32)
            theta_inv = ROPE_THETA ** (-2.0 * dim_index / D_K)
            ang = pos[:, None] * theta_inv[None, :]
            return (jnp.sin(ang), jnp.cos(ang))

        def _apply_rope(x, positions, sin, cos):
            s = sin[positions]
            c = cos[positions]
            x_even = x[..., ::2]
            x_odd = x[..., 1::2]
            y_even = x_even * c - x_odd * s
            y_odd = x_even * s + x_odd * c
            y = jnp.stack([y_even, y_odd], axis=-1)
            return y.reshape(x.shape)
        key = jax.random.key(seed)
        k0, k1, k2, k3, k4 = jax.random.split(key, 5)
        std = np.sqrt(2.0 / (D_MODEL + D_MODEL))
        in_features = jax.random.normal(k0, (2, 256, D_MODEL), dtype=jnp.float32)
        W_q = jax.random.normal(k1, (D_MODEL, D_MODEL), dtype=jnp.float32) * std
        W_k = jax.random.normal(k2, (D_MODEL, D_MODEL), dtype=jnp.float32) * std
        W_v = jax.random.normal(k3, (D_MODEL, D_MODEL), dtype=jnp.float32) * std
        W_o = jax.random.normal(k4, (D_MODEL, D_MODEL), dtype=jnp.float32) * std
        return {'in_features': in_features, 'W_q': W_q, 'W_k': W_k, 'W_v': W_v, 'W_o': W_o}
    _L1_attn_in = _L1_attn_setup()

    def _L1_ffn_setup():
        import jax, jax.numpy as jnp
        import numpy as np
        N_HEADS = 4
        key = jax.random.key(seed)
        k1, k2, k3, k4 = jax.random.split(key, 4)
        dmodel, n_experts, expert_size = (128, 64, 128)
        B, S = (4, 256)
        x = jax.random.normal(k1, (B, S, dmodel), dtype=jnp.float32)
        expert_sel = jax.random.normal(k2, (n_experts, dmodel), dtype=jnp.float32) * dmodel ** (-0.5)
        keys = jax.random.normal(k3, (n_experts, dmodel, expert_size), dtype=jnp.float32) * dmodel ** (-0.5)
        values = jax.random.normal(k4, (n_experts, expert_size, dmodel), dtype=jnp.float32) * (n_experts * expert_size) ** (-0.5)
        return {'x': x, 'expert_sel': expert_sel, 'keys': keys, 'values': values}
    _L1_ffn_in = _L1_ffn_setup()
    _d = {'L0_attn_x': _L0_attn_in['x'], 'L0_attn_W_in': _L0_attn_in['W_in'], 'L0_attn_A_log': _L0_attn_in['A_log'], 'L0_attn_W_B': _L0_attn_in['W_B'], 'L0_attn_W_C': _L0_attn_in['W_C'], 'L0_attn_W_dt': _L0_attn_in['W_dt'], 'L0_attn_b_dt': _L0_attn_in['b_dt'], 'L0_attn_dt_bias': _L0_attn_in['dt_bias'], 'L0_attn_rope_freq': _L0_attn_in['rope_freq'], 'L0_attn_ln_w': _L0_attn_in['ln_w'], 'L0_attn_ln_b': _L0_attn_in['ln_b'], 'L0_attn_W_out': _L0_attn_in['W_out'], 'L0_ffn_w_router': _L0_ffn_in['w_router'], 'L0_ffn_wi': _L0_ffn_in['wi'], 'L0_ffn_wo': _L0_ffn_in['wo'], 'L1_attn_W_q': _L1_attn_in['W_q'], 'L1_attn_W_k': _L1_attn_in['W_k'], 'L1_attn_W_v': _L1_attn_in['W_v'], 'L1_attn_W_o': _L1_attn_in['W_o'], 'L1_ffn_expert_sel': _L1_ffn_in['expert_sel'], 'L1_ffn_keys': _L1_ffn_in['keys'], 'L1_ffn_values': _L1_ffn_in['values']}
    _x0 = _d['L0_attn_x']
    _d['L0_attn_x'] = jax.random.normal(jax.random.fold_in(jax.random.key(seed), 1), (8, 512, 128), dtype=_x0.dtype)
    del _x0
    return _d

def reference(L0_attn_x, L0_attn_W_in, L0_attn_A_log, L0_attn_W_B, L0_attn_W_C, L0_attn_W_dt, L0_attn_b_dt, L0_attn_dt_bias, L0_attn_rope_freq, L0_attn_ln_w, L0_attn_ln_b, L0_attn_W_out, L0_ffn_w_router, L0_ffn_wi, L0_ffn_wo, L1_attn_W_q, L1_attn_W_k, L1_attn_W_v, L1_attn_W_o, L1_ffn_expert_sel, L1_ffn_keys, L1_ffn_values):

    def _L0_attn_ref(x, W_in, A_log, W_B, W_C, W_dt, b_dt, dt_bias, rope_freq, ln_w, ln_b, W_out):
        import jax, jax.numpy as jnp
        import numpy as np
        D_MODEL = 128
        D_STATE = 32
        EXPAND = 2
        D_INNER = D_MODEL * EXPAND
        B_SZ = 2
        SEQ = 64

        def _forward(x, W_in, A_log, W_B, W_C, W_dt, b_dt, dt_bias, rope_freq, ln_w, ln_b, W_out):
            B, L, _ = x.shape
            half = D_STATE // 2
            offset = 0
            xz = jnp.einsum('bld,ed->ble', x, W_in)
            x_inner = xz[..., :D_INNER]
            z = jax.nn.silu(xz[..., D_INNER:])
            A = -jnp.exp(A_log)
            Bm = jnp.einsum('bld,nd->bln', x, W_B)
            Cm = jnp.einsum('bld,nd->bln', x, W_C)
            dt = jax.nn.softplus(jnp.einsum('bld,ed->ble', x, W_dt) + b_dt + dt_bias)
            dtA = dt[..., None] * A
            denom = 1.0 - dtA / 2.0
            A_bar = (1.0 + dtA / 2.0) / denom
            B_bar = dt[..., None] / denom
            t_idx = jnp.arange(L, dtype=jnp.float32) + offset
            ang = t_idx[:, None] * rope_freq
            cos_a = jnp.cos(ang)
            sin_a = jnp.sin(ang)

            def step(state, inp):
                A_t, Bb_t, B_t, x_t, C_t, c_t, s_t = inp
                state = A_t * state + Bb_t * B_t[:, None, :] * x_t[:, :, None]
                real = state[..., :half]
                imag = state[..., half:]
                state = jnp.concatenate([real * c_t - imag * s_t, real * s_t + imag * c_t], axis=-1)
                y_t = jnp.einsum('bds,bs->bd', state, C_t)
                return (state, y_t)
            state0 = jnp.zeros((B, D_INNER, D_STATE), dtype=x.dtype)
            xs = (jnp.swapaxes(A_bar, 0, 1), jnp.swapaxes(B_bar, 0, 1), jnp.swapaxes(Bm, 0, 1), jnp.swapaxes(x_inner, 0, 1), jnp.swapaxes(Cm, 0, 1), cos_a, sin_a)
            final_state, ys = jax.lax.scan(step, state0, xs)
            out = jnp.swapaxes(ys, 0, 1) * z
            mu = jnp.mean(out, axis=-1, keepdims=True)
            var = jnp.mean((out - mu) ** 2, axis=-1, keepdims=True)
            out = (out - mu) * jax.lax.rsqrt(var + 1e-05) * ln_w + ln_b
            out = jnp.einsum('ble,de->bld', out, W_out)
            return (out, final_state)

        def _reference_tuple_inner(x, W_in, A_log, W_B, W_C, W_dt, b_dt, dt_bias, rope_freq, ln_w, ln_b, W_out):
            return _forward(x, W_in, A_log, W_B, W_C, W_dt, b_dt, dt_bias, rope_freq, ln_w, ln_b, W_out)
        return _reference_tuple_inner(x, W_in, A_log, W_B, W_C, W_dt, b_dt, dt_bias, rope_freq, ln_w, ln_b, W_out)[0]

    def _L0_ffn_ref(input_emb, w_router, wi, wo):
        import jax, jax.numpy as jnp
        import numpy as np
        NUM_GROUPS = 2
        EXPERT_CAPACITY = 80
        NUM_SELECTED = 2
        B, S, H = input_emb.shape
        E = w_router.shape[1]
        G = NUM_GROUPS
        T = B * S // G
        C = EXPERT_CAPACITY
        K = NUM_SELECTED
        x = input_emb.reshape(G, T, H)
        router_logits = jnp.einsum('gth,he->gte', x.astype(jnp.float32), w_router.astype(jnp.float32))
        router_probs = jax.nn.softmax(router_logits, axis=-1)
        gate, idx = jax.lax.top_k(router_probs, K)
        mask = jax.nn.one_hot(idx, E, dtype=jnp.float32)
        mask_kt = jnp.swapaxes(mask, 1, 2).reshape(G, K * T, E)
        pos = jnp.cumsum(mask_kt, axis=1) * mask_kt - 1.0
        pos = jnp.swapaxes(pos.reshape(G, K, T, E), 1, 2)
        disp_k = jax.nn.one_hot(pos, C, dtype=jnp.float32) * mask[..., None]
        dispatch = disp_k.sum(axis=2)
        combine = jnp.einsum('gtk,gtkec->gtec', gate, disp_k)
        expert_in = jnp.einsum('gtec,gth->egch', dispatch, x)
        h = jax.nn.relu(jnp.einsum('egch,ehf->egcf', expert_in, wi))
        expert_out = jnp.einsum('egcf,efh->egch', h, wo)
        y = jnp.einsum('gtec,egch->gth', combine, expert_out)
        return y.reshape(B, S, H)

    def _L1_attn_ref(in_features, W_q, W_k, W_v, W_o):
        import jax, jax.numpy as jnp
        import numpy as np
        D_MODEL = 128
        NUM_HEADS = 16
        D_K = D_MODEL // NUM_HEADS
        ROPE_THETA = 10000.0
        MAX_SEQ_LEN = 256

        def _rope_tables():
            dim_index = jnp.arange(D_K // 2, dtype=jnp.float32)
            pos = jnp.arange(MAX_SEQ_LEN, dtype=jnp.float32)
            theta_inv = ROPE_THETA ** (-2.0 * dim_index / D_K)
            ang = pos[:, None] * theta_inv[None, :]
            return (jnp.sin(ang), jnp.cos(ang))

        def _apply_rope(x, positions, sin, cos):
            s = sin[positions]
            c = cos[positions]
            x_even = x[..., ::2]
            x_odd = x[..., 1::2]
            y_even = x_even * c - x_odd * s
            y_odd = x_even * s + x_odd * c
            y = jnp.stack([y_even, y_odd], axis=-1)
            return y.reshape(x.shape)
        B, S, _ = in_features.shape
        sin, cos = _rope_tables()
        positions = jnp.arange(S)

        def proj(W):
            y = jnp.einsum('bsd,od->bso', in_features, W)
            return y.reshape(B, S, NUM_HEADS, D_K).transpose(0, 2, 1, 3)
        Q = _apply_rope(proj(W_q), positions, sin, cos)
        K = _apply_rope(proj(W_k), positions, sin, cos)
        V = proj(W_v)
        scores = jnp.einsum('bhnd,bhmd->bhnm', Q, K) / jnp.sqrt(jnp.float32(D_K))
        causal = jnp.tril(jnp.ones((S, S), dtype=bool))
        scores = jnp.where(causal[None, None], scores, -jnp.inf)
        attn = jax.nn.softmax(scores, axis=-1)
        head = jnp.einsum('bhnm,bhmd->bhnd', attn, V)
        head = head.transpose(0, 2, 1, 3).reshape(B, S, D_MODEL)
        return jnp.einsum('bso,do->bsd', head, W_o.T.T) if False else jnp.einsum('bsi,oi->bso', head, W_o)

    def _L1_ffn_ref(x, expert_sel, keys, values):
        import jax, jax.numpy as jnp
        import numpy as np
        N_HEADS = 4
        B, S, d = x.shape
        n_experts = keys.shape[0]
        xf = x.reshape(-1, d)
        N = xf.shape[0]
        logits = xf @ expert_sel.T
        sel = jax.nn.sigmoid(logits)
        sel_val, sel_idx = jax.lax.top_k(sel, N_HEADS)
        gates = jnp.zeros((N, n_experts), dtype=x.dtype)
        gates = gates.at[jnp.arange(N)[:, None], sel_idx].set(sel_val)
        h = jnp.einsum('nd,kde->nke', xf, keys)
        scores = jax.nn.relu(h) * gates[:, :, None]
        out = jnp.einsum('nke,kev->nv', scores, values)
        return out.reshape(B, S, -1)
    x = L0_attn_x
    xn = _layernorm(x, axis=-1)
    s = _L0_attn_ref(xn, L0_attn_W_in, L0_attn_A_log, L0_attn_W_B, L0_attn_W_C, L0_attn_W_dt, L0_attn_b_dt, L0_attn_dt_bias, L0_attn_rope_freq, L0_attn_ln_w, L0_attn_ln_b, L0_attn_W_out)
    g = _silu(_L0_ffn_ref(xn, L0_ffn_w_router, L0_ffn_wi, L0_ffn_wo))
    x = x + s * g
    xn = _layernorm(x, axis=-1)
    s = _L1_attn_ref(xn, L1_attn_W_q, L1_attn_W_k, L1_attn_W_v, L1_attn_W_o)
    g = _silu(_L1_ffn_ref(xn, L1_ffn_expert_sel, L1_ffn_keys, L1_ffn_values))
    x = x + s * g
    return x

_drawn_inputs = setup_inputs


def setup_inputs(seed=0):
    import zlib

    import numpy as np

    out = dict(_drawn_inputs(seed))
    spreads = {'L0_attn_b_dt': (0.0, 0.8),
     'L0_attn_dt_bias': (-4.0, 0.6),
     'L0_attn_ln_w': (1.0, 0.6),
     'L0_attn_ln_b': (0.0, 0.8)}
    factors = {'L0_attn_W_in': 8.0,
     'L0_attn_A_log': 8.0,
     'L0_attn_W_B': 8.0,
     'L0_attn_W_C': 8.0,
     'L0_attn_W_dt': 8.0,
     'L0_attn_rope_freq': 8.0,
     'L0_attn_W_out': 8.0,
     'L0_ffn_w_router': 8.0,
     'L0_ffn_wi': 8.0,
     'L0_ffn_wo': 8.0,
     'L1_attn_W_q': 5.448,
     'L1_attn_W_k': 5.391,
     'L1_attn_W_v': 4.08,
     'L1_attn_W_o': 4.109,
     'L1_ffn_expert_sel': 4.266,
     'L1_ffn_keys': 4.953,
     'L1_ffn_values': 4.124}
    for name, (base, spread) in spreads.items():
        noise = np.random.default_rng([zlib.crc32(name.encode()), seed]).standard_normal(out[name].shape)
        drawn = base * np.exp(spread * noise) if base else spread * noise
        out[name] = jnp.asarray(drawn.astype(out[name].dtype))
    for name, factor in factors.items():
        out[name] = (out[name] * factor).astype(out[name].dtype)
    return out
```

```python
import numpy as np
from contextlib import ExitStack
import concourse.bass as bass
from concourse import mybir

F32 = mybir.dt.float32
BF16 = mybir.dt.bfloat16
I32 = mybir.dt.int32
U32 = mybir.dt.uint32
ALU = mybir.AluOpType
ACT = mybir.ActivationFunctionType
AX = mybir.AxisListType

P = 128
B, L, D = 8, 512, 128
T = B * L
NT = T // P
TQ = L // P
DI, NS = 256, 32
HALF = NS // 2
E0, C0, F0, G0 = 8, 80, 512, 2
WC = 2 * DI + DI + 2 * NS + E0
EPS = 1e-5
CH = 16
LN2 = float(np.log(2.0))
TINY = 2.0 ** -60
LOG_TINY = 60.0 * LN2


class Tally:

    def __init__(self, eng, sem, base=0):
        self.eng, self.sem, self.base, self.n = eng, sem, base, 0

    def mark(self, ins):
        self.n += 1
        ins.then_inc(self.sem, 1)
        return self.n

    def settle(self):
        self.eng.wait_ge(self.sem, self.base + self.n)

    def __call__(self, ins):
        self.mark(ins)
        self.settle()


class Scope:
    taken = []

    def __init__(self, nc, ctx, tag):
        self.nc, self.ctx, self.tag = nc, ctx, tag

    def sb(self, name, shape, dt=F32):
        return self.ctx.enter_context(self.nc.sbuf_tensor(f"{self.tag}_{name}", shape, dt))

    def ps(self, name, shape, dt=F32):
        return self.ctx.enter_context(self.nc.psum_tensor(f"{self.tag}_{name}", shape, dt))

    def sems(self, names):
        new = [self.nc.alloc_semaphore(f"{self.tag}_{n}") for n in names.split()]
        Scope.taken.extend(new)
        return new

    @staticmethod
    def clear_all(nc):
        nc.clear_and_free_semaphores(Scope.taken)
        Scope.taken = []
        nc.all_engine_barrier()


def over(ap, n):
    return ap.unsqueeze(2).to_broadcast([ap.shape[0], ap.shape[1], n])


def phase_norm(nc, d, s, tag, source):
    with ExitStack() as ctx:
        k = Scope(nc, ctx, tag)
        sq = k.sb("sq", [P, NT, D])
        mean = k.sb("mean", [P, NT])
        var = k.sb("var", [P, NT])
        std = k.sb("std", [P, NT])
        loaded, dv, centred, squared, var_ready, std_ready = k.sems("loaded dv centred squared var_ready std_ready")
        block = ctx.enter_context(nc.Block())

        @block.sync
        def _(sp):
            if source is not None:
                sp.dma_start(s.xc[:, :, :], source.rearrange("b (q p) e -> p (b q) e", p=P)).then_inc(loaded, 16)

        @block.vector
        def _(dve):
            step = Tally(dve, dv)
            step.mark(nc.vector.memset(s.eps[:, :], EPS))
            if source is not None:
                dve.wait_ge(loaded, 16)
            step(nc.vector.tensor_reduce(mean[:, :], s.xc[:, :, :], AX.X, ALU.add))
            step(nc.vector.tensor_scalar(mean[:, :], mean[:, :], 1.0 / D, None, ALU.mult))
            nc.vector.tensor_tensor(s.xc[:, :, :], s.xc[:, :, :], over(mean[:, :], D), ALU.subtract).then_inc(centred, 1)
            dve.wait_ge(squared, 1)
            step(nc.vector.tensor_reduce(var[:, :], sq[:, :, :], AX.X, ALU.add))
            nc.vector.tensor_scalar(var[:, :], var[:, :], 1.0 / D, None, ALU.mult).then_inc(var_ready, 1)
            dve.wait_ge(std_ready, 1)
            step(nc.vector.reciprocal(s.rstd[:, :], std[:, :]))

        @block.scalar
        def _(act):
            act.wait_ge(centred, 1)
            nc.scalar.activation(sq[:, :, :], s.xc[:, :, :], ACT.Square).then_inc(squared, 1)
            act.wait_ge(var_ready, 1)
            nc.scalar.activation(std[:, :], var[:, :], ACT.Sqrt, bias=s.eps[:, 0:1]).then_inc(std_ready, 1)


def phase_project(nc, d, s):
    with ExitStack() as ctx:
        k = Scope(nc, ctx, "p")
        wcat = k.sb("wcat", [P, WC])
        bias = k.sb("bias", [P, DI])
        bias2 = k.sb("bias2", [P, DI])
        xs = k.sb("xs", [P, 2, P])
        xT = k.sb("xT", [P, 2, P])
        psT = k.ps("psT", [P, 2, 512])
        ps1 = k.ps("ps1", [P, 2, 512])
        ps2 = k.ps("ps2", [P, 2, 512])
        loaded, dv, xs_ready, turned, xT_ready, projected, read_act, read_dve = k.sems(
            "loaded dv xs_ready turned xT_ready projected read_act read_dve")
        block = ctx.enter_context(nc.Block())

        @block.sync
        def _(sp):
            sp.dma_start(wcat[:, :], d["wcat"]).then_inc(loaded, 16)
            sp.dma_start(bias[:, :], d["b_dt"]).then_inc(loaded, 16)
            sp.dma_start(bias2[:, :], d["dt_bias"]).then_inc(loaded, 16)

        @block.vector
        def _(dve):
            step = Tally(dve, dv)
            dve.wait_ge(loaded, 48)
            step(nc.vector.tensor_tensor(bias[:, :], bias[:, :], bias2[:, :], ALU.add))

            def normalise(n, r):
                nc.vector.tensor_scalar(xs[:, r, :], s.xc[:, bass.ds(n, 1), :].rearrange("p a e -> p (a e)"),
                                        s.rstd[:, bass.ds(n, 1)], None, ALU.mult).then_inc(xs_ready, 1)

            def take(n, r):
                dve.wait_ge(projected, n + 1)
                nc.vector.tensor_tensor(s.pre[:, bass.ds(n, 1), :].rearrange("p a e -> p (a e)"),
                                        ps2[:, r, 0:DI], bias[:, :], ALU.add)
                nc.vector.tensor_copy(s.bcr[:, bass.ds(n, 1), :].rearrange("p a e -> p (a e)"),
                                      ps2[:, r, DI:WC - 2 * DI]).then_inc(read_dve, 1)

            normalise(0, 0)
            normalise(1, 1)
            with dve.Fori(0, NT // 2 - 1) as pair:
                for r in range(2):
                    n = pair * 2
                    take(n + r, r)
                    dve.wait_ge(turned, n + r + 1)
                    normalise(n + r + 2, r)
            for r in range(2):
                take(NT - 2 + r, r)

        @block.tensor
        def _(pe):
            pe.wait_ge(loaded, 48)

            def tile(n, r, first):
                pe.wait_ge(xs_ready, n + 1)
                nc.tensor.transpose(psT[:, r, 0:P], xs[:, r, :], s.ident[:, :]).then_inc(turned, 1)
                pe.wait_ge(xT_ready, n + 1)
                if not first:
                    pe.wait_ge(read_act, n - 1)
                    pe.wait_ge(read_dve, n - 1)
                nc.tensor.matmul(ps1[:, r, :], xT[:, r, :], wcat[:, 0:512], start=True, stop=True)
                nc.tensor.matmul(ps2[:, r, 0:WC - 512], xT[:, r, :], wcat[:, 512:WC], start=True, stop=True).then_inc(projected, 1)

            for r in range(2):
                tile(r, r, True)
            with pe.Fori(1, NT // 2) as pair:
                for r in range(2):
                    tile(pair * 2 + r, r, False)

        @block.scalar
        def _(act):
            with act.Fori(0, NT // 2) as pair:
                for r in range(2):
                    n = pair * 2
                    act.wait_ge(turned, n + r + 1)
                    nc.scalar.activation(xT[:, r, :], psT[:, r, 0:P], ACT.Copy).then_inc(xT_ready, 1)
                    act.wait_ge(projected, n + r + 1)
                    nc.scalar.activation(s.xi[:, bass.ds(n + r, 1), :].rearrange("p a e -> p (a e)"), ps1[:, r, 0:DI], ACT.Copy)
                    nc.scalar.activation(s.zp[:, bass.ds(n + r, 1), :].rearrange("p a e -> p (a e)"), ps1[:, r, DI:2 * DI], ACT.Silu).then_inc(read_act, 1)

def flat(ap):
    return ap.rearrange("p a e -> p (a e)")

TWO_PI = 2.0 * float(np.pi)
C1 = 6.28125
C2 = float(np.float32(TWO_PI - C1).view(np.uint32) & 0xFFFFF000)
C2 = float(np.array([np.float32(TWO_PI - C1).view(np.uint32) & 0xFFFFF000], np.uint32).view(np.float32)[0])
C3 = float(TWO_PI - C1 - C2)
ROUND = 1.5 * 2.0 ** 23
PI_IN = 3.1415925


def phase_steps(nc, d, s):
    with ExitStack() as ctx:
        k = Scope(nc, ctx, "t")
        W = TQ * DI
        ab, ex, lg, lg2, u1, mm, dt, shift = (k.sb(n, [P, W]) for n in ("ab", "ex", "lg", "lg2", "u1", "mm", "dt", "shift"))
        lnd = k.sb("lnd", [P, 2, W])
        res = k.sb("res", [P, 2, W])
        lparts = k.sb("lparts", [P, 2, 3, W], BF16)
        hparts = k.sb("hparts", [P, 2, 3, W], BF16)
        zero = k.sb("zero", [P, DI], BF16)
        (dv, exp_ready, log_ready, clamped, log2_ready, lnd_ready, hdx_ready, high_ready, rest_ready,
         mid_ready, low_ready, slot_free, stored, zeroed) = k.sems(
            "dv exp_ready log_ready clamped log2_ready lnd_ready hdx_ready high_ready rest_ready "
            "mid_ready low_ready slot_free stored zeroed")
        block = ctx.enter_context(nc.Block())
        per_b = 6

        def rows(ap, b):
            return flat(ap[:, bass.ds(b * TQ, TQ), :])

        @block.sync
        def _(sp):
            sp.wait_ge(zeroed, 1)
            for h in range(2):
                sp.dma_start(d["hdp"][h, :, :, 0, :].rearrange("c f e -> (c f) e"), zero[0:24, :]).then_inc(stored, 16)
            with sp.Fori(0, 2) as h:
                for f in range(4):
                    r = f % 2
                    sp.wait_ge(low_ready, (h * 4 + f) * 2 + 2)
                    for c in range(3):
                        sp.dma_start(d["lnp"][bass.ds(h, 1), c, f].rearrange("h (q p) e -> p (h q) e", p=P),
                                     lparts[:, r, c, :].rearrange("p (q e) -> p q e", e=DI)).then_inc(stored, 16)
                    for c, part in enumerate((0, 1, 2, 0, 1, 0)):
                        sp.dma_start(d["hdp"][bass.ds(h, 1), c, f, 1:, :].rearrange("h (q p) e -> p (h q) e", p=P),
                                     hparts[:, r, part, :].rearrange("p (q e) -> p q e", e=DI)).then_inc(stored, 16)
                    sp.wait_ge(stored, (h * 4 + f) * 144 + 176)
                    sp.sem_inc(slot_free, 1)
            sp.wait_ge(stored, 16 * (2 + 9 * B))

        @block.vector
        def _(dve):
            def sequence(b, r):
                step = Tally(dve, dv, b * per_b)
                pre = rows(s.pre, b)
                dve.wait_ge(lnd_ready, b)
                step.mark(nc.vector.scalar_tensor_tensor(ab[:, :], pre, -1.0, pre, ALU.mult, ALU.max))
                step.mark(nc.vector.tensor_scalar(shift[:, :], pre, LOG_TINY, 0.0, ALU.add, ALU.min))
                dve.wait_ge(exp_ready, b + 1)
                step(nc.vector.tensor_scalar(u1[:, :], ex[:, :], 1.0, -1.0, ALU.add, ALU.add))
                step(nc.vector.tensor_tensor(u1[:, :], ex[:, :], u1[:, :], ALU.subtract))
                dve.wait_ge(log_ready, b + 1)
                step(nc.vector.tensor_tensor(u1[:, :], lg[:, :], u1[:, :], ALU.add))
                step(nc.vector.scalar_tensor_tensor(dt[:, :], pre, 0.0, u1[:, :], ALU.max, ALU.add))
                assert step.n == per_b
                nc.vector.tensor_scalar(mm[:, :], dt[:, :], TINY, None, ALU.max).then_inc(clamped, 1)
                xi = rows(s.xi, b)
                nc.vector.scalar_tensor_tensor(xi, dt[:, :], 0.5, xi, ALU.mult, ALU.mult).then_inc(hdx_ready, 1)
                dve.wait_ge(log2_ready, b + 1)
                dve.wait_ge(low_ready, b * 2)
                nc.vector.tensor_tensor(lnd[:, r, :], lg2[:, :], shift[:, :], ALU.add).then_inc(lnd_ready, 1)

            with dve.Fori(0, B // 2) as pair:
                for r in range(2):
                    sequence(pair * 2 + r, r)

        @block.scalar
        def _(act):
            def sequence(b, r):
                act.wait_ge(dv, b * per_b + 1)
                nc.scalar.activation(ex[:, :], ab[:, :], ACT.Exp, scale=-1.0).then_inc(exp_ready, 1)
                act.wait_ge(exp_ready, b + 1)
                nc.scalar.activation(lg[:, :], ex[:, :], ACT.Ln, bias=1.0).then_inc(log_ready, 1)
                act.wait_ge(clamped, b + 1)
                nc.scalar.activation(lg2[:, :], mm[:, :], ACT.Ln).then_inc(log2_ready, 1)
                act.wait_ge(slot_free, b + 1)
                act.wait_ge(hdx_ready, b + 1)
                nc.scalar.activation(hparts[:, r, 0, :], rows(s.xi, b), ACT.Copy).then_inc(high_ready, 1)
                act.wait_ge(lnd_ready, b + 1)
                nc.scalar.activation(lparts[:, r, 0, :], lnd[:, r, :], ACT.Copy).then_inc(high_ready, 1)
                for i, parts in enumerate((hparts, lparts)):
                    act.wait_ge(rest_ready, b * 2 + i + 1)
                    nc.scalar.activation(parts[:, r, 1, :], res[:, i, :], ACT.Copy).then_inc(mid_ready, 1)

            act.sem_inc(slot_free, 2)
            with act.Fori(0, B // 2) as pair:
                for r in range(2):
                    sequence(pair * 2 + r, r)

        @block.gpsimd
        def _(pool):
            nc.gpsimd.memset(zero[:, :], 0.0).then_inc(zeroed, 1)

            def sequence(b, r):
                whole = (rows(s.xi, b), lnd[:, r, :])
                pool.wait_ge(low_ready, b * 2)
                for i, parts in enumerate((hparts, lparts)):
                    pool.wait_ge(high_ready, b * 2 + i + 1)
                    nc.gpsimd.tensor_tensor(res[:, i, :], whole[i], parts[:, r, 0, :], ALU.subtract).then_inc(rest_ready, 1)
                for i, parts in enumerate((hparts, lparts)):
                    pool.wait_ge(mid_ready, b * 2 + i + 1)
                    nc.gpsimd.tensor_tensor(parts[:, r, 2, :], res[:, i, :], parts[:, r, 1, :], ALU.subtract).then_inc(low_ready, 1)

            with pool.Fori(0, B // 2) as pair:
                for r in range(2):
                    sequence(pair * 2 + r, r)


def split3(nc, dve, step, x, parts, rest):
    step(nc.vector.tensor_copy(parts[0], x))
    step(nc.vector.tensor_tensor(rest, x, parts[0], ALU.subtract))
    step(nc.vector.tensor_copy(parts[1], rest))
    step(nc.vector.tensor_tensor(parts[2], rest, parts[1], ALU.subtract))


def phase_rotation(nc, d, s):
    with ExitStack() as ctx:
        k = Scope(nc, ctx, "r")
        freq = k.sb("freq", [P, HALF])
        freq_col = k.sb("freq_col", [P, 1])
        sign_col = k.sb("sign_col", [P, 1])
        steps = k.sb("steps", [P, TQ])
        steps_row = k.sb("steps_row", [P, L])
        angle = k.sb("angle", [P, TQ, HALF])
        cos_t, sin_t = (k.sb(n, [P, TQ, HALF]) for n in ("cos_t", "sin_t"))
        angle_c = k.sb("angle_c", [P, L])
        turns = k.sb("turns", [P, 2, L])
        left = k.sb("left", [P, 2, L])
        turned_b, turned_c = (k.sb(n, [P, TQ, B, NS]) for n in ("turned_b", "turned_c"))
        prod = k.sb("prod", [P, TQ, B, HALF])
        plain_b = k.sb("plain_b", [P, TQ, B, NS])
        cb = k.sb("cb", [P, TQ, B, NS])
        rest = k.sb("rest", [P, TQ, B, NS])
        parts = k.sb("parts", [P, 3, TQ, B, NS], BF16)
        stack = k.sb("stack", [P, 2, TQ, B, 6, NS], BF16)
        zero = k.sb("zero", [P, 6 * NS], BF16)
        alog = k.sb("alog", [3 * NS, DI])
        alog_rest = k.sb("alog_rest", [3 * NS, DI])
        alog_parts = k.sb("alog_parts", [3 * NS, 3, DI], BF16)
        psT = k.ps("psT", [P, 2, L])
        loaded, dv, angles_ready, sines_ready, turned_ready, columns_ready, stacked, stored = k.sems(
            "loaded dv angles_ready sines_ready turned_ready columns_ready stacked stored")
        block = ctx.enter_context(nc.Block())

        @block.sync
        def _(sp):
            for dst, name in ((freq[:, :], "freq"), (freq_col[:, :], "freq_col"), (sign_col[:, :], "sign_col"),
                              (steps[:, :], "steps"), (steps_row[:, :], "steps_row"), (alog[:, :], "alog")):
                sp.dma_start(dst, d[name]).then_inc(loaded, 16)
            for term in range(2):
                sp.wait_ge(stacked, term + 1)
                for b in range(B):
                    dst = d["st0"][b, 1:] if term == 0 else d["st1"][b]
                    sp.dma_start(dst.rearrange("(q p) e -> p q e", p=P),
                                 stack[:, term, :, b, :, :].rearrange("p q c n -> p q (c n)")).then_inc(stored, 16)
            sp.dma_start(d["st0"][:, 0, :], zero[0:B, :]).then_inc(stored, 16)
            sp.wait_ge(stored, 16 * (2 * B + 1))

        @block.vector
        def _(dve):
            step = Tally(dve, dv)
            step.mark(nc.vector.memset(zero[:, :], 0.0))
            dve.wait_ge(loaded, 96)
            step(nc.vector.tensor_tensor(angle[:, :, :], over(steps[:, :], HALF),
                                         freq[:, :].unsqueeze(1).to_broadcast([P, TQ, HALF]), ALU.mult))
            step(nc.vector.tensor_scalar(angle_c[:, :], steps_row[:, :], freq_col[:, 0:1], None, ALU.mult))

            def reduce(ang, out, turn, quarter):
                step(nc.vector.tensor_scalar(turn, ang, 1.0 / TWO_PI, 0.25 * quarter, ALU.mult, ALU.add))
                step(nc.vector.tensor_scalar(turn, turn, ROUND, -ROUND, ALU.add, ALU.add))
                step(nc.vector.scalar_tensor_tensor(out, turn, -C1, ang, ALU.mult, ALU.add))
                step(nc.vector.scalar_tensor_tensor(out, turn, -C2, out, ALU.mult, ALU.add))
                step(nc.vector.scalar_tensor_tensor(out, turn, -C3, out, ALU.mult, ALU.add))
                step(nc.vector.tensor_scalar(out, out, quarter * TWO_PI / 4, PI_IN, ALU.add, ALU.min))
                step(nc.vector.tensor_scalar(out, out, -PI_IN, None, ALU.max))

            small = flat(angle[:, :, :])
            w = TQ * HALF
            reduce(small, flat(cos_t[:, :, :]), turns[:, 0, 0:w], 1)
            reduce(small, flat(sin_t[:, :, :]), turns[:, 0, 0:w], 0)
            reduce(angle_c[:, :], left[:, 0, :], turns[:, 0, :], 1)
            reduce(angle_c[:, :], left[:, 1, :], turns[:, 1, :], 0)
            step(nc.vector.engine_nop())
            nc.vector.engine_nop().then_inc(angles_ready, 1)

            pieces = [alog_parts[:, c, :] for c in range(3)]
            split3(nc, dve, step, alog[:, :], pieces, alog_rest[:, :])
            for c in range(3):
                lo, hi = c * NS, (c + 1) * NS
                src = alog_parts[lo:hi, c, :].unsqueeze(1).to_broadcast([NS, 2 * CH * 2, DI])
                step.mark(nc.vector.tensor_copy(s.marg[lo:hi, :, :, :, :].rearrange("r a u h e -> r (a u h) e"), src))

            dve.wait_ge(sines_ready, 4)
            step.mark(nc.vector.tensor_scalar(s.sin_c[:, :], s.sin_c[:, :], sign_col[:, 0:1], None, ALU.mult))
            view = s.bcr[:, :, :].rearrange("p (b q) n -> p q b n", q=TQ)
            full = [P, TQ, B, HALF]

            def turn(src, dst, back):
                re, im = src[:, :, :, 0:HALF], src[:, :, :, HALF:NS]
                cos = cos_t[:, :, :].unsqueeze(2).to_broadcast(full)
                sin = sin_t[:, :, :].unsqueeze(2).to_broadcast(full)
                for a, b, lo, op in ((re, im, 0, ALU.add if back else ALU.subtract),
                                     (im, re, HALF, ALU.subtract if back else ALU.add)):
                    out = dst[:, :, :, lo:lo + HALF]
                    for q in range(TQ):
                        step.mark(nc.vector.tensor_tensor(out[:, q], a[:, q], cos[:, q], ALU.mult))
                        step(nc.vector.tensor_tensor(prod[:, q], b[:, q], sin[:, q], ALU.mult))
                    step(nc.vector.tensor_tensor(out, out, prod[:, :, :, :], op))

            turn(view[:, :, :, 0:NS], turned_b, False)
            turn(view[:, :, :, NS:2 * NS], turned_c, True)
            nc.vector.engine_nop().then_inc(turned_ready, 1)
            step(nc.vector.tensor_copy(plain_b[:, :, :, :], view[:, :, :, 0:NS]))
            step(nc.vector.tensor_tensor(cb[:, :, :, :], turned_c[:, :, :, :], plain_b[:, :, :, :], ALU.mult))
            step(nc.vector.tensor_reduce(s.kappa[:, :, :], cb[:, :, :, :], AX.X, ALU.add))
            for term, src in enumerate((turned_b, plain_b)):
                m = "p q b n -> p (q b) n"
                p3 = [parts[:, c, :, :, :].rearrange(m) for c in range(3)]
                split3(nc, dve, step, src[:, :, :, :].rearrange(m), p3, rest[:, :, :, :].rearrange(m))
                st = stack[:, term, :, :, :, :].rearrange("p q b c n -> p (q b) c n")
                for lo, hi, c in ((0, 3, 0), (3, 5, 1), (5, 6, 2)):
                    step(nc.vector.tensor_copy(st[:, :, lo:hi, :],
                                               p3[c].unsqueeze(2).to_broadcast([P, TQ * B, hi - lo, NS])))
                nc.vector.engine_nop().then_inc(stacked, 1)
            dve.wait_ge(columns_ready, 2)
            for h in range(2):
                step.mark(nc.vector.tensor_copy(s.c_col[:, h, :], psT[:, h, :]))

        @block.scalar
        def _(act):
            act.wait_ge(angles_ready, 1)
            nc.scalar.activation(cos_t[:, :, :], cos_t[:, :, :], ACT.Sin).then_inc(sines_ready, 1)
            nc.scalar.activation(sin_t[:, :, :], sin_t[:, :, :], ACT.Sin).then_inc(sines_ready, 1)
            nc.scalar.activation(s.cos_c[:, :], left[:, 0, :], ACT.Sin).then_inc(sines_ready, 1)
            nc.scalar.activation(s.sin_c[:, :], left[:, 1, :], ACT.Sin).then_inc(sines_ready, 1)

        @block.tensor
        def _(pe):
            pe.wait_ge(turned_ready, 1)
            for h in range(2):
                for q in range(TQ):
                    last = nc.tensor.transpose(psT[:, h, q * P:(q + 1) * P],
                                               turned_c[:, q, 4 * h:4 * h + 4, :].rearrange("p f n -> p (f n)"), s.ident[:, :])
                last.then_inc(columns_ready, 1)

BODY = 2 * CH
NB = L // BODY
AHEAD = 2


def phase_scan(nc, d, s):
    with ExitStack() as ctx:
        k = Scope(nc, ctx, "c")
        sel = k.sb("sel", [108, P], BF16)
        sel_f = k.sb("sel_f", [108, P])
        eye_j = k.sb("eye_j", [P, 2, P])
        mask4 = k.sb("mask4", [P, 4])
        half_ln2 = k.sb("half_ln2", [P, 1])
        mv = k.sb("mv", [96, 2, CH, 2, DI], BF16)
        st = k.sb("st", [96, 2, CH, P], BF16)
        rot = k.sb("rot", [P, 2, 8, P])
        tmp = k.sb("tmp", [P, 8, P])
        cy = k.sb("cy", [P, 2, 8, 2, 32])
        a = k.sb("a", [P, 4, 512])
        aq = k.sb("aq", [P, 4, 512])
        yb = k.sb("yb", [P, 2, CH, P])
        args = k.ps("args", [P, 2, 512])
        q = k.ps("q", [P, 2, 2, 512])
        ys = k.ps("ys", [P, 2, 4, P])
        (loaded, cleared, picked, dv, arg_loaded0, arg_loaded1, mv_loaded0, mv_loaded1, arg_ready, mv_used, decay_ready, q_ready, aq_ready, rot_ready,
         y_ready, y_banks, y_stored0, y_stored1, pl) = k.sems(
            "loaded cleared picked dv arg_loaded0 arg_loaded1 mv_loaded0 mv_loaded1 arg_ready mv_used decay_ready q_ready aq_ready rot_ready "
            "y_ready y_banks y_stored0 y_stored1 pl")
        arg_loaded, mv_loaded = (arg_loaded0, arg_loaded1), (mv_loaded0, mv_loaded1)
        y_stored = (y_stored0, y_stored1)
        block = ctx.enter_context(nc.Block())
        y_out = d["y"].rearrange("(h f) l (g e) -> h g f l e", h=2, g=2)
        n_arg, n_mv = 2, 4 + 16

        @block.sync
        def _(sp):
            sp.dma_start(sel_f[:, :], d["sel"]).then_inc(loaded, 16)
            sp.dma_start(eye_j[:, :, :], d["eye_j"]).then_inc(loaded, 16)
            sp.dma_start(mask4[:, :], d["mask4"]).then_inc(loaded, 16)
            sp.wait_ge(cleared, 2)

            def load(c, slot):
                u0 = c * CH
                for h in range(2):
                    sp.dma_start(s.marg[96:108, slot, :, h, :],
                                 d["lnp"][h, :, :, bass.ds(u0, CH), :].rearrange("c f u e -> (c f) u e")).then_inc(arg_loaded[slot], 16)
                for h in range(2):
                    for term in range(2):
                        lo = h * 48 + term * 24
                        sp.dma_start(mv[lo:lo + 24, slot, :, h, :],
                                     d["hdp"][h, :, :, bass.ds(u0 + term, CH), :].rearrange("c f u e -> (c f) u e")).then_inc(mv_loaded[slot], 16)
                        src = d["st0"] if term == 0 else d["st1"]
                        for f in range(4):
                            sp.dma_start(st[lo + f:lo + 24:4, slot, :, f * NS:(f + 1) * NS],
                                         src[h * 4 + f, bass.ds(u0, CH), :].rearrange("u (c n) -> c u n", n=NS)).then_inc(mv_loaded[slot], 16)

            def store(c, slot):
                sp.wait_ge(y_banks, (c + 1) * (CH // 4) + 2)
                for j in range(4):
                    h, g = divmod(j, 2)
                    sp.dma_start(y_out[h, g, :, bass.ds(c * CH, CH), :], yb[32 * j:32 * j + 4, slot, :, :]).then_inc(y_stored[slot], 16)

            for slot in range(2):
                load(slot, slot)
            with sp.Fori(0, NB - 1) as i:
                for slot in range(2):
                    c = i * 2 + slot
                    sp.wait_ge(arg_ready, (c + 1) * CH)
                    sp.wait_ge(mv_used, c + 1)
                    load(c + 2, slot)
                    store(c, slot)
            for slot in range(2):
                store(2 * NB - 2 + slot, slot)
                sp.wait_ge(y_stored[slot], (NB + 1) * 64)

        @block.tensor
        def _(pe):
            pe.wait_ge(picked, 1)

            def argument(i, j):
                slot, u = j // CH % 2, j % CH
                if u == 0:
                    pe.wait_ge(arg_loaded[slot], (i + j // BODY + 1) * 16 * n_arg)
                nc.tensor.matmul(args[:, j % 2, :], sel[:, :], flat(s.marg[:, slot, u]), start=True, stop=True).then_inc(arg_ready, 1)

            def inputs(i, j, only=False):
                slot, u = j // CH % 2, j % CH
                if u == 0:
                    pe.wait_ge(mv_loaded[slot], (i + j // BODY + 1) * 16 * n_mv)
                for h in range(2):
                    ins = nc.tensor.matmul(q[:, j % 2, h, 0:DI], st[:, slot, u, :], mv[:, slot, u, h, :], start=True, stop=only)
                if u == CH - 1:
                    ins.then_inc(mv_used, 1)
                return ins

            def body(i, last):
                for j in range(BODY):
                    end = last and j == BODY - 1
                    if j % 8 == 0:
                        pe.wait_ge(rot_ready, i * (BODY // 8) + j // 8 + 1)
                    slot, v = j // 8 % 2, j % 8
                    for h in range(2):
                        cols = slice(h * DI, (h + 1) * DI)
                        pe.wait_ge(aq_ready, i * (2 * BODY) + 2 * j + h + 1)
                        if not end:
                            nc.tensor.matmul(q[:, (j + 1) % 2, h, 0:DI], rot[:, slot, v, :], aq[:, j % 4, cols],
                                             start=False, stop=True).then_inc(q_ready, 1)
                    if j % 4 == 0:
                        pe.wait_ge(y_banks, i * (BODY // 4) + j // 4 + 1)
                    for g in range(4):
                        ins = nc.tensor.matmul(ys[32 * g:32 * g + 32, j // 4 % 2, j % 4, :], cy[:, slot, v, g // 2, :],
                                               aq[:, j % 4, g * P:(g + 1) * P], start=True, stop=True)
                    if j % 4 == 3:
                        ins.then_inc(y_ready, 1)
                    if not (last and j >= BODY - AHEAD):
                        argument(i, j + AHEAD)
                    if not (last and j >= BODY - 2):
                        ins = inputs(i, j + 2)

            for j in range(AHEAD):
                argument(0, j)
            inputs(0, 0, only=True).then_inc(q_ready, 2)
            inputs(0, 1)
            with pe.Fori(0, NB - 1) as i:
                body(i, False)
            body(NB - 1, True)

        @block.vector
        def _(dve):
            step = Tally(dve, dv)
            step.mark(nc.vector.memset(half_ln2[:, :], LN2 / 2))
            nc.vector.memset(mv[:, :, :, :, :], 0.0).then_inc(cleared, 1)
            nc.vector.memset(st[:, :, :, :], 0.0).then_inc(cleared, 1)
            dve.wait_ge(loaded, 48)
            nc.vector.tensor_copy(sel[:, :], sel_f[:, :]).then_inc(picked, 1)
            with dve.Fori(0, NB) as i:
                for j in range(BODY):
                    dve.wait_ge(decay_ready, i * BODY + j + 1)
                    for h in range(2):
                        cols = slice(h * DI, (h + 1) * DI)
                        dve.wait_ge(q_ready, i * (2 * BODY) + 2 * j + h + 1)
                        nc.vector.tensor_tensor(aq[:, j % 4, cols], q[:, j % 2, h, 0:DI], a[:, j % 4, cols],
                                                ALU.mult).then_inc(aq_ready, 1)

        @block.scalar
        def _(act):
            act.sem_inc(y_banks, 2)
            act.sem_inc(y_stored0, 64)
            act.sem_inc(y_stored1, 64)
            act.wait_ge(picked, 1)

            def decay(i, m):
                act.wait_ge(arg_ready, i * BODY + m + 1)
                nc.scalar.activation(a[:, m % 4, :], args[:, m % 2, :], ACT.Tanh, bias=half_ln2[:, 0:1],
                                     scale=-0.5).then_inc(decay_ready, 1)

            def copy_out(i, n):
                slot = n * 4 // CH
                if n * 4 % CH == 0:
                    act.wait_ge(y_stored[slot], (i + 1) * 64)
                act.wait_ge(y_ready, i * (BODY // 4) + n + 1)
                u = n * 4 % CH
                nc.scalar.activation(yb[:, slot, u:u + 4, :], ys[:, n % 2, :, :], ACT.Copy).then_inc(y_banks, 1)

            def body(i, last):
                for m in range(BODY):
                    if not (last and m >= BODY - AHEAD):
                        decay(i, m + AHEAD)
                    if m % 4 == 3:
                        copy_out(i, m // 4)

            decay(0, 0)
            decay(0, 1)
            with act.Fori(0, NB - 1) as i:
                body(i, False)
            body(NB - 1, True)

        @block.gpsimd
        def _(pool):
            own = Tally(pool, pl)
            own(nc.gpsimd.memset(cy[:, :, :, :, :], 0.0))
            pool.wait_ge(loaded, 48)

            def build(g, slot, base):
                own = Tally(pool, pl, base)
                t = bass.ds(g * 8, 8)
                wide = [P, 8, P]
                own.mark(nc.gpsimd.tensor_tensor(rot[:, slot, :, :], eye_j[:, 0, :].unsqueeze(1).to_broadcast(wide),
                                                 over(s.cos_c[:, t], P), ALU.mult))
                own(nc.gpsimd.tensor_tensor(tmp[:, :, :], eye_j[:, 1, :].unsqueeze(1).to_broadcast(wide),
                                            over(s.sin_c[:, t], P), ALU.mult))
                own(nc.gpsimd.tensor_tensor(rot[:, slot, :, :], rot[:, slot, :, :], tmp[:, :, :], ALU.add))
                for h in range(2):
                    ins = nc.gpsimd.tensor_tensor(cy[:, slot, :, h, 0:4], mask4[:, :].unsqueeze(1).to_broadcast([P, 8, 4]),
                                                  over(s.c_col[:, h, t], 4), ALU.mult)
                ins.then_inc(rot_ready, 1)

            build(0, 0, 1)
            build(1, 1, 4)
            with pool.Fori(0, L // 16 - 1) as i:
                for slot in range(2):
                    g = i * 2 + slot
                    pool.wait_ge(y_ready, g * 2 + 2)
                    build(g + 2, slot, g * 3 + 7)

SLOTS = G0 * E0 * C0
SKIP = 8192.0


def phase_route0(nc, d, s):
    with ExitStack() as ctx:
        k = Scope(nc, ctx, "g")
        W = NT * E0
        logits = s.bcr[:, :, 2 * NS:2 * NS + E0]
        prob, hit, cand, number = (k.sb(n, [P, NT, E0]) for n in ("prob", "hit", "cand", "number"))
        best, first = k.sb("best", [P, 2, NT]), k.sb("first", [P, NT])
        total, inv = k.sb("total", [P, NT]), k.sb("inv", [P, NT])
        pick = k.sb("pick", [P, NT, 2, E0])
        pick_b = k.sb("pick_b", [P, NT, 2, E0], BF16)
        tri_f, tri = k.sb("tri_f", [P, P]), k.sb("tri", [P, P], BF16)
        ones = k.sb("ones", [P, P], BF16)
        count = k.sb("count", [P, NT, 2, E0])
        pos = k.sb("pos", [P, NT, 2, E0])
        offset = k.sb("offset", [P, NT, 2, E0])
        rank, slot, kept, lost = (k.sb(n, [P, NT, 2]) for n in ("rank", "slot", "kept", "lost"))
        psC = k.ps("psC", [P, NT, 2, E0])
        psS = k.ps("psS", [P, NT, 2, E0])
        loaded, dv, shifted, raised, picked, counted = k.sems("loaded dv shifted raised picked counted")
        block = ctx.enter_context(nc.Block())

        @block.sync
        def _(sp):
            sp.dma_start(tri_f[:, :], d["tri"]).then_inc(loaded, 16)
            sp.dma_start(number[:, :, :], d["number"]).then_inc(loaded, 16)
            sp.dma_start(offset[:, :, :, :], d["offset"]).then_inc(loaded, 16)

        @block.vector
        def _(dve):
            v = nc.vector
            step = Tally(dve, dv)
            step.mark(v.memset(ones[:, :], 1.0))
            dve.wait_ge(loaded, 48)
            step.mark(v.tensor_copy(tri[:, :], tri_f[:, :]))
            step(v.tensor_reduce(first[:, :], logits, AX.X, ALU.max))
            v.tensor_tensor(prob[:, :, :], logits, over(first[:, :], E0), ALU.subtract).then_inc(shifted, 1)
            dve.wait_ge(raised, 1)
            step(v.tensor_reduce(total[:, :], prob[:, :, :], AX.X, ALU.add))
            step(v.reciprocal(inv[:, :], total[:, :]))
            step(v.tensor_tensor(prob[:, :, :], prob[:, :, :], over(inv[:, :], E0), ALU.mult))
            for c in range(2):
                one = pick[:, :, c, :]
                step(v.tensor_reduce(best[:, c, :], prob[:, :, :], AX.X, ALU.max))
                step(v.tensor_tensor(hit[:, :, :], prob[:, :, :], over(best[:, c, :], E0), ALU.is_lt))
                step(v.scalar_tensor_tensor(cand[:, :, :], hit[:, :, :], float(E0), number[:, :, :], ALU.mult, ALU.add))
                step(v.tensor_reduce(first[:, :], cand[:, :, :], AX.X, ALU.min))
                step(v.tensor_tensor(one, number[:, :, :], over(first[:, :], E0), ALU.is_equal))
                if c == 0:
                    step(v.scalar_tensor_tensor(prob[:, :, :], one, -2.0, prob[:, :, :], ALU.mult, ALU.add))
            v.tensor_copy(pick_b[:, :, :, :], pick[:, :, :, :]).then_inc(picked, 1)
            dve.wait_ge(counted, 1)
            per_group = NT // G0
            tiles = [ap[:, :, :, :].rearrange("p (g t) c e -> p t g (c e)", g=G0) for ap in (count, psS)]
            step(v.memset(tiles[0][:, 0], 0.0))
            for t in range(1, per_group):
                step(v.tensor_tensor(tiles[0][:, t], tiles[0][:, t - 1], tiles[1][:, t - 1], ALU.add))
            step(v.tensor_tensor(pos[:, :, :, :], count[:, :, :, :], psC[:, :, :, :], ALU.add))
            for g in range(G0):
                last = (g + 1) * per_group - 1
                step(v.tensor_tensor(hit[:, 0, :], count[:, last, 0, :], psS[:, last, 0, :], ALU.add))
                sec = pos[:, g * per_group:(g + 1) * per_group, 1, :]
                step(v.tensor_tensor(sec, sec, hit[:, 0, :].unsqueeze(1).to_broadcast([P, per_group, E0]), ALU.add))
            step(v.tensor_scalar(pos[:, :, :, :], pos[:, :, :, :], -1.0, None, ALU.add))
            step(v.tensor_tensor(count[:, :, :, :], pos[:, :, :, :], pick[:, :, :, :], ALU.mult))
            step(v.tensor_reduce(rank[:, :, :], count[:, :, :, :], AX.X, ALU.add))
            step(v.tensor_tensor(pos[:, :, :, :], pos[:, :, :, :], offset[:, :, :, :], ALU.add))
            step(v.tensor_tensor(count[:, :, :, :], pos[:, :, :, :], pick[:, :, :, :], ALU.mult))
            step(v.tensor_reduce(slot[:, :, :], count[:, :, :, :], AX.X, ALU.add))
            step(v.tensor_scalar(kept[:, :, :], rank[:, :, :], float(C0), None, ALU.is_lt))
            step(v.tensor_scalar(lost[:, :, :], kept[:, :, :], -SKIP, SKIP, ALU.mult, ALU.add))
            step(v.tensor_tensor(lost[:, :, :], lost[:, :, :], slot[:, :, :], ALU.add))
            step(v.tensor_copy(s.place[:, :, :], lost[:, :, :]))
            step(v.tensor_tensor(slot[:, :, :], slot[:, :, :], kept[:, :, :], ALU.mult))
            step(v.tensor_copy(s.fetch[:, :, :], slot[:, :, :]))
            step(v.tensor_tensor(s.gate[:, :, :], kept[:, :, :], best[:, :, :].rearrange("p c t -> p t c"), ALU.mult))

        @block.scalar
        def _(act):
            act.wait_ge(shifted, 1)
            nc.scalar.activation(prob[:, :, :], prob[:, :, :], ACT.Exp).then_inc(raised, 1)

        @block.tensor
        def _(pe):
            pe.wait_ge(picked, 1)
            rhs = pick_b[:, :, :, :].rearrange("p t c e -> p (t c e)")
            nc.tensor.matmul(psC[:, :, :, :].rearrange("p t c e -> p (t c e)"), tri[:, :], rhs, start=True, stop=True)
            nc.tensor.matmul(psS[:, :, :, :].rearrange("p t c e -> p (t c e)"), ones[:, :], rhs, start=True, stop=True).then_inc(counted, 1)


def phase_scatter(nc, d, s, tag, rows, choices, n_rows, fill):
    with ExitStack() as ctx:
        k = Scope(nc, ctx, tag)
        zeros = k.sb("zeros", [P, fill // P, D])
        xs = k.sb("xs", [P, 2, D])
        idx = k.sb("idx", [P, 2, choices, 1], U32)
        cleared, filled, xs_ready, passed, sent0, sent1 = k.sems("cleared filled xs_ready passed sent0 sent1")
        sent = (sent0, sent1)
        block = ctx.enter_context(nc.Block())

        @block.sync
        def _(sp):
            sp.wait_ge(cleared, 1)
            n = n_rows // fill
            view = rows.rearrange("(n p j) e -> n p j e", p=P, j=fill // P)
            for i in range(n):
                sp.dma_start(view[i], zeros[:, :, :]).then_inc(filled, 16)
            sp.wait_ge(filled, 16 * n)

        @block.vector
        def _(dve):
            nc.vector.memset(zeros[:, :, :], 0.0).then_inc(cleared, 1)

            def tile(t, r, wait):
                if wait is not None:
                    dve.wait_ge(sent[r], wait)
                nc.vector.tensor_copy(idx[:, r, :, :].rearrange("p c a -> p (c a)"), flat(s.place[:, bass.ds(t, 1), :]))
                nc.vector.tensor_scalar(xs[:, r, :], flat(s.xc[:, bass.ds(t, 1), :]), s.rstd[:, bass.ds(t, 1)], None,
                                        ALU.mult).then_inc(xs_ready, 1)

            for r in range(2):
                tile(r, r, None)
            with dve.Fori(1, NT // 2) as i:
                for r in range(2):
                    tile(i * 2 + r, r, i * (16 * choices))

        @block.gpsimd
        def _(pool):
            pool.wait_ge(filled, 16 * (n_rows // fill))
            with pool.Fori(0, NT // 2) as i:
                for r in range(2):
                    pool.wait_ge(xs_ready, i * 2 + r + 1)
                    pool.sem_inc(passed, 1)
                    for c in range(choices):
                        nc.gpsimd.indirect_dma_start(
                            out=rows, out_offset=bass.IndirectOffsetOnAxis(ap=idx[:, r, c, :], axis=0),
                            in_=xs[:, r, :], in_offset=None, bounds_check=n_rows - 1, oob_is_err=False).then_inc(sent[r], 16)
            for r in range(2):
                pool.wait_ge(sent[r], NT // 2 * 16 * choices)


def phase_experts0(nc, d, s):
    with ExitStack() as ctx:
        k = Scope(nc, ctx, "e")
        FC = F0 // P
        R = G0 * C0
        x = k.sb("x", [C0, 2, G0, D])
        wi = k.sb("wi", [P, 2, F0])
        wo = k.sb("wo", [P, 2, FC, D])
        xT = k.sb("xT", [P, 2, R])
        hT = k.sb("hT", [P, 2, FC, R])
        o = k.sb("o", [C0, 2, G0, D])
        psX = k.ps("psX", [P, 2, 512])
        psH = k.ps("psH", [P, 4, 512])
        psO = k.ps("psO", [P, 2, 512])
        ld0, ld1, turned, xT_ready, hid, h_ready, outed, o_ready, st0, st1 = k.sems("ld0 ld1 turned xT_ready hid h_ready outed o_ready st0 st1")
        ld, st = (ld0, ld1), (st0, st1)
        block = ctx.enter_context(nc.Block())
        rows_in = d["xin"].rearrange("(g e c) h -> e c g h", g=G0, e=E0)
        rows_out = d["eout"].rearrange("(g e c) h -> e c g h", g=G0, e=E0)
        wo_v = d["wo"].rearrange("e (f p) h -> e p f h", p=P)

        @block.sync
        def _(sp):
            def load(e, r):
                one = bass.ds(e, 1)
                sp.dma_start(x[:, r, :, :], rows_in[one].rearrange("a c g h -> c (a g) h")).then_inc(ld[r], 16)
                sp.dma_start(wi[:, r, :], d["wi"][one].rearrange("a h f -> h (a f)")).then_inc(ld[r], 16)
                sp.dma_start(wo[:, r, :, :], wo_v[one].rearrange("a p f h -> p (a f) h")).then_inc(ld[r], 16)

            def store(e, r):
                sp.wait_ge(o_ready, e * G0 + G0)
                sp.dma_start(rows_out[bass.ds(e, 1)].rearrange("a c g h -> c (a g) h"), o[:, r, :, :]).then_inc(st[r], 16)

            for r in range(2):
                load(r, r)
            with sp.Fori(0, E0 // 2 - 1) as i:
                for r in range(2):
                    store(i * 2 + r, r)
                    load(i * 2 + r + 2, r)
            for r in range(2):
                store(E0 - 2 + r, r)
                sp.wait_ge(st[r], E0 // 2 * 16)

        @block.tensor
        def _(pe):
            with pe.Fori(0, E0 // 2) as i:
                for r in range(2):
                    e = i * 2 + r
                    pe.wait_ge(ld[r], (i + 1) * 48)
                    for g in range(G0):
                        ins = nc.tensor.transpose(psX[:, r, g * C0:(g + 1) * C0], x[:, r, g, :], s.ident[0:C0, 0:C0])
                    ins.then_inc(turned, 1)
                    pe.wait_ge(xT_ready, e + 1)
                    for f in range(FC):
                        pe.wait_ge(h_ready, e * FC)
                        nc.tensor.matmul(psH[:, f, 0:R], wi[:, r, f * P:(f + 1) * P], xT[:, r, :], start=True, stop=True).then_inc(hid, 1)
                    pe.wait_ge(h_ready, e * FC + FC)
                    pe.wait_ge(o_ready, e * G0)
                    for g in range(G0):
                        for f in range(FC):
                            ins = nc.tensor.matmul(psO[0:C0, g, 0:D], hT[:, r, f, g * C0:(g + 1) * C0], wo[:, r, f, :],
                                                   start=f == 0, stop=f == FC - 1)
                        ins.then_inc(outed, 1)

        @block.scalar
        def _(act):
            with act.Fori(0, E0 // 2) as i:
                for r in range(2):
                    for f in range(FC):
                        act.wait_ge(hid, (i * 2 + r) * FC + f + 1)
                        nc.scalar.activation(hT[:, r, f, :], psH[:, f, 0:R], ACT.Relu).then_inc(h_ready, 1)

        @block.vector
        def _(dve):
            with dve.Fori(0, E0 // 2) as i:
                for r in range(2):
                    e = i * 2 + r
                    dve.wait_ge(turned, e + 1)
                    nc.vector.tensor_copy(xT[:, r, :], psX[:, r, 0:R]).then_inc(xT_ready, 1)
                    dve.wait_ge(st[r], i * 16)
                    for g in range(G0):
                        dve.wait_ge(outed, e * G0 + g + 1)
                        nc.vector.tensor_copy(o[:, r, g, :], psO[0:C0, g, 0:D]).then_inc(o_ready, 1)


def phase_gather(nc, d, s, tag, rows, choices, weight, out):
    with ExitStack() as ctx:
        k = Scope(nc, ctx, tag)
        got = k.sb("got", [P, 2, choices, D])
        idx = k.sb("idx", [P, 2, choices, 1], U32)
        acc = k.sb("acc", [P, 2, D])
        idx_ready, passed, got0, got1, dv, summed, gated = k.sems("idx_ready passed got0 got1 dv summed gated")
        arrived = (got0, got1)
        block = ctx.enter_context(nc.Block())

        @block.vector
        def _(dve):
            step = Tally(dve, dv)

            def index(t, r):
                nc.vector.tensor_copy(idx[:, r, :, :].rearrange("p c a -> p (c a)"), flat(s.fetch[:, bass.ds(t, 1), :])).then_inc(idx_ready, 1)

            def combine(t, i, r, base):
                step = Tally(dve, dv, base)
                dve.wait_ge(arrived[r], (i + 1) * (16 * choices))
                dve.wait_ge(gated, t)
                w = flat(weight[:, bass.ds(t, 1), :])
                step(nc.vector.tensor_scalar(acc[:, r, :], got[:, r, 0, :], w[:, 0:1], None, ALU.mult))
                for c in range(1, choices):
                    ins = nc.vector.scalar_tensor_tensor(acc[:, r, :], got[:, r, c, :], w[:, c:c + 1], acc[:, r, :], ALU.mult, ALU.add)
                    if c < choices - 1:
                        step(ins)
                ins.then_inc(summed, 1)
                assert step.n == choices - 1

            for r in range(2):
                index(r, r)
            with dve.Fori(0, NT // 2 - 1) as i:
                for r in range(2):
                    combine(i * 2 + r, i, r, (i * 2 + r) * (choices - 1))
                    index(i * 2 + r + 2, r)
            for r in range(2):
                combine(NT - 2 + r, NT // 2 - 1, r, (NT - 2 + r) * (choices - 1))

        @block.gpsimd
        def _(pool):
            with pool.Fori(0, NT // 2) as i:
                for r in range(2):
                    t = i * 2 + r
                    pool.wait_ge(idx_ready, t + 1)
                    pool.wait_ge(summed, i * 2)
                    pool.sem_inc(passed, 1)
                    for c in range(choices):
                        nc.gpsimd.indirect_dma_start(
                            out=got[:, r, c, :], out_offset=None, in_=rows,
                            in_offset=bass.IndirectOffsetOnAxis(ap=idx[:, r, c, :], axis=0)).then_inc(arrived[r], 16)

        @block.scalar
        def _(act):
            with act.Fori(0, NT // 2) as i:
                for r in range(2):
                    t = i * 2 + r
                    act.wait_ge(summed, t + 1)
                    nc.scalar.activation(flat(out[:, bass.ds(t, 1), :]), acc[:, r, :], ACT.Silu).then_inc(gated, 1)

NH, DK = 16, 8
HG = 4
UN = B * NH // HG
COMBOS = [(i, j) for i in range(3) for j in range(3)]
KR = 9 * DK
NEG = -1e30
INV_SQRT_DK = float(1.0 / np.sqrt(np.float32(DK)))


def phase_output0(nc, d, s):
    with ExitStack() as ctx:
        k = Scope(nc, ctx, "o")
        lnw, lnb = k.sb("lnw", [P, DI]), k.sb("lnb", [P, DI])
        wout = k.sb("wout", [P, 2, D])
        y, hd, z = (k.sb(n, [P, 2, TQ, DI]) for n in ("y", "hd", "z"))
        x = k.sb("x", [P, 2, TQ, D])
        sq = k.sb("sq", [P, TQ, DI])
        mean, var, std, inv = (k.sb(n, [P, TQ]) for n in ("mean", "var", "std", "inv"))
        yT = k.sb("yT", [P, 2, TQ, P])
        sg = k.sb("sg", [P, TQ, D])
        psT = k.ps("psT", [P, 2, 2, TQ, P])
        psO = k.ps("psO", [P, 2, TQ, D])
        (loaded, in0, in1, dv, centred, squared, var_ready, std_ready, scaled, shifted, turned, yT_ready, outed, x_ready, stored) = k.sems(
            "loaded in0 in1 dv centred squared var_ready std_ready scaled shifted turned yT_ready outed x_ready stored")
        arrived = (in0, in1)
        block = ctx.enter_context(nc.Block())
        per_b = TQ + 6

        @block.sync
        def _(sp):
            sp.dma_start(lnw[:, :], d["ln_w"]).then_inc(loaded, 16)
            sp.dma_start(lnb[:, :], d["ln_b"]).then_inc(loaded, 16)
            sp.dma_start(wout[:, :, :], d["wout"].rearrange("(c p) o -> p c o", p=P)).then_inc(loaded, 16)

            def load(b, r):
                one = bass.ds(b, 1)
                for dst, name in ((y, "y"), (hd, "hdx"), (z, "z"), (x, "x")):
                    sp.dma_start(dst[:, r, :, :], d[name][one].rearrange("a (q p) e -> p (a q) e", p=P)).then_inc(arrived[r], 16)

            for r in range(2):
                load(r, r)
            with sp.Fori(0, B // 2 - 1) as i:
                for r in range(2):
                    sp.wait_ge(x_ready, i * 2 + r + 1)
                    load(i * 2 + r + 2, r)
            sp.wait_ge(x_ready, B)
            sp.dma_start(d["x1"].rearrange("b (q p) e -> p (b q) e", p=P), s.xc[:, :, :]).then_inc(stored, 16)
            sp.wait_ge(stored, 16)

        @block.vector
        def _(dve):
            v = nc.vector
            dve.wait_ge(loaded, 48)

            def sequence(i, r):
                b = i * 2 + r
                step = Tally(dve, dv, b * per_b)
                yb, hb, zb = y[:, r], hd[:, r], z[:, r]
                dve.wait_ge(arrived[r], (i + 1) * 64)
                for q in range(TQ):
                    step.mark(v.scalar_tensor_tensor(yb[:, q, :], hb[:, q, :], s.kappa[:, q, bass.ds(b, 1)], yb[:, q, :], ALU.mult, ALU.add))
                step.settle()
                step(v.tensor_tensor(yb, yb, zb, ALU.mult))
                step(v.tensor_reduce(mean[:, :], yb, AX.X, ALU.add))
                step(v.tensor_scalar(mean[:, :], mean[:, :], 1.0 / DI, None, ALU.mult))
                v.tensor_tensor(yb, yb, over(mean[:, :], DI), ALU.subtract).then_inc(centred, 1)
                dve.wait_ge(squared, b + 1)
                step(v.tensor_reduce(var[:, :], sq[:, :, :], AX.X, ALU.add))
                v.tensor_scalar(var[:, :], var[:, :], 1.0 / DI, None, ALU.mult).then_inc(var_ready, 1)
                dve.wait_ge(std_ready, b + 1)
                step(v.reciprocal(inv[:, :], std[:, :]))
                v.tensor_tensor(yb, yb, over(inv[:, :], DI), ALU.mult).then_inc(scaled, 1)
                dve.wait_ge(outed, b + 1)
                rows = bass.ds(b * TQ, TQ)
                step(v.tensor_tensor(sg[:, :, :], psO[:, r, :, :], s.g0[:, rows, :], ALU.mult))
                v.tensor_tensor(s.xc[:, rows, :], sg[:, :, :], x[:, r, :, :], ALU.add).then_inc(x_ready, 1)
                assert step.n == per_b

            with dve.Fori(0, B // 2) as i:
                for r in range(2):
                    sequence(i, r)

        @block.gpsimd
        def _(pool):
            pool.wait_ge(loaded, 48)
            with pool.Fori(0, B // 2) as i:
                for r in range(2):
                    pool.wait_ge(scaled, i * 2 + r + 1)
                    wide = [P, TQ, DI]
                    nc.gpsimd.tensor_tensor(z[:, r], y[:, r], lnw[:, :].unsqueeze(1).to_broadcast(wide), ALU.mult).then_inc(shifted, 1)
                    pool.wait_ge(shifted, (i * 2 + r) * 2 + 1)
                    nc.gpsimd.tensor_tensor(hd[:, r], z[:, r], lnb[:, :].unsqueeze(1).to_broadcast(wide), ALU.add).then_inc(shifted, 1)

        @block.tensor
        def _(pe):
            pe.wait_ge(loaded, 48)
            with pe.Fori(0, B // 2) as i:
                for r in range(2):
                    b = i * 2 + r
                    pe.wait_ge(shifted, b * 2 + 2)
                    for c in range(2):
                        for q in range(TQ):
                            ins = nc.tensor.transpose(psT[:, r, c, q, :], hd[:, r, q, c * P:(c + 1) * P], s.ident[:, :])
                        ins.then_inc(turned, 1)
                    pe.wait_ge(yT_ready, b * 2 + 2)
                    for q in range(TQ):
                        for c in range(2):
                            ins = nc.tensor.matmul(psO[:, r, q, :], yT[:, c, q, :], wout[:, c, :], start=c == 0, stop=c == 1)
                    ins.then_inc(outed, 1)

        @block.scalar
        def _(act):
            with act.Fori(0, B // 2) as i:
                for r in range(2):
                    b = i * 2 + r
                    act.wait_ge(centred, b + 1)
                    nc.scalar.activation(sq[:, :, :], y[:, r], ACT.Square).then_inc(squared, 1)
                    act.wait_ge(var_ready, b + 1)
                    nc.scalar.activation(std[:, :], var[:, :], ACT.Sqrt, bias=s.eps[:, 0:1]).then_inc(std_ready, 1)
                    for c in range(2):
                        act.wait_ge(turned, b * 2 + c + 1)
                        nc.scalar.activation(yT[:, c, :, :], psT[:, r, c, :, :], ACT.Copy).then_inc(yT_ready, 1)


def phase_qkv(nc, d, s):
    with ExitStack() as ctx:
        k = Scope(nc, ctx, "q")
        w = k.sb("w", [P, 5, D])
        cos, sin = k.sb("cos", [P, L]), k.sb("sin", [P, L])
        xs = k.sb("xs", [P, TQ, D])
        xT = k.sb("xT", [P, L])
        prod = k.sb("prod", [P, 2, L])
        qk = k.sb("qk", [P, 2, L])
        rest = k.sb("rest", [P, 2, L])
        parts = k.sb("parts", [P, 2, 2, 3, L], BF16)
        psT = k.ps("psT", [P, TQ, P])
        psP = k.ps("psP", [P, 4, L])
        psV = k.ps("psV", [P, TQ, D])
        (loaded, dv, xs_ready, turned, xT_ready, projected, v_projected, v_copied, qk_ready, high, rested, mid, low, slot_free, out0, out1) = k.sems(
            "loaded dv xs_ready turned xT_ready projected v_projected v_copied qk_ready high rested mid low slot_free out0 out1")
        out = (out0, out1)
        block = ctx.enter_context(nc.Block())

        @block.sync
        def _(sp):
            sp.dma_start(w[:, :, :], d["w_qkv"]).then_inc(loaded, 16)
            sp.dma_start(cos[:, :], d["rope_cos"]).then_inc(loaded, 16)
            sp.dma_start(sin[:, :], d["rope_sin"]).then_inc(loaded, 16)
            with sp.Fori(0, B // 2) as i:
                for r in range(2):
                    b = i * 2 + r
                    sp.wait_ge(low, b * 2 + 2)
                    for c, (pq, pk) in enumerate(COMBOS):
                        for m, part in ((0, pq), (1, pk)):
                            sp.dma_start(d["qk9"][m, bass.ds(b, 1), :, c].rearrange("a h k t -> (a h) k t"), parts[:, r, m, part, :]).then_inc(out[r], 16)
                    sp.wait_ge(out[r], (i + 1) * (18 * 16))
                    sp.sem_inc(slot_free, 1)

        @block.vector
        def _(dve):
            v = nc.vector
            dve.wait_ge(loaded, 48)
            with dve.Fori(0, B) as b:
                step = Tally(dve, dv, b * 4)
                dve.wait_ge(turned, b)
                rows = bass.ds(b * TQ, TQ)
                v.tensor_tensor(xs[:, :, :], s.xc[:, rows, :], over(s.rstd[:, rows], D), ALU.mult).then_inc(xs_ready, 1)
                dve.wait_ge(low, b * 2)
                for m in range(2):
                    dve.wait_ge(projected, b * 2 + m + 1)
                    step.mark(v.tensor_tensor(qk[:, m, :], psP[:, 2 * m, :], cos[:, :], ALU.mult))
                    step(v.tensor_tensor(prod[:, m, :], psP[:, 2 * m + 1, :], sin[:, :], ALU.mult))
                    v.tensor_tensor(qk[:, m, :], qk[:, m, :], prod[:, m, :], ALU.add).then_inc(qk_ready, 1)

        @block.tensor
        def _(pe):
            pe.wait_ge(loaded, 48)
            with pe.Fori(0, B) as b:
                pe.wait_ge(xs_ready, b + 1)
                for q in range(TQ):
                    ins = nc.tensor.transpose(psT[:, q, :], xs[:, q, :], s.ident[:, :])
                ins.then_inc(turned, 1)
                pe.wait_ge(xT_ready, b + 1)
                pe.wait_ge(qk_ready, b * 2)
                pe.wait_ge(v_copied, b)
                for m in range(2):
                    for n in range(2):
                        ins = nc.tensor.matmul(psP[:, 2 * m + n, :], w[:, 2 * m + n, :], xT[:, :], start=True, stop=True)
                    ins.then_inc(projected, 1)
                for q in range(TQ):
                    ins = nc.tensor.matmul(psV[:, q, :], xT[:, q * P:(q + 1) * P], w[:, 4, :], start=True, stop=True)
                ins.then_inc(v_projected, 1)

        @block.scalar
        def _(act):
            act.sem_inc(slot_free, 2)
            with act.Fori(0, B // 2) as i:
                for r in range(2):
                    b = i * 2 + r
                    act.wait_ge(turned, b + 1)
                    act.wait_ge(v_projected, b)
                    nc.scalar.activation(xT[:, :], psT[:, :, :].rearrange("p q t -> p (q t)"), ACT.Copy).then_inc(xT_ready, 1)
                    act.wait_ge(slot_free, b + 1)
                    for m in range(2):
                        act.wait_ge(qk_ready, b * 2 + m + 1)
                        nc.scalar.activation(parts[:, r, m, 0, :], qk[:, m, :], ACT.Copy).then_inc(high, 1)
                    act.wait_ge(v_projected, b + 1)
                    nc.scalar.activation(s.v[:, bass.ds(b * TQ, TQ), :], psV[:, :, :], ACT.Copy).then_inc(v_copied, 1)
                    for m in range(2):
                        act.wait_ge(rested, b * 2 + m + 1)
                        nc.scalar.activation(parts[:, r, m, 1, :], rest[:, m, :], ACT.Copy).then_inc(mid, 1)

        @block.gpsimd
        def _(pool):
            with pool.Fori(0, B // 2) as i:
                for r in range(2):
                    b = i * 2 + r
                    pool.wait_ge(low, b * 2)
                    for m in range(2):
                        pool.wait_ge(high, b * 2 + m + 1)
                        nc.gpsimd.tensor_tensor(rest[:, m, :], qk[:, m, :], parts[:, r, m, 0, :], ALU.subtract).then_inc(rested, 1)
                    for m in range(2):
                        pool.wait_ge(mid, b * 2 + m + 1)
                        nc.gpsimd.tensor_tensor(parts[:, r, m, 2, :], rest[:, m, :], parts[:, r, m, 1, :], ALU.subtract).then_inc(low, 1)

GROUPS = [(0, h, 1) for h in range(HG)] + [(1, h, 1) for h in range(HG)] + [(2, 0, 2), (2, 2, 2)] + [(3, 0, HG)]
NG = len(GROUPS)
ENDS = [4, 8, 10, 11]
HB = B // 2


def phase_attention(nc, d, s):
    with ExitStack() as ctx:
        k = Scope(nc, ctx, "a")
        q = k.sb("q", [KR + 1, 4, HG, L], BF16)
        key = k.sb("key", [KR + 1, 4, HG, L], BF16)
        mask_f, mask = k.sb("mask_f", [P, 2, P]), k.sb("mask", [P, 2, P], BF16)
        eye = k.sb("eye", [P, P], BF16)
        top = k.sb("top", [P, 2, HG, TQ])
        top_row = k.sb("top_row", [HG * TQ, 2, P], BF16)
        pt = k.sb("pt", [P, 2, HG, L])
        vaug = k.sb("vaug", [P, 2, TQ, HG, 32])
        ot = k.sb("ot", [P, 2, L])
        inv = k.sb("inv", [P, TQ, HG])
        psA = k.ps("psA", [P, 2, 512])
        psB = k.ps("psB", [P, 2, 512])
        psO = k.ps("psO", [P, 512])
        psT = k.ps("psT", [P, TQ, HG, 32])
        psM = k.ps("psM", [P, 512])
        (loaded, dv, consts, key_wiped, ld0, ld1, ld2, ld3, mr0, mr1, mr2, mr3, scored, maxed, top_turned, top_ready, rev_scored, raised, v_ready, summed,
         o_copied, o_turned, o_ready, wiped) = k.sems(
            "loaded dv consts key_wiped ld0 ld1 ld2 ld3 mr0 mr1 mr2 mr3 scored maxed top_turned top_ready rev_scored raised v_ready summed "
            "o_copied o_turned o_ready wiped")
        ld, row_in = (ld0, ld1, ld2, ld3), (mr0, mr1, mr2, mr3)
        block = ctx.enter_context(nc.Block())

        def run(eng, unit, finish):
            for hg in range(4):
                unit(0, hg, True, False)
            with eng.Fori(1, B - 1) as i:
                for hg in range(4):
                    unit(i, hg, False, False)
            for hg in range(4):
                unit(B - 1, hg, False, True)
            finish()

        @block.sync
        def _(sp):
            sp.dma_start(mask_f[:, :, :], d["mask"]).then_inc(loaded, 16)

            def load(i, hg):
                for m, dst in ((0, q), (1, key)):
                    sp.dma_start(dst[0:KR, hg, :, :], d["qk9"][m, bass.ds(i, 1), hg * HG:(hg + 1) * HG].rearrange("a h c k t -> (a c k) h t")).then_inc(ld[hg], 16)

            def row(n, hg):
                sp.wait_ge(top_ready, n + 1)
                sp.dma_start(q[KR:KR + 1, hg, :, :], top_row[:, (hg % 2), :]).then_inc(row_in[hg], 16)

            def unit(i, hg, first, last):
                if not (first and hg == 0) and not (last and hg == 3):
                    row(i * 4 + hg + 1, (hg + 1) % 4)
                if not last:
                    sp.wait_ge(rev_scored, (i * 4 + hg + 1) * NG)
                    load(i + 1, hg)

            sp.wait_ge(key_wiped, 1)
            for hg in range(4):
                load(0, hg)
            for n in range(2):
                row(n, n)
            run(sp, unit, lambda: None)

        def max_groups(g):
            far, h0, hn = GROUPS[g]
            return TQ - 1 - far, h0, hn, (TQ - far) * P

        @block.tensor
        def _(pe):
            pe.wait_ge(consts, 1)

            def scores(n, slot, g):
                qt, h0, hn, w = max_groups(g)
                bank = (slot * NG + g) % 2
                if not isinstance(n, int) or n * NG + g > 1:
                    pe.wait_ge(maxed, n * NG + g - 1)
                for j in range(hn):
                    h, lo = h0 + j, j * w
                    nc.tensor.matmul(psA[:, bank, lo:lo + w], q[0:KR, slot, h, qt * P:(qt + 1) * P], key[0:KR, slot, h, 0:w], start=True, stop=False)
                    ins = nc.tensor.matmul(psA[:, bank, lo + w - P:lo + w], eye[:, :], mask[:, 0, :], start=False, stop=True)
                ins.then_inc(scored, 1)

            def reversed_scores(n, slot, g):
                kt, h0, hn = GROUPS[g]
                w = (TQ - kt) * P
                bank = (slot * NG + g) % 2
                if not isinstance(n, int) or n * NG + g > 1:
                    pe.wait_ge(raised, n * NG + g - 1)
                for j in range(hn):
                    h, lo = h0 + j, j * w
                    nc.tensor.matmul(psB[:, bank, lo:lo + w], key[:, slot, h, kt * P:(kt + 1) * P], q[:, slot, h, kt * P:L], start=True, stop=False)
                    ins = nc.tensor.matmul(psB[:, bank, lo:lo + P], eye[:, :], mask[:, 1, :], start=False, stop=True)
                ins.then_inc(rev_scored, 1)

            def turn_top(n, r):
                pe.wait_ge(maxed, (n + 1) * NG)
                if not isinstance(n, int) or n:
                    pe.wait_ge(top_ready, n)
                nc.tensor.transpose(psM[0:HG * TQ, 0:P], flat(top[:, r, :, :]), s.ident[:, :]).then_inc(top_turned, 1)

            def sum_v(n, slot, kt):
                pe.wait_ge(raised, n * NG + ENDS[kt])
                if kt == 0:
                    pe.wait_ge(v_ready, n + 1)
                    if not isinstance(n, int) or n:
                        pe.wait_ge(o_copied, n)
                for h in range(HG):
                    ins = nc.tensor.matmul(psO[32 * h:32 * h + 32, kt * P:L], vaug[:, slot % 2, kt, h, :], pt[:, kt % 2, h, 0:L - kt * P], start=kt == 0, stop=kt == TQ - 1)
                ins.then_inc(summed, 1)

            def turn_o(n, r):
                pe.wait_ge(o_copied, n + 1)
                if not isinstance(n, int) or n:
                    pe.wait_ge(o_ready, n)
                for qt in range(TQ):
                    ins = nc.tensor.transpose(flat(psT[:, qt, :, :]), ot[:, r, qt * P:(qt + 1) * P], s.ident[:, :])
                ins.then_inc(o_turned, 1)

            def unit(i, hg, first, last):
                n = i * 4 + hg
                ahead = not (last and hg >= 2)
                for g in range(NG):
                    if g == 0:
                        if ahead:
                            pe.wait_ge(ld[(hg + 2) % 4], (i + 1 + (hg >= 2)) * 32)
                        pe.wait_ge(row_in[hg], (i + 1) * 16)
                    if ahead:
                        scores(n + 2, (hg + 2) % 4, g)
                    reversed_scores(n, hg, g)
                    if g == 2 and not (first and hg == 0) and not (last and hg == 3):
                        turn_top(n + 1, (hg + 1) % 2)
                    if g == 4 and not (first and hg == 0):
                        turn_o(n - 1, (hg + 1) % 2)
                    if g == 5:
                        sum_v(n, hg, 0)
                    if g == 9:
                        sum_v(n, hg, 1)
                sum_v(n, hg, 2)
                sum_v(n, hg, 3)

            for n in range(2):
                pe.wait_ge(ld[n], 32)
                for g in range(NG):
                    scores(n, n, g)
            for n in range(2):
                turn_top(n, n)
            run(pe, unit, lambda: turn_o(UN - 1, 1))

        @block.vector
        def _(dve):
            v = nc.vector
            step = Tally(dve, dv)
            nc.vector.memset(key[64:KR + 1, :, :, :], -1.0).then_inc(key_wiped, 1)
            dve.wait_ge(loaded, 16)
            step.mark(v.tensor_copy(mask[:, :, :], mask_f[:, :, :]))
            v.tensor_copy(eye[:, :], s.ident[:, :]).then_inc(consts, 1)

            def maxima(n, slot, g):
                qt, h0, hn, w = max_groups(g)
                dve.wait_ge(scored, n * NG + g + 1)
                if g == 0 and not (isinstance(n, int) and n < 2):
                    dve.wait_ge(top_turned, n - 1)
                v.tensor_reduce(top[:, slot % 2, h0:h0 + hn, qt], psA[:, (slot * NG + g) % 2, 0:hn * w].rearrange("p (h w) -> p h w", w=w),
                                AX.X, ALU.max).then_inc(maxed, 1)

            def copy_top(i, n, hg):
                dve.wait_ge(top_turned, n + 1)
                before = (hg + 2) % 4
                if not (isinstance(n, int) and n < 2):
                    dve.wait_ge(row_in[before], (i if hg < 2 else i + 1) * 16)
                v.tensor_copy(top_row[:, hg % 2, :], psM[0:HG * TQ, 0:P]).then_inc(top_ready, 1)

            def divide(i, n, hg):
                dve.wait_ge(o_turned, n + 1)
                dve.wait_ge(o_ready, n) if not (isinstance(n, int) and n == 0) else None
                v.reciprocal(inv[:, :, :], psT[:, :, :, DK]).then_inc(dv, 1)
                dve.wait_ge(dv, n + 2)
                v.tensor_tensor(s.o[:, bass.ds(i * TQ, TQ), hg * 32:hg * 32 + 32].rearrange("p q (h c) -> p q h c", c=DK), psT[:, :, :, 0:DK],
                                inv[:, :, :].unsqueeze(3).to_broadcast([P, TQ, HG, DK]), ALU.mult).then_inc(o_ready, 1)

            def unit(i, hg, first, last):
                n = i * 4 + hg
                for g in range(NG):
                    if not (last and hg >= 2):
                        maxima(n + 2, (hg + 2) % 4, g)
                    if g == 3 and not (first and hg == 0) and not (last and hg == 3):
                        copy_top(i if hg < 3 else i + 1, n + 1, (hg + 1) % 4)
                    if g == 5 and not (first and hg == 0):
                        divide(i if hg else i - 1, n - 1, (hg + 3) % 4)

            for n in range(2):
                for g in range(NG):
                    maxima(n, n, g)
            for n in range(2):
                copy_top(0, n, n)
            run(dve, unit, lambda: divide(B - 1, UN - 1, 3))

        @block.scalar
        def _(act):
            def copy_o(n, r):
                act.wait_ge(summed, (n + 1) * TQ)
                if not (isinstance(n, int) and n < 2):
                    act.wait_ge(o_turned, n - 1)
                nc.scalar.activation(ot[:, r, :], psO[:, :], ACT.Copy).then_inc(o_copied, 1)

            def unit(i, hg, first, last):
                n = i * 4 + hg
                for g in range(NG):
                    kt, h0, hn = GROUPS[g]
                    w = (TQ - kt) * P
                    act.wait_ge(rev_scored, n * NG + g + 1)
                    if g in (0, 4, 8, 10) and not (first and hg == 0 and kt < 2):
                        act.wait_ge(summed, n * TQ + kt - 1)
                    nc.scalar.activation(pt[:, kt % 2, h0:h0 + hn, 0:w], psB[:, (hg * NG + g) % 2, 0:hn * w].rearrange("p (h w) -> p h w", w=w),
                                         ACT.Exp, scale=INV_SQRT_DK).then_inc(raised, 1)
                    if g == 1 and not (first and hg == 0):
                        copy_o(n - 1, (hg + 1) % 2)

            run(act, unit, lambda: copy_o(UN - 1, 1))

        @block.gpsimd
        def _(pool):
            nc.gpsimd.memset(vaug[:, :, :, :, :], 0.0).then_inc(wiped, 1)
            pool.wait_ge(wiped, 1)
            nc.gpsimd.memset(vaug[:, :, :, :, DK:DK + 1], 1.0).then_inc(wiped, 1)
            pool.wait_ge(wiped, 2)

            def unit(i, hg, first, last):
                n = i * 4 + hg
                if not (first and hg < 2):
                    pool.wait_ge(summed, (n - 1) * TQ)
                nc.gpsimd.tensor_copy(vaug[:, hg % 2, :, :, 0:DK], s.v[:, bass.ds(i * TQ, TQ), hg * 32:hg * 32 + 32].rearrange("p q (h c) -> p q h c", c=DK)).then_inc(v_ready, 1)

            run(pool, unit, lambda: None)


def phase_attention_out(nc, d, s):
    with ExitStack() as ctx:
        k = Scope(nc, ctx, "ao")
        w = k.sb("w", [P, D])
        oT = k.sb("oT", [P, 2, TQ, P])
        psT = k.ps("psT", [P, 2, TQ, P])
        psS = k.ps("psS", [P, 2, TQ, D])
        o = k.sb("o", [P, 2, TQ, D])
        loaded, o_ready, turned, oT_ready, projected, copied = k.sems("loaded o_ready turned oT_ready projected copied")
        block = ctx.enter_context(nc.Block())

        @block.sync
        def _(sp):
            sp.dma_start(w[:, :], d["w_o"]).then_inc(loaded, 16)

        @block.tensor
        def _(pe):
            def turn(b, r):
                pe.wait_ge(o_ready, b + 1)
                for q in range(TQ):
                    ins = nc.tensor.transpose(psT[:, r, q, :], o[:, r, q, :], s.ident[:, :])
                ins.then_inc(turned, 1)

            def project(b, r):
                pe.wait_ge(oT_ready, b + 1)
                for q in range(TQ):
                    ins = nc.tensor.matmul(psS[:, r, q, :], oT[:, r, q, :], w[:, :], start=True, stop=True)
                ins.then_inc(projected, 1)

            pe.wait_ge(loaded, 16)
            for r in range(2):
                turn(r, r)
            with pe.Fori(0, HB - 1) as i:
                for r in range(2):
                    b = i * 2 + r
                    pe.wait_ge(copied, i * 2)
                    project(b, r)
                    turn(b + 2, r)
            for r in range(2):
                pe.wait_ge(copied, (HB - 1) * 2)
                project(B - 2 + r, r)

        @block.vector
        def _(dve):
            with dve.Fori(0, HB) as i:
                for r in range(2):
                    b = i * 2 + r
                    dve.wait_ge(turned, b + 1)
                    dve.wait_ge(projected, i * 2)
                    nc.vector.tensor_copy(oT[:, r, :, :], psT[:, r, :, :]).then_inc(oT_ready, 1)

        @block.scalar
        def _(act):
            with act.Fori(0, HB) as i:
                for r in range(2):
                    b = i * 2 + r
                    act.wait_ge(projected, b + 1)
                    nc.scalar.activation(s.s1[:, bass.ds(b * TQ, TQ), :], psS[:, r, :, :], ACT.Copy).then_inc(copied, 1)

        @block.gpsimd
        def _(pool):
            def bring(b, r):
                nc.gpsimd.tensor_copy(o[:, r, :, :], s.o[:, bass.ds(b * TQ, TQ), :]).then_inc(o_ready, 1)

            for r in range(2):
                bring(r, r)
            with pool.Fori(0, HB - 1) as i:
                for r in range(2):
                    pool.wait_ge(turned, i * 2 + r + 1)
                    bring(i * 2 + r + 2, r)

E1, K1 = 64, 4
BLK = B


def phase_route1(nc, d, s):
    with ExitStack() as ctx:
        k = Scope(nc, ctx, "u")
        sel_w = k.sb("sel_w", [P, 2 * E1])
        number = k.sb("number", [P, E1])
        xs = k.sb("xs", [P, 2, TQ, D])
        xT = k.sb("xT", [P, 2, TQ, P])
        sel, low, one = (k.sb(n, [P, NT, E1]) for n in ("sel", "low", "one"))
        best, first = k.sb("best", [P, NT]), k.sb("first", [P, NT])
        psT = k.ps("psT", [P, 2, TQ, P])
        psL = k.ps("psL", [P, 2, TQ, 2 * E1])
        loaded, dv, xs_ready, turned, xT_ready, scored, raised = k.sems("loaded dv xs_ready turned xT_ready scored raised")
        block = ctx.enter_context(nc.Block())

        @block.sync
        def _(sp):
            sp.dma_start(sel_w[:, :], d["sel_w"]).then_inc(loaded, 16)
            sp.dma_start(number[:, :], d["number1"]).then_inc(loaded, 16)

        @block.vector
        def _(dve):
            v = nc.vector
            step = Tally(dve, dv)

            def normalise(b, r):
                rows = bass.ds(b * TQ, TQ)
                v.tensor_tensor(xs[:, r, :, :], s.xc[:, rows, :], over(s.rstd[:, rows], D), ALU.mult).then_inc(xs_ready, 1)

            for r in range(2):
                normalise(r, r)
            with dve.Fori(0, HB - 1) as i:
                for r in range(2):
                    dve.wait_ge(turned, i * 2 + r + 1)
                    normalise(i * 2 + r + 2, r)
            dve.wait_ge(loaded, 32)
            dve.wait_ge(raised, B)
            step(v.tensor_scalar(low[:, :, :], sel[:, :, :], 1.0, None, ALU.add))
            step(v.reciprocal(sel[:, :, :], low[:, :, :]))
            wide = [P, NT, E1]
            for c in range(K1):
                step(v.tensor_reduce(best[:, :], sel[:, :, :], AX.X, ALU.max))
                step(v.tensor_tensor(low[:, :, :], sel[:, :, :], over(best[:, :], E1), ALU.is_lt))
                step(v.scalar_tensor_tensor(low[:, :, :], low[:, :, :], float(E1), number[:, :].unsqueeze(1).to_broadcast(wide), ALU.mult, ALU.add))
                step(v.tensor_reduce(first[:, :], low[:, :, :], AX.X, ALU.min))
                step(v.tensor_tensor(one[:, :, :], number[:, :].unsqueeze(1).to_broadcast(wide), over(first[:, :], E1), ALU.is_equal))
                if c == 0:
                    step(v.tensor_tensor(s.gates[:, :, :], one[:, :, :], over(best[:, :], E1), ALU.mult))
                else:
                    step(v.tensor_tensor(low[:, :, :], one[:, :, :], over(best[:, :], E1), ALU.mult))
                    step(v.tensor_tensor(s.gates[:, :, :], s.gates[:, :, :], low[:, :, :], ALU.add))
                if c < K1 - 1:
                    step(v.scalar_tensor_tensor(sel[:, :, :], one[:, :, :], -2.0, sel[:, :, :], ALU.mult, ALU.add))

        @block.tensor
        def _(pe):
            pe.wait_ge(loaded, 32)

            def turn(b, r):
                pe.wait_ge(xs_ready, b + 1)
                for t in range(TQ):
                    ins = nc.tensor.transpose(psT[:, r, t, :], xs[:, r, t, :], s.ident[:, :])
                ins.then_inc(turned, 1)

            def score(b, r):
                pe.wait_ge(xT_ready, b + 1)
                for t in range(TQ):
                    ins = nc.tensor.matmul(psL[:, r, t, :], xT[:, r, t, :], sel_w[:, :], start=True, stop=True)
                ins.then_inc(scored, 1)

            for r in range(2):
                turn(r, r)
            with pe.Fori(0, HB - 1) as i:
                for r in range(2):
                    pe.wait_ge(raised, i * 2)
                    score(i * 2 + r, r)
                    turn(i * 2 + r + 2, r)
            for r in range(2):
                pe.wait_ge(raised, B - 2)
                score(B - 2 + r, r)

        @block.scalar
        def _(act):
            with act.Fori(0, HB) as i:
                for r in range(2):
                    b = i * 2 + r
                    act.wait_ge(turned, b + 1)
                    act.wait_ge(scored, i * 2)
                    nc.scalar.activation(xT[:, r, :, :], psT[:, r, :, :], ACT.Copy).then_inc(xT_ready, 1)
                    act.wait_ge(xT_ready, b + 1)
                    nc.scalar.activation(s.xT[:, bass.ds(b * TQ, TQ), :], xT[:, r, :, :], ACT.Copy)
                    act.wait_ge(scored, b + 1)
                    nc.scalar.activation(sel[:, bass.ds(b * TQ, TQ), :], psL[:, r, :, 0:E1], ACT.Exp, scale=-1.0).then_inc(raised, 1)


def phase_experts1(nc, d, s):
    with ExitStack() as ctx:
        k = Scope(nc, ctx, "x")
        keys, values = k.sb("keys", [P, 2, P]), k.sb("values", [P, 2, P])
        hT = k.sb("hT", [P, 2, L])
        psH = k.ps("psH", [P, 2, L])
        psO = k.ps("psO", [P, 2, TQ, D])
        ld0, ld1, hidden, h_ready, outed, added, wiped = k.sems("ld0 ld1 hidden h_ready outed added wiped")
        ld = (ld0, ld1)
        block = ctx.enter_context(nc.Block())

        @block.sync
        def _(sp):
            def load(e, r):
                one = bass.ds(e, 1)
                sp.dma_start(keys[:, r, :], d["keys"][one].rearrange("a p h -> (a p) h")).then_inc(ld[r], 16)
                sp.dma_start(values[:, r, :], d["values"][one].rearrange("a p h -> (a p) h")).then_inc(ld[r], 16)

            for r in range(2):
                load(r, r)
            with sp.Fori(0, E1 // 2 - 1) as i:
                for r in range(2):
                    sp.wait_ge(outed, (i * 2 + r + 1) * BLK)
                    load(i * 2 + r + 2, r)

        @block.tensor
        def _(pe):
            def hide(n, r, b):
                nc.tensor.matmul(psH[:, b % 2, :], keys[:, r, :], s.xT[:, b * TQ:(b + 1) * TQ, :].rearrange("p q t -> p (q t)"), start=True, stop=True).then_inc(hidden, 1)

            with pe.Fori(0, E1 // 2) as i:
                for r in range(2):
                    n = (i * 2 + r) * BLK
                    pe.wait_ge(ld[r], (i + 1) * 32)
                    pe.wait_ge(h_ready, n)
                    hide(n, r, 0)
                    for b in range(BLK):
                        if b + 1 < BLK:
                            if b:
                                pe.wait_ge(h_ready, n + b)
                            hide(n + b + 1, r, b + 1)
                        pe.wait_ge(h_ready, n + b + 1)
                        pe.wait_ge(added, n + b)
                        for t in range(TQ):
                            ins = nc.tensor.matmul(psO[:, b % 2, t, :], hT[:, b % 2, t * P:(t + 1) * P], values[:, r, :], start=True, stop=True)
                        ins.then_inc(outed, 1)

        @block.scalar
        def _(act):
            with act.Fori(0, E1 // 2) as i:
                for r in range(2):
                    n = (i * 2 + r) * BLK
                    for b in range(BLK):
                        act.wait_ge(hidden, n + b + 1)
                        act.wait_ge(outed, n + b - 1) if b else act.wait_ge(outed, n)
                        nc.scalar.activation(hT[:, b % 2, :], psH[:, b % 2, :], ACT.Relu).then_inc(h_ready, 1)

        @block.vector
        def _(dve):
            nc.vector.memset(s.acc[:, :, :], 0.0).then_inc(wiped, 1)
            dve.wait_ge(wiped, 1)
            dve.sem_inc(added, 1)
            with dve.Fori(0, E1 // 2) as i:
                for r in range(2):
                    e = i * 2 + r
                    for b in range(BLK):
                        dve.wait_ge(outed, e * BLK + b + 1)
                        if b == 0:
                            dve.wait_ge(added, e * BLK + 1)
                        for t in range(TQ):
                            q = b * TQ + t
                            ins = nc.vector.scalar_tensor_tensor(s.acc[:, q, :], psO[:, b % 2, t, :], s.gates[:, q, bass.ds(e, 1)], s.acc[:, q, :], ALU.mult, ALU.add)
                        ins.then_inc(added, 1)


def phase_final(nc, d, s):
    with ExitStack() as ctx:
        k = Scope(nc, ctx, "z")
        x = k.sb("x", [P, NT, D])
        loaded, gated, multiplied, ready, stored = k.sems("loaded gated multiplied ready stored")
        block = ctx.enter_context(nc.Block())
        tok = "b (q p) e -> p b q e"

        def cut(ap, b):
            return ap[:, b * TQ:(b + 1) * TQ, :]

        @block.sync
        def _(sp):
            sp.dma_start(x[:, :, :], d["x1"].rearrange("b (q p) e -> p (b q) e", p=P)).then_inc(loaded, 16)
            for b in range(B):
                sp.wait_ge(ready, b + 1)
                sp.dma_start(d["out"][b].rearrange("(q p) e -> p q e", p=P), cut(x, b)).then_inc(stored, 16)
            sp.wait_ge(stored, 16 * B)

        @block.scalar
        def _(act):
            for b in range(B):
                nc.scalar.activation(cut(s.acc, b), cut(s.acc, b), ACT.Silu).then_inc(gated, 1)

        @block.vector
        def _(dve):
            for b in range(B):
                dve.wait_ge(gated, b + 1)
                nc.vector.tensor_tensor(cut(s.acc, b), cut(s.acc, b), cut(s.s1, b), ALU.mult).then_inc(multiplied, 1)
                if b == 0:
                    dve.wait_ge(loaded, 16)
                dve.wait_ge(multiplied, b + 1)
                nc.vector.tensor_tensor(cut(x, b), cut(x, b), cut(s.acc, b), ALU.add).then_inc(ready, 1)


class Shared:
    pass


def phase_start(nc, d, s, k):
    loaded, = k.sems("ident_loaded")
    with nc.Block() as block:
        @block.sync
        def _(sp):
            sp.dma_start(s.ident[:, :], d["ident"]).then_inc(loaded, 16)
            sp.wait_ge(loaded, 16)


def phase_store(nc, k, name, src, dst):
    stored, = k.sems(name)
    with nc.Block() as block:
        @block.sync
        def _(sp):
            sp.dma_start(dst.rearrange("b (q p) e -> p (b q) e", p=P), src).then_inc(stored, 16)
            sp.wait_ge(stored, 16)


def program(nc, d):
    def dram(name, shape, dt=F32):
        d[name] = nc.dram_tensor(name, shape, dt).ap()

    dram("lnp", (2, 3, 4, L, DI), BF16)
    dram("hdp", (2, 6, 4, L + 1, DI), BF16)
    dram("st0", (B, L + 1, 6 * NS), BF16)
    dram("st1", (B, L, 6 * NS), BF16)
    dram("y", (B, L, DI))
    dram("hdx", (B, L, DI))
    dram("z", (B, L, DI))
    dram("xin", (SLOTS, D))
    dram("eout", (SLOTS, D))
    dram("x1", (B, L, D))
    dram("qk9", (2, B, NH, 9, DK, L), BF16)
    s = Shared()
    Scope.taken = []
    with ExitStack() as whole:
        k = Scope(nc, whole, "s")
        s.ident, s.eps, s.rstd = k.sb("ident", [P, P]), k.sb("eps", [P, 1]), k.sb("rstd", [P, NT])
        s.xc = k.sb("xc", [P, NT, D])
        phase_start(nc, d, s, k)
        with ExitStack() as layer0:
            k0 = Scope(nc, layer0, "s0")
            s.g0 = k0.sb("g0", [P, NT, D])
            s.kappa = k0.sb("kappa", [P, TQ, B])
            with ExitStack() as before_output:
                k1 = Scope(nc, before_output, "s1")
                s.bcr = k1.sb("bcr", [P, NT, WC - 3 * DI])
                with ExitStack() as projections:
                    k2 = Scope(nc, projections, "s2")
                    s.xi, s.pre = k2.sb("xi", [P, NT, DI]), k2.sb("pre", [P, NT, DI])
                    with ExitStack() as tokens:
                        k3 = Scope(nc, tokens, "s3")
                        s.zp = k3.sb("zp", [P, NT, DI])
                        s.place, s.fetch = k3.sb("place", [P, NT, 2], U32), k3.sb("fetch", [P, NT, 2], U32)
                        s.gate = k3.sb("gate", [P, NT, 2])
                        phase_norm(nc, d, s, "n0", d["x"])
                        phase_project(nc, d, s)
                        phase_route0(nc, d, s)
                        phase_scatter(nc, d, s, "d0", d["xin"], 2, SLOTS, SLOTS)
                        phase_experts0(nc, d, s)
                        phase_gather(nc, d, s, "h0", d["eout"], 2, s.gate, s.g0)
                        phase_store(nc, k3, "z_stored", s.zp[:, :, :], d["z"])
                    phase_steps(nc, d, s)
                    phase_store(nc, k2, "hdx_stored", s.xi[:, :, :], d["hdx"])
                k4 = Scope(nc, before_output, "s4")
                s.cos_c, s.sin_c = k4.sb("cos_c", [P, L]), k4.sb("sin_c", [P, L])
                s.c_col = k4.sb("c_col", [P, 2, L])
                s.marg = k4.sb("marg", [108, 2, CH, 2, DI], BF16)
                phase_rotation(nc, d, s)
                phase_scan(nc, d, s)
            phase_output0(nc, d, s)
        Scope.clear_all(nc)
        s.s1 = k.sb("s1", [P, NT, D])
        phase_norm(nc, d, s, "n1", None)
        with ExitStack() as attention:
            k6 = Scope(nc, attention, "s6")
            s.v, s.o = k6.sb("v", [P, NT, D]), k6.sb("o", [P, NT, D])
            phase_qkv(nc, d, s)
            phase_attention(nc, d, s)
            phase_attention_out(nc, d, s)
        s.xT, s.gates, s.acc = k.sb("xT", [P, NT, D]), k.sb("gates", [P, NT, E1]), k.sb("acc", [P, NT, D])
        phase_route1(nc, d, s)
        phase_experts1(nc, d, s)
        phase_final(nc, d, s)


def lay_out(inputs):
    w = {name: np.asarray(a) for name, a in inputs.items()}
    state = np.arange(P) % NS
    rows = lambda a: np.tile(a, (P, 1))
    f = {"x": w["L0_attn_x"], "ident": np.eye(P, dtype=np.float32)}
    f["wcat"] = np.concatenate([w["L0_attn_W_in"].T, w["L0_attn_W_dt"].T, w["L0_attn_W_B"].T, w["L0_attn_W_C"].T, w["L0_ffn_w_router"]], 1)
    f["b_dt"], f["dt_bias"] = rows(w["L0_attn_b_dt"]), rows(w["L0_attn_dt_bias"])
    freq = w["L0_attn_rope_freq"]
    f["freq"], f["freq_col"] = rows(freq), np.tile(freq, 2 * 4)[:, None]
    f["sign_col"] = np.where(state < HALF, 1.0, -1.0)[:, None]
    f["steps"] = np.arange(L).reshape(TQ, P).T
    f["steps_row"] = rows(np.arange(L))
    f["alog"] = np.tile(w["L0_attn_A_log"].T, (3, 1))
    at = np.arange(P)
    group = at // NS
    same = group[:, None] == group[None]
    f["eye_j"] = np.stack([np.eye(P), same & ((at[:, None] + HALF) % NS == state[None])], 1)
    f["mask4"] = group[:, None] == np.arange(4)[None]
    r = np.arange(3 * NS + 12)
    f["sel"] = np.where(r[:, None] < 3 * NS, r[:, None] % NS == state[None], (r[:, None] - 3 * NS) % 4 == group[None])
    f["tri"] = at[:, None] <= at[None]
    f["number"] = np.tile(np.arange(E0), (P, NT, 1))
    f["offset"] = np.broadcast_to((np.arange(NT) // (NT // G0) * E0 * C0)[None, :, None, None] + (np.arange(E0) * C0), (P, NT, 2, E0))
    f["wi"], f["wo"] = w["L0_ffn_wi"], w["L0_ffn_wo"]
    f["ln_w"], f["ln_b"] = rows(w["L0_attn_ln_w"]), rows(w["L0_attn_ln_b"])
    f["wout"] = w["L0_attn_W_out"].T
    q, key, v, o = (w["L1_attn_W_" + c].T for c in "qkvo")
    swap = at ^ 1
    f["w_qkv"], f["w_o"] = np.stack([q, q[:, swap], key, key[:, swap], v], 1), o
    theta = np.float32(10000.0) ** (-2.0 * np.arange(DK // 2, dtype=np.float32) / np.float32(DK))
    angle = np.minimum(np.arange(L), 255).astype(np.float32)[:, None] * theta[None].astype(np.float32)
    pair = at % DK // 2
    f["rope_cos"] = np.cos(angle)[:, pair].T
    f["rope_sin"] = (np.sin(angle)[:, pair] * np.where(at % 2 == 0, -1, 1)).T
    f["mask"] = np.stack([np.where(at[None] > at[:, None], NEG, 0), np.where(at[None] < at[:, None], NEG, 0)], 1)
    f["sel_w"] = np.tile(w["L1_ffn_expert_sel"].T, (1, 2))
    f["number1"] = rows(np.arange(E1))
    f["keys"], f["values"] = w["L1_ffn_keys"], w["L1_ffn_values"]
    return {name: np.ascontiguousarray(a, dtype=np.float32) for name, a in f.items()}


def kernel(**inputs):
    import concourse.bacc as bacc
    from concourse.bass_utils import run_bass_kernel_spmd

    arrays = lay_out(inputs)
    nc = bacc.Bacc("TRN2", target_bir_lowering=False, num_devices=1)
    d = {name: nc.dram_tensor(name, a.shape, F32, kind="ExternalInput").ap() for name, a in arrays.items()}
    d["out"] = nc.dram_tensor("out", (B, L, D), F32, kind="ExternalOutput").ap()
    program(nc, d)
    r = run_bass_kernel_spmd(nc, [arrays], core_ids=[0])
    return r.results[0]["out"]
```

```python
import numpy as np
from contextlib import ExitStack
import concourse.bass as bass
from concourse import mybir

F32 = mybir.dt.float32
BF16 = mybir.dt.bfloat16
I32 = mybir.dt.int32
U32 = mybir.dt.uint32
ALU = mybir.AluOpType
ACT = mybir.ActivationFunctionType
AX = mybir.AxisListType

P = 128
B, L, D = 8, 512, 128
T = B * L
NT = T // P
TQ = L // P
DI, NS = 256, 32
HALF = NS // 2
E0, C0, F0, G0 = 8, 80, 512, 2
WC = 2 * DI + DI + 2 * NS + E0
E1, K1 = 64, 4
TILES1 = T * K1 // P + E1
GR = TILES1 // 4
SLOTS1 = TILES1 * P
EPS = 1e-5
CH = 16
LN2 = float(np.log(2.0))
TINY = 2.0 ** -60
LOG_TINY = 60.0 * LN2


class Tally:

    def __init__(self, eng, sem, base=0):
        self.eng, self.sem, self.base, self.n = eng, sem, base, 0

    def mark(self, ins):
        self.n += 1
        ins.then_inc(self.sem, 1)
        return self.n

    def settle(self):
        self.eng.wait_ge(self.sem, self.base + self.n)

    def __call__(self, ins):
        self.mark(ins)
        self.settle()


class Scope:
    taken = []

    def __init__(self, nc, ctx, tag):
        self.nc, self.ctx, self.tag = nc, ctx, tag

    def sb(self, name, shape, dt=F32):
        return self.ctx.enter_context(self.nc.sbuf_tensor(f"{self.tag}_{name}", shape, dt))

    def ps(self, name, shape, dt=F32):
        return self.ctx.enter_context(self.nc.psum_tensor(f"{self.tag}_{name}", shape, dt))

    def sems(self, names):
        new = [self.nc.alloc_semaphore(f"{self.tag}_{n}") for n in names.split()]
        Scope.taken.extend(new)
        return new

    @staticmethod
    def clear_all(nc):
        nc.clear_and_free_semaphores(Scope.taken)
        Scope.taken = []
        nc.all_engine_barrier()


def at_least(n, low):
    return not isinstance(n, int) or n >= low


def over(ap, n):
    return ap.unsqueeze(2).to_broadcast([ap.shape[0], ap.shape[1], n])


def phase_norm(nc, d, s, tag, source, scaled):
    with ExitStack() as ctx:
        k = Scope(nc, ctx, tag)
        sq = k.sb("sq", [P, NT, D])
        mean = k.sb("mean", [P, NT])
        var = k.sb("var", [P, NT])
        std = k.sb("std", [P, NT])
        loaded, dv, centred, squared, var_ready, std_ready = k.sems("loaded dv centred squared var_ready std_ready")
        block = ctx.enter_context(nc.Block())

        @block.sync
        def _(sp):
            if source is not None:
                sp.dma_start(s.xc[:, :, :], source.rearrange("b (q p) e -> p (b q) e", p=P)).then_inc(loaded, 16)

        @block.vector
        def _(dve):
            step = Tally(dve, dv)
            step.mark(nc.vector.memset(s.eps[:, :], EPS))
            if source is not None:
                dve.wait_ge(loaded, 16)
            step(nc.vector.tensor_reduce(mean[:, :], s.xc[:, :, :], AX.X, ALU.add))
            step(nc.vector.tensor_scalar(mean[:, :], mean[:, :], 1.0 / D, None, ALU.mult))
            nc.vector.tensor_tensor(s.xc[:, :, :], s.xc[:, :, :], over(mean[:, :], D), ALU.subtract).then_inc(centred, 1)
            dve.wait_ge(squared, 1)
            step(nc.vector.tensor_reduce(var[:, :], sq[:, :, :], AX.X, ALU.add))
            nc.vector.tensor_scalar(var[:, :], var[:, :], 1.0 / D, None, ALU.mult).then_inc(var_ready, 1)
            dve.wait_ge(std_ready, 1)
            step(nc.vector.reciprocal(s.rstd[:, :], std[:, :]))
            if scaled:
                step(nc.vector.tensor_tensor(s.xc[:, :, :], s.xc[:, :, :], over(s.rstd[:, :], D), ALU.mult))

        @block.scalar
        def _(act):
            act.wait_ge(centred, 1)
            nc.scalar.activation(sq[:, :, :], s.xc[:, :, :], ACT.Square).then_inc(squared, 1)
            act.wait_ge(var_ready, 1)
            nc.scalar.activation(std[:, :], var[:, :], ACT.Sqrt, bias=s.eps[:, 0:1]).then_inc(std_ready, 1)


def phase_project(nc, d, s):
    with ExitStack() as ctx:
        k = Scope(nc, ctx, "p")
        wcat = k.sb("wcat", [P, WC])
        bias = k.sb("bias", [P, DI])
        bias2 = k.sb("bias2", [P, DI])
        xs = k.sb("xs", [P, 2, P])
        xT = k.sb("xT", [P, 2, P])
        psT = k.ps("psT", [P, 2, 512])
        ps1 = k.ps("ps1", [P, 2, 512])
        ps2 = k.ps("ps2", [P, 2, 512])
        loaded, dv, xs_ready, turned, xT_ready, projected, read_act, read_dve = k.sems(
            "loaded dv xs_ready turned xT_ready projected read_act read_dve")
        block = ctx.enter_context(nc.Block())

        @block.sync
        def _(sp):
            sp.dma_start(wcat[:, :], d["wcat"]).then_inc(loaded, 16)
            sp.dma_start(bias[:, :], d["b_dt"]).then_inc(loaded, 16)
            sp.dma_start(bias2[:, :], d["dt_bias"]).then_inc(loaded, 16)

        @block.vector
        def _(dve):
            step = Tally(dve, dv)
            dve.wait_ge(loaded, 48)
            step(nc.vector.tensor_tensor(bias[:, :], bias[:, :], bias2[:, :], ALU.add))

            def normalise(n, r):
                nc.vector.tensor_scalar(xs[:, r, :], s.xc[:, bass.ds(n, 1), :].rearrange("p a e -> p (a e)"),
                                        s.rstd[:, bass.ds(n, 1)], None, ALU.mult).then_inc(xs_ready, 1)

            def take(n, r):
                dve.wait_ge(projected, n + 1)
                nc.vector.tensor_tensor(s.pre[:, bass.ds(n, 1), :].rearrange("p a e -> p (a e)"),
                                        ps2[:, r, 0:DI], bias[:, :], ALU.add)
                nc.vector.tensor_copy(s.bcr[:, bass.ds(n, 1), :].rearrange("p a e -> p (a e)"),
                                      ps2[:, r, DI:WC - 2 * DI]).then_inc(read_dve, 1)

            normalise(0, 0)
            normalise(1, 1)
            with dve.Fori(0, NT // 2 - 1) as pair:
                for r in range(2):
                    n = pair * 2
                    take(n + r, r)
                    dve.wait_ge(turned, n + r + 1)
                    normalise(n + r + 2, r)
            for r in range(2):
                take(NT - 2 + r, r)

        @block.tensor
        def _(pe):
            pe.wait_ge(loaded, 48)

            def turn(n, r):
                pe.wait_ge(xs_ready, n + 1)
                nc.tensor.transpose(psT[:, r, 0:P], xs[:, r, :], s.ident[:, :]).then_inc(turned, 1)

            def tile(n, r, first, last=False):
                if not last:
                    turn(n + 1, 1 - r)
                pe.wait_ge(xT_ready, n + 1)
                if not first:
                    pe.wait_ge(read_act, n - 1)
                    pe.wait_ge(read_dve, n - 1)
                nc.tensor.matmul(ps1[:, r, :], xT[:, r, :], wcat[:, 0:512], start=True, stop=True)
                nc.tensor.matmul(ps2[:, r, 0:WC - 512], xT[:, r, :], wcat[:, 512:WC], start=True, stop=True).then_inc(projected, 1)

            turn(0, 0)
            for r in range(2):
                tile(r, r, True)
            with pe.Fori(1, NT // 2 - 1) as pair:
                for r in range(2):
                    tile(pair * 2 + r, r, False)
            for r in range(2):
                tile(NT - 2 + r, r, False, r == 1)

        @block.scalar
        def _(act):
            def take(n, r):
                act.wait_ge(turned, n + 1)
                nc.scalar.activation(xT[:, r, :], psT[:, r, 0:P], ACT.Copy).then_inc(xT_ready, 1)

            take(0, 0)
            def tile(n, r, last=False):
                if not last:
                    take(n + 1, 1 - r)
                act.wait_ge(projected, n + 1)
                one = bass.ds(n, 1)
                nc.scalar.activation(flat(s.xi[:, one, :]), ps1[:, r, 0:DI], ACT.Copy)
                nc.scalar.activation(flat(s.zp[:, one, :]), ps1[:, r, DI:2 * DI], ACT.Copy).then_inc(read_act, 1)

            with act.Fori(0, NT // 2 - 1) as pair:
                for r in range(2):
                    tile(pair * 2 + r, r)
            for r in range(2):
                tile(NT - 2 + r, r, r == 1)

def flat(ap):
    return ap.rearrange("p a e -> p (a e)")

TWO_PI = 2.0 * float(np.pi)
C1 = 6.28125
C2 = float(np.float32(TWO_PI - C1).view(np.uint32) & 0xFFFFF000)
C2 = float(np.array([np.float32(TWO_PI - C1).view(np.uint32) & 0xFFFFF000], np.uint32).view(np.float32)[0])
C3 = float(TWO_PI - C1 - C2)
ROUND = 1.5 * 2.0 ** 23
PI_IN = 3.1415925


def phase_steps(nc, d, s):
    with ExitStack() as ctx:
        k = Scope(nc, ctx, "t")
        W = TQ * DI
        ab, ex, lg, lg2, u1, mm, dt, shift = (k.sb(n, [P, W]) for n in ("ab", "ex", "lg", "lg2", "u1", "mm", "dt", "shift"))
        lnd = k.sb("lnd", [P, 2, W])
        res = k.sb("res", [P, 2, W])
        lparts = k.sb("lparts", [P, 2, 3, W], BF16)
        hparts = k.sb("hparts", [P, 2, 3, W], BF16)
        zero = k.sb("zero", [P, DI], BF16)
        (dv, exp_ready, log_ready, clamped, log2_ready, lnd_ready, hdx_ready, high_ready, rest_ready,
         mid_ready, low_ready, slot_free, stored, zeroed) = k.sems(
            "dv exp_ready log_ready clamped log2_ready lnd_ready hdx_ready high_ready rest_ready "
            "mid_ready low_ready slot_free stored zeroed")
        block = ctx.enter_context(nc.Block())
        per_b = 6

        def rows(ap, b):
            return flat(ap[:, bass.ds(b * TQ, TQ), :])

        @block.sync
        def _(sp):
            sp.wait_ge(zeroed, 1)
            for h in range(2):
                sp.dma_start(d["hdp"][h, :, :, 0, :].rearrange("c f e -> (c f) e"), zero[0:24, :]).then_inc(stored, 16)
            with sp.Fori(0, 2) as h:
                for f in range(4):
                    r = f % 2
                    sp.wait_ge(low_ready, (h * 4 + f) * 2 + 2)
                    for c in range(3):
                        sp.dma_start(d["lnp"][bass.ds(h, 1), c, f].rearrange("h (q p) e -> p (h q) e", p=P),
                                     lparts[:, r, c, :].rearrange("p (q e) -> p q e", e=DI)).then_inc(stored, 16)
                    for c, part in enumerate((0, 1, 2, 0, 1, 0)):
                        sp.dma_start(d["hdp"][bass.ds(h, 1), c, f, 1:, :].rearrange("h (q p) e -> p (h q) e", p=P),
                                     hparts[:, r, part, :].rearrange("p (q e) -> p q e", e=DI)).then_inc(stored, 16)
                    sp.wait_ge(stored, (h * 4 + f) * 144 + 176)
                    sp.sem_inc(slot_free, 1)
            sp.wait_ge(stored, 16 * (2 + 9 * B))

        @block.vector
        def _(dve):
            def sequence(b, r):
                step = Tally(dve, dv, b * per_b)
                pre = rows(s.pre, b)
                dve.wait_ge(lnd_ready, b)
                step.mark(nc.vector.scalar_tensor_tensor(ab[:, :], pre, -1.0, pre, ALU.mult, ALU.max))
                step.mark(nc.vector.tensor_scalar(shift[:, :], pre, LOG_TINY, 0.0, ALU.add, ALU.min))
                dve.wait_ge(exp_ready, b + 1)
                step(nc.vector.tensor_scalar(u1[:, :], ex[:, :], 1.0, -1.0, ALU.add, ALU.add))
                step(nc.vector.tensor_tensor(u1[:, :], ex[:, :], u1[:, :], ALU.subtract))
                dve.wait_ge(log_ready, b + 1)
                step(nc.vector.tensor_tensor(u1[:, :], lg[:, :], u1[:, :], ALU.add))
                step(nc.vector.scalar_tensor_tensor(dt[:, :], pre, 0.0, u1[:, :], ALU.max, ALU.add))
                assert step.n == per_b
                nc.vector.tensor_scalar(mm[:, :], dt[:, :], TINY, None, ALU.max).then_inc(clamped, 1)
                xi = rows(s.xi, b)
                nc.vector.scalar_tensor_tensor(xi, dt[:, :], 0.5, xi, ALU.mult, ALU.mult).then_inc(hdx_ready, 1)
                dve.wait_ge(log2_ready, b + 1)
                dve.wait_ge(low_ready, b * 2)
                nc.vector.tensor_tensor(lnd[:, r, :], lg2[:, :], shift[:, :], ALU.add).then_inc(lnd_ready, 1)

            with dve.Fori(0, B // 2) as pair:
                for r in range(2):
                    sequence(pair * 2 + r, r)

        @block.scalar
        def _(act):
            def sequence(b, r):
                act.wait_ge(dv, b * per_b + 1)
                nc.scalar.activation(ex[:, :], ab[:, :], ACT.Exp, scale=-1.0).then_inc(exp_ready, 1)
                act.wait_ge(exp_ready, b + 1)
                nc.scalar.activation(lg[:, :], ex[:, :], ACT.Ln, bias=1.0).then_inc(log_ready, 1)
                act.wait_ge(clamped, b + 1)
                nc.scalar.activation(lg2[:, :], mm[:, :], ACT.Ln).then_inc(log2_ready, 1)
                act.wait_ge(slot_free, b + 1)
                act.wait_ge(hdx_ready, b + 1)
                nc.scalar.activation(hparts[:, r, 0, :], rows(s.xi, b), ACT.Copy).then_inc(high_ready, 1)
                act.wait_ge(lnd_ready, b + 1)
                nc.scalar.activation(lparts[:, r, 0, :], lnd[:, r, :], ACT.Copy).then_inc(high_ready, 1)
                for i, parts in enumerate((hparts, lparts)):
                    act.wait_ge(rest_ready, b * 2 + i + 1)
                    nc.scalar.activation(parts[:, r, 1, :], res[:, i, :], ACT.Copy).then_inc(mid_ready, 1)

            act.sem_inc(slot_free, 2)
            with act.Fori(0, B // 2) as pair:
                for r in range(2):
                    sequence(pair * 2 + r, r)

        @block.gpsimd
        def _(pool):
            nc.gpsimd.memset(zero[:, :], 0.0).then_inc(zeroed, 1)

            def sequence(b, r):
                whole = (rows(s.xi, b), lnd[:, r, :])
                pool.wait_ge(low_ready, b * 2)
                for i, parts in enumerate((hparts, lparts)):
                    pool.wait_ge(high_ready, b * 2 + i + 1)
                    nc.gpsimd.tensor_tensor(res[:, i, :], whole[i], parts[:, r, 0, :], ALU.subtract).then_inc(rest_ready, 1)
                for i, parts in enumerate((hparts, lparts)):
                    pool.wait_ge(mid_ready, b * 2 + i + 1)
                    nc.gpsimd.tensor_tensor(parts[:, r, 2, :], res[:, i, :], parts[:, r, 1, :], ALU.subtract).then_inc(low_ready, 1)

            with pool.Fori(0, B // 2) as pair:
                for r in range(2):
                    sequence(pair * 2 + r, r)


def split3(nc, dve, step, x, parts, rest):
    step(nc.vector.tensor_copy(parts[0], x))
    step(nc.vector.tensor_tensor(rest, x, parts[0], ALU.subtract))
    step(nc.vector.tensor_copy(parts[1], rest))
    step(nc.vector.tensor_tensor(parts[2], rest, parts[1], ALU.subtract))


def phase_rotation(nc, d, s):
    with ExitStack() as ctx:
        k = Scope(nc, ctx, "r")
        freq = k.sb("freq", [P, HALF])
        freq_col = k.sb("freq_col", [P, 1])
        sign_col = k.sb("sign_col", [P, 1])
        steps = k.sb("steps", [P, TQ])
        steps_row = k.sb("steps_row", [P, L])
        angle = k.sb("angle", [P, TQ, HALF])
        cos_t, sin_t = (k.sb(n, [P, TQ, HALF]) for n in ("cos_t", "sin_t"))
        angle_c = k.sb("angle_c", [P, L])
        turns = k.sb("turns", [P, 2, L])
        left = k.sb("left", [P, 2, L])
        turned_b, turned_c = (k.sb(n, [P, TQ, B, NS]) for n in ("turned_b", "turned_c"))
        prod = k.sb("prod", [P, TQ, B, HALF])
        plain_b = k.sb("plain_b", [P, TQ, B, NS])
        cb = k.sb("cb", [P, TQ, B, NS])
        rest = k.sb("rest", [P, TQ, B, NS])
        parts = k.sb("parts", [P, 3, TQ, B, NS], BF16)
        stack = k.sb("stack", [P, 2, TQ, B, 6, NS], BF16)
        zero = k.sb("zero", [P, 6 * NS], BF16)
        alog = k.sb("alog", [3 * NS, DI])
        alog_rest = k.sb("alog_rest", [3 * NS, DI])
        alog_parts = k.sb("alog_parts", [3 * NS, 3, DI], BF16)
        psT = k.ps("psT", [P, 2, L])
        loaded, dv, angles_ready, sines_ready, turned_ready, columns_ready, stacked, stored = k.sems(
            "loaded dv angles_ready sines_ready turned_ready columns_ready stacked stored")
        block = ctx.enter_context(nc.Block())

        @block.sync
        def _(sp):
            for dst, name in ((freq[:, :], "freq"), (freq_col[:, :], "freq_col"), (sign_col[:, :], "sign_col"),
                              (steps[:, :], "steps"), (steps_row[:, :], "steps_row"), (alog[:, :], "alog")):
                sp.dma_start(dst, d[name]).then_inc(loaded, 16)
            for term in range(2):
                sp.wait_ge(stacked, term + 1)
                for b in range(B):
                    dst = d["st0"][b, 1:] if term == 0 else d["st1"][b]
                    sp.dma_start(dst.rearrange("(q p) e -> p q e", p=P),
                                 stack[:, term, :, b, :, :].rearrange("p q c n -> p q (c n)")).then_inc(stored, 16)
            sp.dma_start(d["st0"][:, 0, :], zero[0:B, :]).then_inc(stored, 16)
            sp.wait_ge(stored, 16 * (2 * B + 1))

        @block.vector
        def _(dve):
            step = Tally(dve, dv)
            step.mark(nc.vector.memset(zero[:, :], 0.0))
            dve.wait_ge(loaded, 96)
            step(nc.vector.tensor_tensor(angle[:, :, :], over(steps[:, :], HALF),
                                         freq[:, :].unsqueeze(1).to_broadcast([P, TQ, HALF]), ALU.mult))
            step(nc.vector.tensor_scalar(angle_c[:, :], steps_row[:, :], freq_col[:, 0:1], None, ALU.mult))

            def reduce(ang, out, turn, quarter):
                step(nc.vector.tensor_scalar(turn, ang, 1.0 / TWO_PI, 0.25 * quarter, ALU.mult, ALU.add))
                step(nc.vector.tensor_scalar(turn, turn, ROUND, -ROUND, ALU.add, ALU.add))
                step(nc.vector.scalar_tensor_tensor(out, turn, -C1, ang, ALU.mult, ALU.add))
                step(nc.vector.scalar_tensor_tensor(out, turn, -C2, out, ALU.mult, ALU.add))
                step(nc.vector.scalar_tensor_tensor(out, turn, -C3, out, ALU.mult, ALU.add))
                step(nc.vector.tensor_scalar(out, out, quarter * TWO_PI / 4, PI_IN, ALU.add, ALU.min))
                step(nc.vector.tensor_scalar(out, out, -PI_IN, None, ALU.max))

            small = flat(angle[:, :, :])
            w = TQ * HALF
            reduce(small, flat(cos_t[:, :, :]), turns[:, 0, 0:w], 1)
            reduce(small, flat(sin_t[:, :, :]), turns[:, 0, 0:w], 0)
            reduce(angle_c[:, :], left[:, 0, :], turns[:, 0, :], 1)
            reduce(angle_c[:, :], left[:, 1, :], turns[:, 1, :], 0)
            step(nc.vector.engine_nop())
            nc.vector.engine_nop().then_inc(angles_ready, 1)

            pieces = [alog_parts[:, c, :] for c in range(3)]
            split3(nc, dve, step, alog[:, :], pieces, alog_rest[:, :])
            for c in range(3):
                lo, hi = c * NS, (c + 1) * NS
                src = alog_parts[lo:hi, c, :].unsqueeze(1).to_broadcast([NS, 2 * CH * 2, DI])
                step.mark(nc.vector.tensor_copy(s.marg[lo:hi, :, :, :, :].rearrange("r a u h e -> r (a u h) e"), src))

            dve.wait_ge(sines_ready, 4)
            step.mark(nc.vector.tensor_scalar(s.sin_c[:, :], s.sin_c[:, :], sign_col[:, 0:1], None, ALU.mult))
            view = s.bcr[:, :, :].rearrange("p (b q) n -> p q b n", q=TQ)
            full = [P, TQ, B, HALF]

            def turn(src, dst, back):
                re, im = src[:, :, :, 0:HALF], src[:, :, :, HALF:NS]
                cos = cos_t[:, :, :].unsqueeze(2).to_broadcast(full)
                sin = sin_t[:, :, :].unsqueeze(2).to_broadcast(full)
                for a, b, lo, op in ((re, im, 0, ALU.add if back else ALU.subtract),
                                     (im, re, HALF, ALU.subtract if back else ALU.add)):
                    out = dst[:, :, :, lo:lo + HALF]
                    for q in range(TQ):
                        step.mark(nc.vector.tensor_tensor(out[:, q], a[:, q], cos[:, q], ALU.mult))
                        step(nc.vector.tensor_tensor(prod[:, q], b[:, q], sin[:, q], ALU.mult))
                    step(nc.vector.tensor_tensor(out, out, prod[:, :, :, :], op))

            turn(view[:, :, :, 0:NS], turned_b, False)
            turn(view[:, :, :, NS:2 * NS], turned_c, True)
            nc.vector.engine_nop().then_inc(turned_ready, 1)
            step(nc.vector.tensor_copy(plain_b[:, :, :, :], view[:, :, :, 0:NS]))
            step(nc.vector.tensor_tensor(cb[:, :, :, :], turned_c[:, :, :, :], plain_b[:, :, :, :], ALU.mult))
            step(nc.vector.tensor_reduce(s.kappa[:, :, :], cb[:, :, :, :], AX.X, ALU.add))
            for term, src in enumerate((turned_b, plain_b)):
                m = "p q b n -> p (q b) n"
                p3 = [parts[:, c, :, :, :].rearrange(m) for c in range(3)]
                split3(nc, dve, step, src[:, :, :, :].rearrange(m), p3, rest[:, :, :, :].rearrange(m))
                st = stack[:, term, :, :, :, :].rearrange("p q b c n -> p (q b) c n")
                for lo, hi, c in ((0, 3, 0), (3, 5, 1), (5, 6, 2)):
                    step(nc.vector.tensor_copy(st[:, :, lo:hi, :],
                                               p3[c].unsqueeze(2).to_broadcast([P, TQ * B, hi - lo, NS])))
                nc.vector.engine_nop().then_inc(stacked, 1)
            dve.wait_ge(columns_ready, 2)
            for h in range(2):
                step.mark(nc.vector.tensor_copy(s.c_col[:, h, :], psT[:, h, :]))

        @block.scalar
        def _(act):
            act.wait_ge(angles_ready, 1)
            nc.scalar.activation(cos_t[:, :, :], cos_t[:, :, :], ACT.Sin).then_inc(sines_ready, 1)
            nc.scalar.activation(sin_t[:, :, :], sin_t[:, :, :], ACT.Sin).then_inc(sines_ready, 1)
            nc.scalar.activation(s.cos_c[:, :], left[:, 0, :], ACT.Sin).then_inc(sines_ready, 1)
            nc.scalar.activation(s.sin_c[:, :], left[:, 1, :], ACT.Sin).then_inc(sines_ready, 1)

        @block.tensor
        def _(pe):
            pe.wait_ge(turned_ready, 1)
            for h in range(2):
                for q in range(TQ):
                    last = nc.tensor.transpose(psT[:, h, q * P:(q + 1) * P],
                                               turned_c[:, q, 4 * h:4 * h + 4, :].rearrange("p f n -> p (f n)"), s.ident[:, :])
                last.then_inc(columns_ready, 1)

BODY = 2 * CH
NB = L // BODY
FILL = SLOTS1 // P // NB
AHEAD = 2


def phase_scan(nc, d, s):
    with ExitStack() as ctx:
        k = Scope(nc, ctx, "c")
        sel = k.sb("sel", [108, P], BF16)
        sel_f = k.sb("sel_f", [108, P])
        eye_j = k.sb("eye_j", [P, 2, P])
        mask4 = k.sb("mask4", [P, 4])
        zeros = k.sb("zeros", [P, FILL, D])
        half_ln2 = k.sb("half_ln2", [P, 1])
        mv = k.sb("mv", [96, 2, CH, 2, DI], BF16)
        st = k.sb("st", [96, 2, CH, P], BF16)
        rot = k.sb("rot", [P, 2, 8, P])
        tmp = k.sb("tmp", [P, 8, P])
        cy = k.sb("cy", [P, 2, 8, 2, 32])
        a = k.sb("a", [P, 4, 512])
        aq = k.sb("aq", [P, 4, 512])
        yb = k.sb("yb", [P, 2, CH, P])
        args = k.ps("args", [P, 2, 512])
        q = k.ps("q", [P, 2, 2, 512])
        ys = k.ps("ys", [P, 2, 4, P])
        (loaded, cleared, picked, dv, arg_loaded0, arg_loaded1, mv_loaded0, mv_loaded1, arg_ready, mv_used, decay_ready, q_ready, aq_ready, rot_ready,
         y_ready, y_banks, y_stored0, y_stored1, pl, filled) = k.sems(
            "loaded cleared picked dv arg_loaded0 arg_loaded1 mv_loaded0 mv_loaded1 arg_ready mv_used decay_ready q_ready aq_ready rot_ready "
            "y_ready y_banks y_stored0 y_stored1 pl filled")
        arg_loaded, mv_loaded = (arg_loaded0, arg_loaded1), (mv_loaded0, mv_loaded1)
        y_stored = (y_stored0, y_stored1)
        block = ctx.enter_context(nc.Block())
        y_out = d["y"].rearrange("(h f) l (g e) -> h g f l e", h=2, g=2)
        n_arg, n_mv = 2, 4 + 16

        @block.sync
        def _(sp):
            sp.dma_start(sel_f[:, :], d["sel"]).then_inc(loaded, 16)
            sp.dma_start(eye_j[:, :, :], d["eye_j"]).then_inc(loaded, 16)
            sp.dma_start(mask4[:, :], d["mask4"]).then_inc(loaded, 16)
            sp.wait_ge(cleared, 3)

            def load(c, slot):
                u0 = c * CH
                for h in range(2):
                    sp.dma_start(s.marg[96:108, slot, :, h, :],
                                 d["lnp"][h, :, :, bass.ds(u0, CH), :].rearrange("c f u e -> (c f) u e")).then_inc(arg_loaded[slot], 16)
                for h in range(2):
                    for term in range(2):
                        lo = h * 48 + term * 24
                        sp.dma_start(mv[lo:lo + 24, slot, :, h, :],
                                     d["hdp"][h, :, :, bass.ds(u0 + term, CH), :].rearrange("c f u e -> (c f) u e")).then_inc(mv_loaded[slot], 16)
                        src = d["st0"] if term == 0 else d["st1"]
                        for f in range(4):
                            sp.dma_start(st[lo + f:lo + 24:4, slot, :, f * NS:(f + 1) * NS],
                                         src[h * 4 + f, bass.ds(u0, CH), :].rearrange("u (c n) -> c u n", n=NS)).then_inc(mv_loaded[slot], 16)

            def store(c, slot):
                sp.wait_ge(y_banks, (c + 1) * (CH // 4) + 2)
                for j in range(4):
                    h, g = divmod(j, 2)
                    sp.dma_start(y_out[h, g, :, bass.ds(c * CH, CH), :], yb[32 * j:32 * j + 4, slot, :, :]).then_inc(y_stored[slot], 16)

            for slot in range(2):
                load(slot, slot)
            wiped = d["rows1"].rearrange("(n p j) e -> n p j e", p=P, j=FILL)
            sp.dma_start(wiped[0], zeros[:, :, :]).then_inc(filled, 16)
            with sp.Fori(0, NB - 1) as i:
                sp.dma_start(wiped[bass.ds(i + 1, 1)].rearrange("a p j e -> (a p) j e"), zeros[:, :, :]).then_inc(filled, 16)
                for slot in range(2):
                    c = i * 2 + slot
                    sp.wait_ge(arg_ready, (c + 1) * CH)
                    sp.wait_ge(mv_used, c + 1)
                    load(c + 2, slot)
                    store(c, slot)
            for slot in range(2):
                store(2 * NB - 2 + slot, slot)
                sp.wait_ge(y_stored[slot], (NB + 1) * 64)
            sp.wait_ge(filled, NB * 16)

        @block.tensor
        def _(pe):
            pe.wait_ge(picked, 1)

            def argument(i, j):
                slot, u = j // CH % 2, j % CH
                if u == 0:
                    pe.wait_ge(arg_loaded[slot], (i + j // BODY + 1) * 16 * n_arg)
                nc.tensor.matmul(args[:, j % 2, :], sel[:, :], flat(s.marg[:, slot, u]), start=True, stop=True).then_inc(arg_ready, 1)

            def inputs(i, j, only=False):
                slot, u = j // CH % 2, j % CH
                if u == 0:
                    pe.wait_ge(mv_loaded[slot], (i + j // BODY + 1) * 16 * n_mv)
                for h in range(2):
                    ins = nc.tensor.matmul(q[:, j % 2, h, 0:DI], st[:, slot, u, :], mv[:, slot, u, h, :], start=True, stop=only)
                if u == CH - 1:
                    ins.then_inc(mv_used, 1)
                return ins

            def body(i, last):
                for j in range(BODY):
                    end = last and j == BODY - 1
                    if j % 8 == 0:
                        pe.wait_ge(rot_ready, i * (BODY // 8) + j // 8 + 1)
                    slot, v = j // 8 % 2, j % 8
                    for h in range(2):
                        cols = slice(h * DI, (h + 1) * DI)
                        pe.wait_ge(aq_ready, i * (2 * BODY) + 2 * j + h + 1)
                        if not end:
                            nc.tensor.matmul(q[:, (j + 1) % 2, h, 0:DI], rot[:, slot, v, :], aq[:, j % 4, cols],
                                             start=False, stop=True).then_inc(q_ready, 1)
                    if j % 4 == 0:
                        pe.wait_ge(y_banks, i * (BODY // 4) + j // 4 + 1)
                    for g in range(4):
                        ins = nc.tensor.matmul(ys[32 * g:32 * g + 32, j // 4 % 2, j % 4, :], cy[:, slot, v, g // 2, :],
                                               aq[:, j % 4, g * P:(g + 1) * P], start=True, stop=True)
                    if j % 4 == 3:
                        ins.then_inc(y_ready, 1)
                    if not (last and j >= BODY - AHEAD):
                        argument(i, j + AHEAD)
                    if not (last and j >= BODY - 2):
                        ins = inputs(i, j + 2)

            for j in range(AHEAD):
                argument(0, j)
            inputs(0, 0, only=True).then_inc(q_ready, 2)
            inputs(0, 1)
            with pe.Fori(0, NB - 1) as i:
                body(i, False)
            body(NB - 1, True)

        @block.vector
        def _(dve):
            step = Tally(dve, dv)
            step.mark(nc.vector.memset(half_ln2[:, :], LN2 / 2))
            nc.vector.memset(zeros[:, :, :], 0.0).then_inc(cleared, 1)
            nc.vector.memset(mv[:, :, :, :, :], 0.0).then_inc(cleared, 1)
            nc.vector.memset(st[:, :, :, :], 0.0).then_inc(cleared, 1)
            dve.wait_ge(loaded, 48)
            nc.vector.tensor_copy(sel[:, :], sel_f[:, :]).then_inc(picked, 1)
            with dve.Fori(0, NB) as i:
                for j in range(BODY):
                    dve.wait_ge(decay_ready, i * BODY + j + 1)
                    for h in range(2):
                        cols = slice(h * DI, (h + 1) * DI)
                        dve.wait_ge(q_ready, i * (2 * BODY) + 2 * j + h + 1)
                        nc.vector.tensor_tensor(aq[:, j % 4, cols], q[:, j % 2, h, 0:DI], a[:, j % 4, cols],
                                                ALU.mult).then_inc(aq_ready, 1)

        @block.scalar
        def _(act):
            act.sem_inc(y_banks, 2)
            act.sem_inc(y_stored0, 64)
            act.sem_inc(y_stored1, 64)
            act.wait_ge(picked, 1)

            def decay(i, m):
                act.wait_ge(arg_ready, i * BODY + m + 1)
                nc.scalar.activation(a[:, m % 4, :], args[:, m % 2, :], ACT.Tanh, bias=half_ln2[:, 0:1],
                                     scale=-0.5).then_inc(decay_ready, 1)

            def copy_out(i, n):
                slot = n * 4 // CH
                if n * 4 % CH == 0:
                    act.wait_ge(y_stored[slot], (i + 1) * 64)
                act.wait_ge(y_ready, i * (BODY // 4) + n + 1)
                u = n * 4 % CH
                nc.scalar.activation(yb[:, slot, u:u + 4, :], ys[:, n % 2, :, :], ACT.Copy).then_inc(y_banks, 1)

            def body(i, last):
                for m in range(BODY):
                    if not (last and m >= BODY - AHEAD):
                        decay(i, m + AHEAD)
                    if m % 4 == 3:
                        copy_out(i, m // 4)

            decay(0, 0)
            decay(0, 1)
            with act.Fori(0, NB - 1) as i:
                body(i, False)
            body(NB - 1, True)

        @block.gpsimd
        def _(pool):
            own = Tally(pool, pl)
            own(nc.gpsimd.memset(cy[:, :, :, :, :], 0.0))
            pool.wait_ge(loaded, 48)

            def build(g, slot, base):
                own = Tally(pool, pl, base)
                t = bass.ds(g * 8, 8)
                wide = [P, 8, P]
                own.mark(nc.gpsimd.tensor_tensor(rot[:, slot, :, :], eye_j[:, 0, :].unsqueeze(1).to_broadcast(wide),
                                                 over(s.cos_c[:, t], P), ALU.mult))
                own(nc.gpsimd.tensor_tensor(tmp[:, :, :], eye_j[:, 1, :].unsqueeze(1).to_broadcast(wide),
                                            over(s.sin_c[:, t], P), ALU.mult))
                own(nc.gpsimd.tensor_tensor(rot[:, slot, :, :], rot[:, slot, :, :], tmp[:, :, :], ALU.add))
                for h in range(2):
                    ins = nc.gpsimd.tensor_tensor(cy[:, slot, :, h, 0:4], mask4[:, :].unsqueeze(1).to_broadcast([P, 8, 4]),
                                                  over(s.c_col[:, h, t], 4), ALU.mult)
                ins.then_inc(rot_ready, 1)

            build(0, 0, 1)
            build(1, 1, 4)
            with pool.Fori(0, L // 16 - 1) as i:
                for slot in range(2):
                    g = i * 2 + slot
                    pool.wait_ge(y_ready, g * 2 + 2)
                    build(g + 2, slot, g * 3 + 7)

SLOTS = G0 * E0 * C0
SKIP = 8192.0


def phase_route0(nc, d, s):
    with ExitStack() as ctx:
        k = Scope(nc, ctx, "g")
        W = NT * E0
        logits = s.bcr[:, :, 2 * NS:2 * NS + E0]
        prob, hit, cand, number = (k.sb(n, [P, NT, E0]) for n in ("prob", "hit", "cand", "number"))
        best, first = k.sb("best", [P, 2, NT]), k.sb("first", [P, NT])
        total, inv = k.sb("total", [P, NT]), k.sb("inv", [P, NT])
        pick = k.sb("pick", [P, NT, 2, E0])
        pick_b = k.sb("pick_b", [P, NT, 2, E0], BF16)
        tri_f, tri = k.sb("tri_f", [P, P]), k.sb("tri", [P, P], BF16)
        ones = k.sb("ones", [P, P], BF16)
        count = k.sb("count", [P, NT, 2, E0])
        pos = k.sb("pos", [P, NT, 2, E0])
        offset = k.sb("offset", [P, NT, 2, E0])
        rank, slot, kept, lost = (k.sb(n, [P, NT, 2]) for n in ("rank", "slot", "kept", "lost"))
        psC = k.ps("psC", [P, NT, 2, E0])
        psS = k.ps("psS", [P, NT, 2, E0])
        loaded, dv, shifted, raised, picked, counted = k.sems("loaded dv shifted raised picked counted")
        block = ctx.enter_context(nc.Block())

        @block.sync
        def _(sp):
            sp.dma_start(tri_f[:, :], d["tri"]).then_inc(loaded, 16)
            sp.dma_start(number[:, :, :], d["number"]).then_inc(loaded, 16)
            sp.dma_start(offset[:, :, :, :], d["offset"]).then_inc(loaded, 16)

        @block.vector
        def _(dve):
            v = nc.vector
            step = Tally(dve, dv)
            step.mark(v.memset(ones[:, :], 1.0))
            dve.wait_ge(loaded, 48)
            step.mark(v.tensor_copy(tri[:, :], tri_f[:, :]))
            step(v.tensor_reduce(first[:, :], logits, AX.X, ALU.max))
            v.tensor_tensor(prob[:, :, :], logits, over(first[:, :], E0), ALU.subtract).then_inc(shifted, 1)
            dve.wait_ge(raised, 1)
            step(v.tensor_reduce(total[:, :], prob[:, :, :], AX.X, ALU.add))
            step(v.reciprocal(inv[:, :], total[:, :]))
            step(v.tensor_tensor(prob[:, :, :], prob[:, :, :], over(inv[:, :], E0), ALU.mult))
            for c in range(2):
                one = pick[:, :, c, :]
                step(v.tensor_reduce(best[:, c, :], prob[:, :, :], AX.X, ALU.max))
                step(v.tensor_tensor(hit[:, :, :], prob[:, :, :], over(best[:, c, :], E0), ALU.is_lt))
                step(v.scalar_tensor_tensor(cand[:, :, :], hit[:, :, :], float(E0), number[:, :, :], ALU.mult, ALU.add))
                step(v.tensor_reduce(first[:, :], cand[:, :, :], AX.X, ALU.min))
                step(v.tensor_tensor(one, number[:, :, :], over(first[:, :], E0), ALU.is_equal))
                if c == 0:
                    step(v.scalar_tensor_tensor(prob[:, :, :], one, -2.0, prob[:, :, :], ALU.mult, ALU.add))
            v.tensor_copy(pick_b[:, :, :, :], pick[:, :, :, :]).then_inc(picked, 1)
            dve.wait_ge(counted, 1)
            per_group = NT // G0
            tiles = [ap[:, :, :, :].rearrange("p (g t) c e -> p t g (c e)", g=G0) for ap in (count, psS)]
            step(v.memset(tiles[0][:, 0], 0.0))
            for t in range(1, per_group):
                step(v.tensor_tensor(tiles[0][:, t], tiles[0][:, t - 1], tiles[1][:, t - 1], ALU.add))
            step(v.tensor_tensor(pos[:, :, :, :], count[:, :, :, :], psC[:, :, :, :], ALU.add))
            for g in range(G0):
                last = (g + 1) * per_group - 1
                step(v.tensor_tensor(hit[:, 0, :], count[:, last, 0, :], psS[:, last, 0, :], ALU.add))
                sec = pos[:, g * per_group:(g + 1) * per_group, 1, :]
                step(v.tensor_tensor(sec, sec, hit[:, 0, :].unsqueeze(1).to_broadcast([P, per_group, E0]), ALU.add))
            step(v.tensor_scalar(pos[:, :, :, :], pos[:, :, :, :], -1.0, None, ALU.add))
            step(v.tensor_tensor(count[:, :, :, :], pos[:, :, :, :], pick[:, :, :, :], ALU.mult))
            step(v.tensor_reduce(rank[:, :, :], count[:, :, :, :], AX.X, ALU.add))
            step(v.tensor_tensor(pos[:, :, :, :], pos[:, :, :, :], offset[:, :, :, :], ALU.add))
            step(v.tensor_tensor(count[:, :, :, :], pos[:, :, :, :], pick[:, :, :, :], ALU.mult))
            step(v.tensor_reduce(slot[:, :, :], count[:, :, :, :], AX.X, ALU.add))
            step(v.tensor_scalar(kept[:, :, :], rank[:, :, :], float(C0), None, ALU.is_lt))
            step(v.tensor_scalar(lost[:, :, :], kept[:, :, :], -SKIP, SKIP, ALU.mult, ALU.add))
            step(v.tensor_tensor(lost[:, :, :], lost[:, :, :], slot[:, :, :], ALU.add))
            step(v.tensor_copy(s.place[:, :, :], lost[:, :, :]))
            step(v.tensor_tensor(slot[:, :, :], slot[:, :, :], kept[:, :, :], ALU.mult))
            step(v.tensor_copy(s.fetch[:, :, :], slot[:, :, :]))
            step(v.tensor_tensor(s.gate[:, :, :], kept[:, :, :], best[:, :, :].rearrange("p c t -> p t c"), ALU.mult))

        @block.scalar
        def _(act):
            act.wait_ge(shifted, 1)
            nc.scalar.activation(prob[:, :, :], prob[:, :, :], ACT.Exp).then_inc(raised, 1)
            nc.scalar.activation(s.zp[:, :, :], s.zp[:, :, :], ACT.Silu).then_inc(raised, 1)

        @block.tensor
        def _(pe):
            pe.wait_ge(picked, 1)
            rhs = pick_b[:, :, :, :].rearrange("p t c e -> p (t c e)")
            nc.tensor.matmul(psC[:, :, :, :].rearrange("p t c e -> p (t c e)"), tri[:, :], rhs, start=True, stop=True)
            nc.tensor.matmul(psS[:, :, :, :].rearrange("p t c e -> p (t c e)"), ones[:, :], rhs, start=True, stop=True).then_inc(counted, 1)


def phase_scatter(nc, d, s, tag, rows, choices, n_rows, fill):
    with ExitStack() as ctx:
        k = Scope(nc, ctx, tag)
        zeros = k.sb("zeros", [P, fill // P, D])
        xs = k.sb("xs", [P, 2, D])
        idx = k.sb("idx", [P, 2, choices, 1], U32)
        cleared, filled, xs_ready, passed, sent0, sent1 = k.sems("cleared filled xs_ready passed sent0 sent1")
        sent = (sent0, sent1)
        block = ctx.enter_context(nc.Block())

        @block.sync
        def _(sp):
            sp.wait_ge(cleared, 1)
            n = n_rows // fill
            view = rows.rearrange("(n p j) e -> n p j e", p=P, j=fill // P)
            for i in range(n):
                sp.dma_start(view[i], zeros[:, :, :]).then_inc(filled, 16)
            sp.wait_ge(filled, 16 * n)

        @block.vector
        def _(dve):
            nc.vector.memset(zeros[:, :, :], 0.0).then_inc(cleared, 1)

            def tile(t, r, wait):
                if wait is not None:
                    dve.wait_ge(sent[r], wait)
                nc.vector.tensor_copy(idx[:, r, :, :].rearrange("p c a -> p (c a)"), flat(s.place[:, bass.ds(t, 1), :]))
                nc.vector.tensor_scalar(xs[:, r, :], flat(s.xc[:, bass.ds(t, 1), :]), s.rstd[:, bass.ds(t, 1)], None,
                                        ALU.mult).then_inc(xs_ready, 1)

            for r in range(2):
                tile(r, r, None)
            with dve.Fori(1, NT // 2) as i:
                for r in range(2):
                    tile(i * 2 + r, r, i * (16 * choices))

        @block.gpsimd
        def _(pool):
            pool.wait_ge(filled, 16 * (n_rows // fill))
            with pool.Fori(0, NT // 2) as i:
                for r in range(2):
                    pool.wait_ge(xs_ready, i * 2 + r + 1)
                    pool.sem_inc(passed, 1)
                    for c in range(choices):
                        nc.gpsimd.indirect_dma_start(
                            out=rows, out_offset=bass.IndirectOffsetOnAxis(ap=idx[:, r, c, :], axis=0),
                            in_=xs[:, r, :], in_offset=None, bounds_check=n_rows - 1, oob_is_err=False).then_inc(sent[r], 16)
            for r in range(2):
                pool.wait_ge(sent[r], NT // 2 * 16 * choices)


def phase_experts0(nc, d, s):
    with ExitStack() as ctx:
        k = Scope(nc, ctx, "e")
        FC = F0 // P
        R = G0 * C0
        x = k.sb("x", [C0, 2, G0, D])
        wi = k.sb("wi", [P, 2, F0])
        wo = k.sb("wo", [P, 2, FC, D])
        xT = k.sb("xT", [P, 2, R])
        hT = k.sb("hT", [P, 2, FC, R])
        o = k.sb("o", [C0, 2, G0, D])
        psX = k.ps("psX", [P, 2, 512])
        psH = k.ps("psH", [P, 4, 512])
        psO = k.ps("psO", [P, 2, 512])
        ld0, ld1, turned, xT_ready, hid, h_ready, outed, o_ready, st0, st1 = k.sems("ld0 ld1 turned xT_ready hid h_ready outed o_ready st0 st1")
        ld, st = (ld0, ld1), (st0, st1)
        block = ctx.enter_context(nc.Block())
        rows_in = d["xin"].rearrange("(g e c) h -> e c g h", g=G0, e=E0)
        rows_out = d["eout"].rearrange("(g e c) h -> e c g h", g=G0, e=E0)
        wo_v = d["wo"].rearrange("e (f p) h -> e p f h", p=P)

        @block.sync
        def _(sp):
            def load(e, r):
                one = bass.ds(e, 1)
                sp.dma_start(x[:, r, :, :], rows_in[one].rearrange("a c g h -> c (a g) h")).then_inc(ld[r], 16)
                sp.dma_start(wi[:, r, :], d["wi"][one].rearrange("a h f -> h (a f)")).then_inc(ld[r], 16)
                sp.dma_start(wo[:, r, :, :], wo_v[one].rearrange("a p f h -> p (a f) h")).then_inc(ld[r], 16)

            def store(e, r):
                sp.wait_ge(o_ready, e * G0 + G0)
                sp.dma_start(rows_out[bass.ds(e, 1)].rearrange("a c g h -> c (a g) h"), o[:, r, :, :]).then_inc(st[r], 16)

            for r in range(2):
                load(r, r)
            with sp.Fori(0, E0 // 2 - 1) as i:
                for r in range(2):
                    store(i * 2 + r, r)
                    load(i * 2 + r + 2, r)
            for r in range(2):
                store(E0 - 2 + r, r)
                sp.wait_ge(st[r], E0 // 2 * 16)

        @block.tensor
        def _(pe):
            with pe.Fori(0, E0 // 2) as i:
                for r in range(2):
                    e = i * 2 + r
                    pe.wait_ge(ld[r], (i + 1) * 48)
                    for g in range(G0):
                        ins = nc.tensor.transpose(psX[:, r, g * C0:(g + 1) * C0], x[:, r, g, :], s.ident[0:C0, 0:C0])
                    ins.then_inc(turned, 1)
                    pe.wait_ge(xT_ready, e + 1)
                    for f in range(FC):
                        pe.wait_ge(h_ready, e * FC)
                        nc.tensor.matmul(psH[:, f, 0:R], wi[:, r, f * P:(f + 1) * P], xT[:, r, :], start=True, stop=True).then_inc(hid, 1)
                    pe.wait_ge(h_ready, e * FC + FC)
                    pe.wait_ge(o_ready, e * G0)
                    for g in range(G0):
                        for f in range(FC):
                            ins = nc.tensor.matmul(psO[0:C0, g, 0:D], hT[:, r, f, g * C0:(g + 1) * C0], wo[:, r, f, :],
                                                   start=f == 0, stop=f == FC - 1)
                        ins.then_inc(outed, 1)

        @block.scalar
        def _(act):
            with act.Fori(0, E0 // 2) as i:
                for r in range(2):
                    for f in range(FC):
                        act.wait_ge(hid, (i * 2 + r) * FC + f + 1)
                        nc.scalar.activation(hT[:, r, f, :], psH[:, f, 0:R], ACT.Relu).then_inc(h_ready, 1)

        @block.vector
        def _(dve):
            with dve.Fori(0, E0 // 2) as i:
                for r in range(2):
                    e = i * 2 + r
                    dve.wait_ge(turned, e + 1)
                    nc.vector.tensor_copy(xT[:, r, :], psX[:, r, 0:R]).then_inc(xT_ready, 1)
                    dve.wait_ge(st[r], i * 16)
                    for g in range(G0):
                        dve.wait_ge(outed, e * G0 + g + 1)
                        nc.vector.tensor_copy(o[:, r, g, :], psO[0:C0, g, 0:D]).then_inc(o_ready, 1)


def phase_gather(nc, d, s, tag, rows, choices, weight, out):
    with ExitStack() as ctx:
        k = Scope(nc, ctx, tag)
        got = k.sb("got", [P, 4, choices, D])
        idx = k.sb("idx", [P, 4, choices, 1], U32)
        acc = k.sb("acc", [P, 4, D])
        idx_ready, passed, dv, summed, gated = k.sems("idx_ready passed dv summed gated")
        arrived = k.sems("got0 got1 got2 got3")
        block = ctx.enter_context(nc.Block())
        QT = NT // 4

        @block.vector
        def _(dve):
            def index(i, r):
                nc.vector.tensor_copy(idx[:, r, :, :].rearrange("p c a -> p (c a)"), flat(s.fetch[:, bass.ds(i * 4 + r, 1), :])).then_inc(idx_ready, 1)

            def combine(i, r):
                t = i * 4 + r
                step = Tally(dve, dv, t * (choices - 1))
                dve.wait_ge(arrived[r], (i + 1) * (16 * choices))
                if at_least(t, 4):
                    dve.wait_ge(gated, t - 3)
                w = flat(weight[:, bass.ds(t, 1), :])
                step(nc.vector.tensor_scalar(acc[:, r, :], got[:, r, 0, :], w[:, 0:1], None, ALU.mult))
                for c in range(1, choices):
                    ins = nc.vector.scalar_tensor_tensor(acc[:, r, :], got[:, r, c, :], w[:, c:c + 1], acc[:, r, :], ALU.mult, ALU.add)
                    if c < choices - 1:
                        step(ins)
                ins.then_inc(summed, 1)

            for r in range(4):
                index(0, r)
            for r in range(4):
                combine(0, r)
                index(1, r)
            with dve.Fori(1, QT - 1) as i:
                for r in range(4):
                    combine(i, r)
                    index(i + 1, r)
            for r in range(4):
                combine(QT - 1, r)

        @block.gpsimd
        def _(pool):
            def fetch(i, r):
                t = i * 4 + r
                pool.wait_ge(idx_ready, t + 1)
                if at_least(t, 4):
                    pool.wait_ge(summed, t - 3)
                    pool.sem_inc(passed, 1)
                for c in range(choices):
                    nc.gpsimd.indirect_dma_start(
                        out=got[:, r, c, :], out_offset=None, in_=rows,
                        in_offset=bass.IndirectOffsetOnAxis(ap=idx[:, r, c, :], axis=0)).then_inc(arrived[r], 16)

            for r in range(4):
                fetch(0, r)
            with pool.Fori(1, QT) as i:
                for r in range(4):
                    fetch(i, r)

        @block.scalar
        def _(act):
            with act.Fori(0, QT) as i:
                for r in range(4):
                    t = i * 4 + r
                    act.wait_ge(summed, t + 1)
                    nc.scalar.activation(flat(out[:, bass.ds(t, 1), :]), acc[:, r, :], ACT.Silu).then_inc(gated, 1)

NH, DK = 16, 8
HG = 4
UN = B * NH // HG
COMBOS = [(i, j) for i in range(3) for j in range(3)]
KR = 9 * DK
NEG = -1e30
INV_SQRT_DK = float(1.0 / np.sqrt(np.float32(DK)))


def phase_output0(nc, d, s):
    with ExitStack() as ctx:
        k = Scope(nc, ctx, "o")
        lnw, lnb = k.sb("lnw", [P, DI]), k.sb("lnb", [P, DI])
        wout = k.sb("wout", [P, 2, D])
        y, hd, z = (k.sb(n, [P, 2, TQ, DI]) for n in ("y", "hd", "z"))
        x = k.sb("x", [P, 2, TQ, D])
        sq = k.sb("sq", [P, TQ, DI])
        mean, var, std, inv = (k.sb(n, [P, TQ]) for n in ("mean", "var", "std", "inv"))
        yT = k.sb("yT", [P, 2, TQ, P])
        sg = k.sb("sg", [P, TQ, D])
        psT = k.ps("psT", [P, 2, 2, TQ, P])
        psO = k.ps("psO", [P, 2, TQ, D])
        (loaded, in0, in1, dv, centred, squared, var_ready, std_ready, scaled, shifted, turned, yT_ready, outed, x_ready, stored) = k.sems(
            "loaded in0 in1 dv centred squared var_ready std_ready scaled shifted turned yT_ready outed x_ready stored")
        arrived = (in0, in1)
        block = ctx.enter_context(nc.Block())
        per_b = TQ + 6

        @block.sync
        def _(sp):
            sp.dma_start(lnw[:, :], d["ln_w"]).then_inc(loaded, 16)
            sp.dma_start(lnb[:, :], d["ln_b"]).then_inc(loaded, 16)
            sp.dma_start(wout[:, :, :], d["wout"].rearrange("(c p) o -> p c o", p=P)).then_inc(loaded, 16)

            def load(b, r):
                one = bass.ds(b, 1)
                for dst, name in ((y, "y"), (hd, "hdx"), (z, "z"), (x, "x")):
                    sp.dma_start(dst[:, r, :, :], d[name][one].rearrange("a (q p) e -> p (a q) e", p=P)).then_inc(arrived[r], 16)

            for r in range(2):
                load(r, r)
            with sp.Fori(0, B // 2 - 1) as i:
                for r in range(2):
                    sp.wait_ge(x_ready, i * 2 + r + 1)
                    load(i * 2 + r + 2, r)
            sp.wait_ge(x_ready, B)
            sp.dma_start(d["x1"].rearrange("b (q p) e -> p (b q) e", p=P), s.xc[:, :, :]).then_inc(stored, 16)
            sp.wait_ge(stored, 16)

        @block.vector
        def _(dve):
            v = nc.vector
            dve.wait_ge(loaded, 48)

            def sequence(i, r):
                b = i * 2 + r
                step = Tally(dve, dv, b * per_b)
                yb, hb, zb = y[:, r], hd[:, r], z[:, r]
                dve.wait_ge(arrived[r], (i + 1) * 64)
                for q in range(TQ):
                    step.mark(v.scalar_tensor_tensor(yb[:, q, :], hb[:, q, :], s.kappa[:, q, bass.ds(b, 1)], yb[:, q, :], ALU.mult, ALU.add))
                step.settle()
                step(v.tensor_tensor(yb, yb, zb, ALU.mult))
                step(v.tensor_reduce(mean[:, :], yb, AX.X, ALU.add))
                step(v.tensor_scalar(mean[:, :], mean[:, :], 1.0 / DI, None, ALU.mult))
                v.tensor_tensor(yb, yb, over(mean[:, :], DI), ALU.subtract).then_inc(centred, 1)
                dve.wait_ge(squared, b + 1)
                step(v.tensor_reduce(var[:, :], sq[:, :, :], AX.X, ALU.add))
                v.tensor_scalar(var[:, :], var[:, :], 1.0 / DI, None, ALU.mult).then_inc(var_ready, 1)
                dve.wait_ge(std_ready, b + 1)
                step(v.reciprocal(inv[:, :], std[:, :]))
                v.tensor_tensor(yb, yb, over(inv[:, :], DI), ALU.mult).then_inc(scaled, 1)
                dve.wait_ge(outed, b + 1)
                rows = bass.ds(b * TQ, TQ)
                step(v.tensor_tensor(sg[:, :, :], psO[:, r, :, :], s.g0[:, rows, :], ALU.mult))
                v.tensor_tensor(s.xc[:, rows, :], sg[:, :, :], x[:, r, :, :], ALU.add).then_inc(x_ready, 1)
                assert step.n == per_b

            with dve.Fori(0, B // 2) as i:
                for r in range(2):
                    sequence(i, r)

        @block.gpsimd
        def _(pool):
            pool.wait_ge(loaded, 48)
            with pool.Fori(0, B // 2) as i:
                for r in range(2):
                    pool.wait_ge(scaled, i * 2 + r + 1)
                    wide = [P, TQ, DI]
                    nc.gpsimd.tensor_tensor(z[:, r], y[:, r], lnw[:, :].unsqueeze(1).to_broadcast(wide), ALU.mult).then_inc(shifted, 1)
                    pool.wait_ge(shifted, (i * 2 + r) * 2 + 1)
                    nc.gpsimd.tensor_tensor(hd[:, r], z[:, r], lnb[:, :].unsqueeze(1).to_broadcast(wide), ALU.add).then_inc(shifted, 1)

        @block.tensor
        def _(pe):
            pe.wait_ge(loaded, 48)
            with pe.Fori(0, B // 2) as i:
                for r in range(2):
                    b = i * 2 + r
                    pe.wait_ge(shifted, b * 2 + 2)
                    for c in range(2):
                        for q in range(TQ):
                            ins = nc.tensor.transpose(psT[:, r, c, q, :], hd[:, r, q, c * P:(c + 1) * P], s.ident[:, :])
                        ins.then_inc(turned, 1)
                    pe.wait_ge(yT_ready, b * 2 + 2)
                    for q in range(TQ):
                        for c in range(2):
                            ins = nc.tensor.matmul(psO[:, r, q, :], yT[:, c, q, :], wout[:, c, :], start=c == 0, stop=c == 1)
                    ins.then_inc(outed, 1)

        @block.scalar
        def _(act):
            with act.Fori(0, B // 2) as i:
                for r in range(2):
                    b = i * 2 + r
                    act.wait_ge(centred, b + 1)
                    nc.scalar.activation(sq[:, :, :], y[:, r], ACT.Square).then_inc(squared, 1)
                    act.wait_ge(var_ready, b + 1)
                    nc.scalar.activation(std[:, :], var[:, :], ACT.Sqrt, bias=s.eps[:, 0:1]).then_inc(std_ready, 1)
                    for c in range(2):
                        act.wait_ge(turned, b * 2 + c + 1)
                        nc.scalar.activation(yT[:, c, :, :], psT[:, r, c, :, :], ACT.Copy).then_inc(yT_ready, 1)


def phase_qkv(nc, d, s):
    with ExitStack() as ctx:
        k = Scope(nc, ctx, "q")
        w = k.sb("w", [P, 5, D])
        cos, sin = k.sb("cos", [P, L]), k.sb("sin", [P, L])
        xs = k.sb("xs", [P, TQ, D])
        xT = k.sb("xT", [P, L])
        prod = k.sb("prod", [P, 2, L])
        qk = k.sb("qk", [P, 2, L])
        rest = k.sb("rest", [P, 2, L])
        parts = k.sb("parts", [P, 2, 2, 3, L], BF16)
        psT = k.ps("psT", [P, TQ, P])
        psP = k.ps("psP", [P, 4, L])
        psV = k.ps("psV", [P, TQ, D])
        (loaded, dv, xs_ready, turned, xT_ready, projected, v_projected, v_copied, qk_ready, high, rested, mid, low, slot_free, out0, out1) = k.sems(
            "loaded dv xs_ready turned xT_ready projected v_projected v_copied qk_ready high rested mid low slot_free out0 out1")
        out = (out0, out1)
        block = ctx.enter_context(nc.Block())

        @block.sync
        def _(sp):
            sp.dma_start(w[:, :, :], d["w_qkv"]).then_inc(loaded, 16)
            sp.dma_start(cos[:, :], d["rope_cos"]).then_inc(loaded, 16)
            sp.dma_start(sin[:, :], d["rope_sin"]).then_inc(loaded, 16)
            with sp.Fori(0, B // 2) as n:
                for r in range(2):
                    b = n * 2 + r
                    sp.wait_ge(low, b * 2 + 2)
                    for i in range(3):
                        for m, rows in ((0, slice(3 * i, 3 * i + 3)), (1, slice(i, 9, 3))):
                            src = parts[:, r, m, i, :].unsqueeze(1).to_broadcast([P, 3, L])
                            sp.dma_start(d["qk9"][m, bass.ds(b, 1), rows].rearrange("a c k h t -> (a k h) c t"), src).then_inc(out[r], 16)
                    sp.wait_ge(out[r], (n + 1) * 96)
                    sp.sem_inc(slot_free, 1)

        @block.vector
        def _(dve):
            v = nc.vector
            dve.wait_ge(loaded, 48)
            with dve.Fori(0, B) as b:
                step = Tally(dve, dv, b * 4)
                dve.wait_ge(turned, b)
                rows = bass.ds(b * TQ, TQ)
                v.tensor_copy(xs[:, :, :], s.xc[:, rows, :]).then_inc(xs_ready, 1)
                dve.wait_ge(low, b * 2)
                for m in range(2):
                    dve.wait_ge(projected, b * 2 + m + 1)
                    step.mark(v.tensor_tensor(qk[:, m, :], psP[:, 2 * m, :], cos[:, :], ALU.mult))
                    step(v.tensor_tensor(prod[:, m, :], psP[:, 2 * m + 1, :], sin[:, :], ALU.mult))
                    v.tensor_tensor(qk[:, m, :], qk[:, m, :], prod[:, m, :], ALU.add).then_inc(qk_ready, 1)

        @block.tensor
        def _(pe):
            pe.wait_ge(loaded, 48)
            with pe.Fori(0, B) as b:
                pe.wait_ge(xs_ready, b + 1)
                for q in range(TQ):
                    ins = nc.tensor.transpose(psT[:, q, :], xs[:, q, :], s.ident[:, :])
                ins.then_inc(turned, 1)
                pe.wait_ge(xT_ready, b + 1)
                pe.wait_ge(qk_ready, b * 2)
                pe.wait_ge(v_copied, b)
                for m in range(2):
                    for n in range(2):
                        ins = nc.tensor.matmul(psP[:, 2 * m + n, :], w[:, 2 * m + n, :], xT[:, :], start=True, stop=True)
                    ins.then_inc(projected, 1)
                for q in range(TQ):
                    ins = nc.tensor.matmul(psV[:, q, :], xT[:, q * P:(q + 1) * P], w[:, 4, :], start=True, stop=True)
                ins.then_inc(v_projected, 1)

        @block.scalar
        def _(act):
            act.sem_inc(slot_free, 2)
            with act.Fori(0, B // 2) as i:
                for r in range(2):
                    b = i * 2 + r
                    act.wait_ge(turned, b + 1)
                    act.wait_ge(v_projected, b)
                    nc.scalar.activation(xT[:, :], psT[:, :, :].rearrange("p q t -> p (q t)"), ACT.Copy).then_inc(xT_ready, 1)
                    act.wait_ge(slot_free, b + 1)
                    for m in range(2):
                        act.wait_ge(qk_ready, b * 2 + m + 1)
                        nc.scalar.activation(parts[:, r, m, 0, :], qk[:, m, :], ACT.Copy).then_inc(high, 1)
                    act.wait_ge(v_projected, b + 1)
                    nc.scalar.activation(s.v[:, bass.ds(b * TQ, TQ), :], psV[:, :, :], ACT.Copy).then_inc(v_copied, 1)
                    for m in range(2):
                        act.wait_ge(rested, b * 2 + m + 1)
                        nc.scalar.activation(parts[:, r, m, 1, :], rest[:, m, :], ACT.Copy).then_inc(mid, 1)

        @block.gpsimd
        def _(pool):
            with pool.Fori(0, B // 2) as i:
                for r in range(2):
                    b = i * 2 + r
                    pool.wait_ge(low, b * 2)
                    for m in range(2):
                        pool.wait_ge(high, b * 2 + m + 1)
                        nc.gpsimd.tensor_tensor(rest[:, m, :], qk[:, m, :], parts[:, r, m, 0, :], ALU.subtract).then_inc(rested, 1)
                    for m in range(2):
                        pool.wait_ge(mid, b * 2 + m + 1)
                        nc.gpsimd.tensor_tensor(parts[:, r, m, 2, :], rest[:, m, :], parts[:, r, m, 1, :], ALU.subtract).then_inc(low, 1)

GROUPS = [(0, h, 1) for h in range(HG)] + [(1, h, 1) for h in range(HG)] + [(2, 0, 2), (2, 2, 2)] + [(3, 0, HG)]
NG = len(GROUPS)
ENDS = [4, 8, 10, 11]
HB = B // 2


def phase_attention(nc, d, s):
    with ExitStack() as ctx:
        k = Scope(nc, ctx, "a")
        q = k.sb("q", [KR + 1, 4, HG, L], BF16)
        key = k.sb("key", [KR + 1, 4, HG, L], BF16)
        mask_f, mask = k.sb("mask_f", [P, 2, P]), k.sb("mask", [P, 2, P], BF16)
        eye = k.sb("eye", [P, P], BF16)
        top = k.sb("top", [P, 2, HG, TQ])
        top_row = k.sb("top_row", [HG * TQ, 2, P], BF16)
        pt = k.sb("pt", [P, 2, HG, L])
        vaug = k.sb("vaug", [P, 2, TQ, HG, 32])
        ot = k.sb("ot", [P, 2, L])
        inv = k.sb("inv", [P, TQ, HG])
        xs = k.sb("xs", [P, 2, D])
        idx = k.sb("idx", [P, 2, K1, 1], U32)
        psA = k.ps("psA", [P, 2, 512])
        psB = k.ps("psB", [P, 2, 512])
        psO = k.ps("psO", [P, 512])
        psT = k.ps("psT", [P, TQ, HG, 32])
        psM = k.ps("psM", [P, 512])
        (loaded, dv, consts, key_wiped, ld0, ld1, ld2, ld3, mr0, mr1, mr2, mr3, scored, maxed, top_turned, top_ready, rev_scored, raised, v_ready, summed,
         o_copied, o_turned, o_ready, wiped, sent0, sent1, brought, passed) = k.sems(
            "loaded dv consts key_wiped ld0 ld1 ld2 ld3 mr0 mr1 mr2 mr3 scored maxed top_turned top_ready rev_scored raised v_ready summed "
            "o_copied o_turned o_ready wiped sent0 sent1 brought passed")
        sent = (sent0, sent1)
        ld, row_in = (ld0, ld1, ld2, ld3), (mr0, mr1, mr2, mr3)
        block = ctx.enter_context(nc.Block())

        def run(eng, unit, finish):
            for hg in range(4):
                unit(0, hg, True, False)
            with eng.Fori(1, B - 1) as i:
                for hg in range(4):
                    unit(i, hg, False, False)
            for hg in range(4):
                unit(B - 1, hg, False, True)
            finish()

        @block.sync
        def _(sp):
            sp.dma_start(mask_f[:, :, :], d["mask"]).then_inc(loaded, 16)

            def load(i, hg):
                for m, dst in ((0, q), (1, key)):
                    sp.dma_start(dst[0:KR, hg, :, :], d["qk9"][m, bass.ds(i, 1), :, :, hg * HG:(hg + 1) * HG].rearrange("a c k h t -> (a c k) h t")).then_inc(ld[hg], 16)

            def row(n, hg):
                sp.wait_ge(top_ready, n + 1)
                sp.dma_start(q[KR:KR + 1, hg, :, :], top_row[:, (hg % 2), :]).then_inc(row_in[hg], 16)

            def unit(i, hg, first, last):
                if not (first and hg == 0) and not (last and hg == 3):
                    row(i * 4 + hg + 1, (hg + 1) % 4)
                if not last:
                    sp.wait_ge(rev_scored, (i * 4 + hg + 1) * NG)
                    load(i + 1, hg)

            sp.wait_ge(key_wiped, 1)
            for hg in range(4):
                load(0, hg)
            for n in range(2):
                row(n, n)
            run(sp, unit, lambda: None)

        def max_groups(g):
            far, h0, hn = GROUPS[g]
            return TQ - 1 - far, h0, hn, (TQ - far) * P

        @block.tensor
        def _(pe):
            pe.wait_ge(consts, 1)

            def scores(n, slot, g):
                qt, h0, hn, w = max_groups(g)
                bank = (slot * NG + g) % 2
                if at_least(n * NG + g, 2):
                    pe.wait_ge(maxed, n * NG + g - 1)
                for j in range(hn):
                    h, lo = h0 + j, j * w
                    nc.tensor.matmul(psA[:, bank, lo:lo + w], q[0:KR, slot, h, qt * P:(qt + 1) * P], key[0:KR, slot, h, 0:w], start=True, stop=False)
                    ins = nc.tensor.matmul(psA[:, bank, lo + w - P:lo + w], eye[:, :], mask[:, 0, :], start=False, stop=True)
                ins.then_inc(scored, 1)

            def reversed_scores(n, slot, g):
                kt, h0, hn = GROUPS[g]
                w = (TQ - kt) * P
                bank = (slot * NG + g) % 2
                if at_least(n * NG + g, 2):
                    pe.wait_ge(raised, n * NG + g - 1)
                for j in range(hn):
                    h, lo = h0 + j, j * w
                    nc.tensor.matmul(psB[:, bank, lo:lo + w], key[:, slot, h, kt * P:(kt + 1) * P], q[:, slot, h, kt * P:L], start=True, stop=False)
                    ins = nc.tensor.matmul(psB[:, bank, lo:lo + P], eye[:, :], mask[:, 1, :], start=False, stop=True)
                ins.then_inc(rev_scored, 1)

            def turn_top(n, r):
                pe.wait_ge(maxed, (n + 1) * NG)
                if at_least(n, 1):
                    pe.wait_ge(top_ready, n)
                nc.tensor.transpose(psM[0:HG * TQ, 0:P], flat(top[:, r, :, :]), s.ident[:, :]).then_inc(top_turned, 1)

            def sum_v(n, slot, kt):
                pe.wait_ge(raised, n * NG + ENDS[kt])
                if kt == 0:
                    pe.wait_ge(v_ready, n + 1)
                    if at_least(n, 1):
                        pe.wait_ge(o_copied, n)
                for h in range(HG):
                    ins = nc.tensor.matmul(psO[32 * h:32 * h + 32, kt * P:L], vaug[:, slot % 2, kt, h, :], pt[:, kt % 2, h, 0:L - kt * P], start=kt == 0, stop=kt == TQ - 1)
                ins.then_inc(summed, 1)

            def turn_o(n, r):
                pe.wait_ge(o_copied, n + 1)
                if at_least(n, 1):
                    pe.wait_ge(o_ready, n)
                for qt in range(TQ):
                    ins = nc.tensor.transpose(flat(psT[:, qt, :, :]), ot[:, r, qt * P:(qt + 1) * P], s.ident[:, :])
                ins.then_inc(o_turned, 1)

            def unit(i, hg, first, last):
                n = i * 4 + hg
                ahead = not (last and hg >= 2)
                for g in range(NG):
                    if g == 0:
                        if ahead:
                            pe.wait_ge(ld[(hg + 2) % 4], (i + 1 + (hg >= 2)) * 32)
                        pe.wait_ge(row_in[hg], (i + 1) * 16)
                    if ahead:
                        scores(n + 2, (hg + 2) % 4, g)
                    reversed_scores(n, hg, g)
                    if g == 2 and not (first and hg == 0) and not (last and hg == 3):
                        turn_top(n + 1, (hg + 1) % 2)
                    if g == 4 and not (first and hg == 0):
                        turn_o(n - 1, (hg + 1) % 2)
                    if g == 5:
                        sum_v(n, hg, 0)
                    if g == 9:
                        sum_v(n, hg, 1)
                sum_v(n, hg, 2)
                sum_v(n, hg, 3)

            for n in range(2):
                pe.wait_ge(ld[n], 32)
                for g in range(NG):
                    scores(n, n, g)
            for n in range(2):
                turn_top(n, n)
            run(pe, unit, lambda: turn_o(UN - 1, 1))

        @block.vector
        def _(dve):
            v = nc.vector
            step = Tally(dve, dv)
            nc.vector.memset(key[64:KR + 1, :, :, :], -1.0).then_inc(key_wiped, 1)
            dve.wait_ge(loaded, 16)
            step.mark(v.tensor_copy(mask[:, :, :], mask_f[:, :, :]))
            v.tensor_copy(eye[:, :], s.ident[:, :]).then_inc(consts, 1)

            def maxima(n, slot, g):
                qt, h0, hn, w = max_groups(g)
                dve.wait_ge(scored, n * NG + g + 1)
                if g == 0 and at_least(n, 2):
                    dve.wait_ge(top_turned, n - 1)
                v.tensor_reduce(top[:, slot % 2, h0:h0 + hn, qt], psA[:, (slot * NG + g) % 2, 0:hn * w].rearrange("p (h w) -> p h w", w=w),
                                AX.X, ALU.max).then_inc(maxed, 1)

            def copy_top(i, n, hg):
                dve.wait_ge(top_turned, n + 1)
                before = (hg + 2) % 4
                if at_least(n, 2):
                    dve.wait_ge(row_in[before], (i if hg < 2 else i + 1) * 16)
                v.tensor_copy(top_row[:, hg % 2, :], psM[0:HG * TQ, 0:P]).then_inc(top_ready, 1)

            def divide(i, n, hg):
                dve.wait_ge(o_turned, n + 1)
                if at_least(n, 1):
                    dve.wait_ge(o_ready, n)
                v.reciprocal(inv[:, :, :], psT[:, :, :, DK]).then_inc(dv, 1)
                dve.wait_ge(dv, n + 2)
                v.tensor_tensor(s.o[:, bass.ds(i * TQ, TQ), hg * 32:hg * 32 + 32].rearrange("p q (h c) -> p q h c", c=DK), psT[:, :, :, 0:DK],
                                inv[:, :, :].unsqueeze(3).to_broadcast([P, TQ, HG, DK]), ALU.mult).then_inc(o_ready, 1)

            def unit(i, hg, first, last):
                n = i * 4 + hg
                for g in range(NG):
                    if not (last and hg >= 2):
                        maxima(n + 2, (hg + 2) % 4, g)
                    if g == 3 and not (first and hg == 0) and not (last and hg == 3):
                        copy_top(i if hg < 3 else i + 1, n + 1, (hg + 1) % 4)
                    if g == 5 and not (first and hg == 0):
                        divide(i if hg else i - 1, n - 1, (hg + 3) % 4)

            for n in range(2):
                for g in range(NG):
                    maxima(n, n, g)
            for n in range(2):
                copy_top(0, n, n)
            run(dve, unit, lambda: divide(B - 1, UN - 1, 3))

        @block.scalar
        def _(act):
            def copy_o(n, r):
                act.wait_ge(summed, (n + 1) * TQ)
                if at_least(n, 2):
                    act.wait_ge(o_turned, n - 1)
                nc.scalar.activation(ot[:, r, :], psO[:, :], ACT.Copy).then_inc(o_copied, 1)

            def unit(i, hg, first, last):
                n = i * 4 + hg
                for g in range(NG):
                    kt, h0, hn = GROUPS[g]
                    w = (TQ - kt) * P
                    act.wait_ge(rev_scored, n * NG + g + 1)
                    if g in (0, 4, 8, 10) and not (first and hg == 0 and kt < 2):
                        act.wait_ge(summed, n * TQ + kt - 1)
                    nc.scalar.activation(pt[:, kt % 2, h0:h0 + hn, 0:w], psB[:, (hg * NG + g) % 2, 0:hn * w].rearrange("p (h w) -> p h w", w=w),
                                         ACT.Exp, scale=INV_SQRT_DK).then_inc(raised, 1)
                    if g == 1 and not (first and hg == 0):
                        copy_o(n - 1, (hg + 1) % 2)

            run(act, unit, lambda: copy_o(UN - 1, 1))

        @block.gpsimd
        def _(pool):
            nc.gpsimd.memset(vaug[:, :, :, :, :], 0.0).then_inc(wiped, 1)
            pool.wait_ge(wiped, 1)
            nc.gpsimd.memset(vaug[:, :, :, :, DK:DK + 1], 1.0).then_inc(wiped, 1)
            pool.wait_ge(wiped, 2)

            def send(i, hg, first):
                n, r = i * 4 + hg, hg % 2
                if not (first and hg < 2):
                    pool.wait_ge(sent[r], i * (2 * K1 * 16) + hg // 2 * (K1 * 16))
                nc.gpsimd.tensor_copy(idx[:, r, :, :].rearrange("p c a -> p (c a)"), flat(s.place[:, bass.ds(n, 1), :])).then_inc(brought, 1)
                nc.gpsimd.tensor_copy(xs[:, r, :], flat(s.xc[:, bass.ds(n, 1), :])).then_inc(brought, 1)
                pool.wait_ge(brought, n * 2 + 2)
                pool.sem_inc(passed, 1)
                for c in range(K1):
                    nc.gpsimd.indirect_dma_start(
                        out=d["rows1"], out_offset=bass.IndirectOffsetOnAxis(ap=idx[:, r, c, :], axis=0),
                        in_=xs[:, r, :], in_offset=None, bounds_check=SLOTS1 - 1, oob_is_err=False).then_inc(sent[r], 16)

            def unit(i, hg, first, last):
                n = i * 4 + hg
                if not (first and hg < 2):
                    pool.wait_ge(summed, (n - 1) * TQ)
                nc.gpsimd.tensor_copy(vaug[:, hg % 2, :, :, 0:DK], s.v[:, bass.ds(i * TQ, TQ), hg * 32:hg * 32 + 32].rearrange("p q (h c) -> p q h c", c=DK)).then_inc(v_ready, 1)
                send(i, hg, first)

            run(pool, unit, lambda: None)
            for r in range(2):
                pool.wait_ge(sent[r], NT // 2 * K1 * 16)


def phase_attention_out(nc, d, s):
    with ExitStack() as ctx:
        k = Scope(nc, ctx, "ao")
        w = k.sb("w", [P, D])
        oT = k.sb("oT", [P, 2, TQ, P])
        psT = k.ps("psT", [P, 2, TQ, P])
        psS = k.ps("psS", [P, 2, TQ, D])
        o = k.sb("o", [P, 2, TQ, D])
        loaded, o_ready, turned, oT_ready, projected, copied = k.sems("loaded o_ready turned oT_ready projected copied")
        block = ctx.enter_context(nc.Block())

        @block.sync
        def _(sp):
            sp.dma_start(w[:, :], d["w_o"]).then_inc(loaded, 16)

        @block.tensor
        def _(pe):
            def turn(b, r):
                pe.wait_ge(o_ready, b + 1)
                for q in range(TQ):
                    ins = nc.tensor.transpose(psT[:, r, q, :], o[:, r, q, :], s.ident[:, :])
                ins.then_inc(turned, 1)

            def project(b, r):
                pe.wait_ge(oT_ready, b + 1)
                for q in range(TQ):
                    ins = nc.tensor.matmul(psS[:, r, q, :], oT[:, r, q, :], w[:, :], start=True, stop=True)
                ins.then_inc(projected, 1)

            pe.wait_ge(loaded, 16)
            for r in range(2):
                turn(r, r)
            with pe.Fori(0, HB - 1) as i:
                for r in range(2):
                    b = i * 2 + r
                    pe.wait_ge(copied, i * 2)
                    project(b, r)
                    turn(b + 2, r)
            for r in range(2):
                pe.wait_ge(copied, (HB - 1) * 2)
                project(B - 2 + r, r)

        @block.vector
        def _(dve):
            with dve.Fori(0, HB) as i:
                for r in range(2):
                    b = i * 2 + r
                    dve.wait_ge(turned, b + 1)
                    dve.wait_ge(projected, i * 2)
                    nc.vector.tensor_copy(oT[:, r, :, :], psT[:, r, :, :]).then_inc(oT_ready, 1)

        @block.scalar
        def _(act):
            with act.Fori(0, HB) as i:
                for r in range(2):
                    b = i * 2 + r
                    act.wait_ge(projected, b + 1)
                    nc.scalar.activation(s.s1[:, bass.ds(b * TQ, TQ), :], psS[:, r, :, :], ACT.Copy).then_inc(copied, 1)

        @block.gpsimd
        def _(pool):
            def bring(b, r):
                nc.gpsimd.tensor_copy(o[:, r, :, :], s.o[:, bass.ds(b * TQ, TQ), :]).then_inc(o_ready, 1)

            for r in range(2):
                bring(r, r)
            with pool.Fori(0, HB - 1) as i:
                for r in range(2):
                    pool.wait_ge(turned, i * 2 + r + 1)
                    bring(i * 2 + r + 2, r)

def phase_route1(nc, d, s):
    with ExitStack() as ctx:
        k = Scope(nc, ctx, "u")
        sel_w = k.sb("sel_w", [P, 2 * E1])
        number = k.sb("number", [P, E1])
        tri_f, tri = k.sb("tri_f", [P, P]), k.sb("tri", [P, P], BF16)
        ones = k.sb("ones", [P, P], BF16)
        tile_no = k.sb("tile_no", [P, 2])
        xs = k.sb("xs", [P, 2, TQ, D])
        xT = k.sb("xT", [P, 2, TQ, P])
        sel, low = (k.sb(n, [P, NT, E1]) for n in ("sel", "low"))
        one = k.sb("one", [P, K1, NT, E1], BF16)
        picks = k.sb("picks", [P, NT, E1], BF16)
        best, first = k.sb("best", [P, NT]), k.sb("first", [P, NT])
        tiles, grown = k.sb("tiles", [P, E1]), k.sb("grown", [P, 2, E1])
        done = k.sb("done", [P, 2, E1])
        expert, expert_i = k.sb("expert", [P, 2]), k.sb("expert_i", [P, 2], I32)
        ps = k.ps("ps", [P, 8, 512])
        psT = [ps[:, r, :].rearrange("p (q t) -> p q t", t=P) for r in range(2)]
        psL = [ps[:, 2 + r, :].rearrange("p (q t) -> p q t", t=P) for r in range(2)]
        per_bank = 512 // E1
        loaded, dv, xs_ready, turned, xT_ready, scored, raised, picked, counted, named, written = k.sems(
            "loaded dv xs_ready turned xT_ready scored raised picked counted named written")
        block = ctx.enter_context(nc.Block())

        @block.sync
        def _(sp):
            sp.dma_start(sel_w[:, :], d["sel_w"]).then_inc(loaded, 16)
            sp.dma_start(number[:, :], d["number1"]).then_inc(loaded, 16)
            sp.dma_start(tri_f[:, :], d["tri"]).then_inc(loaded, 16)
            sp.dma_start(tile_no[:, :], d["tile_no"]).then_inc(loaded, 16)
            sp.wait_ge(named, 1)
            sp.dma_start(d["expert_of"].rearrange("(p a) -> p a", p=P), expert_i[:, :]).then_inc(written, 16)
            sp.wait_ge(written, 16)
            sp.dma_start(s.tile_expert[:, :], d["expert_of"].rearrange("(o t) -> o t", o=1)).then_inc(written, 16)
            sp.wait_ge(written, 32)

        @block.vector
        def _(dve):
            v = nc.vector
            step = Tally(dve, dv)
            step.mark(v.memset(ones[:, :], 1.0))

            def bring(b, r):
                v.tensor_copy(xs[:, r, :, :], s.xc[:, bass.ds(b * TQ, TQ), :]).then_inc(xs_ready, 1)

            for r in range(2):
                bring(r, r)
            with dve.Fori(0, HB - 1) as i:
                for r in range(2):
                    dve.wait_ge(turned, i * 2 + r + 1)
                    bring(i * 2 + r + 2, r)
            dve.wait_ge(loaded, 64)
            step.mark(v.tensor_copy(tri[:, :], tri_f[:, :]))
            dve.wait_ge(raised, B)
            step(v.tensor_scalar(low[:, :, :], sel[:, :, :], 1.0, None, ALU.add))
            step(v.reciprocal(sel[:, :, :], low[:, :, :]))
            wide = [P, NT, E1]
            for c in range(K1):
                step(v.tensor_reduce(best[:, :], sel[:, :, :], AX.X, ALU.max))
                step.mark(v.tensor_copy(s.chosen[:, :, c], best[:, :]))
                step(v.tensor_tensor(low[:, :, :], sel[:, :, :], over(best[:, :], E1), ALU.is_lt))
                step(v.scalar_tensor_tensor(low[:, :, :], low[:, :, :], float(E1), number[:, :].unsqueeze(1).to_broadcast(wide), ALU.mult, ALU.add))
                step(v.tensor_reduce(first[:, :], low[:, :, :], AX.X, ALU.min))
                step(v.tensor_tensor(one[:, c], number[:, :].unsqueeze(1).to_broadcast(wide), over(first[:, :], E1), ALU.is_equal))
                if c < K1 - 1:
                    step(v.scalar_tensor_tensor(sel[:, :, :], one[:, c], -2.0, sel[:, :, :], ALU.mult, ALU.add))
            step(v.tensor_tensor(picks[:, :, :], one[:, 0], one[:, 1], ALU.add))
            step(v.tensor_tensor(picks[:, :, :], picks[:, :, :], one[:, 2], ALU.add))
            v.tensor_tensor(picks[:, :, :], picks[:, :, :], one[:, 3], ALU.add).then_inc(picked, 1)
            dve.wait_ge(counted, 1)

            def in_tile(t):
                lo = t % per_bank * E1
                return ps[:, 4 + t // per_bank, lo:lo + E1]

            step(v.memset(low[:, 0, :], 0.0))
            for t in range(1, NT):
                step(v.tensor_tensor(low[:, t, :], low[:, t - 1, :], in_tile(t - 1), ALU.add))
            step(v.tensor_tensor(tiles[:, :], low[:, NT - 1, :], in_tile(NT - 1), ALU.add))
            step(v.tensor_scalar(tiles[:, :], tiles[:, :], 1.0 / P, (P / 2 - 0.5) / P, ALU.mult, ALU.add))
            step(v.tensor_scalar(tiles[:, :], tiles[:, :], ROUND, -ROUND, ALU.add, ALU.add))
            step(v.tensor_copy(grown[:, 0, :], tiles[:, :]))
            at, by = 0, 1
            while by < E1:
                step.mark(v.tensor_copy(grown[:, 1 - at, 0:by], grown[:, at, 0:by]))
                step(v.tensor_tensor(grown[:, 1 - at, by:E1], grown[:, at, by:E1], grown[:, at, 0:E1 - by], ALU.add))
                at, by = 1 - at, by * 2
            end, start = grown[:, at, :], grown[:, 1 - at, :]
            step(v.tensor_tensor(done[:, :, :], end.unsqueeze(1).to_broadcast([P, 2, E1]), over(tile_no[:, :], E1), ALU.is_le))
            step(v.tensor_reduce(expert[:, :], done[:, :, :], AX.X, ALU.add))
            step(v.tensor_scalar(expert[:, :], expert[:, :], float(E1 - 1), None, ALU.min))
            v.tensor_copy(expert_i[:, :], expert[:, :]).then_inc(named, 1)
            step(v.tensor_tensor(start, end, tiles[:, :], ALU.subtract))
            step(v.tensor_scalar(start, start, float(P), -1.0, ALU.mult, ALU.add))
            for n in range(4):
                rows = slice(n * per_bank, (n + 1) * per_bank)
                step.mark(v.tensor_tensor(low[:, rows, :], low[:, rows, :], ps[:, n, :].rearrange("p (t e) -> p t e", e=E1), ALU.add))
            step.settle()
            step(v.tensor_tensor(low[:, :, :], low[:, :, :], start.unsqueeze(1).to_broadcast(wide), ALU.add))
            for c in range(K1):
                step(v.tensor_tensor(sel[:, :, :], low[:, :, :], one[:, c], ALU.mult))
                step(v.tensor_reduce(first[:, :], sel[:, :, :], AX.X, ALU.add))
                step(v.tensor_copy(s.place[:, :, c], first[:, :]))

        @block.tensor
        def _(pe):
            pe.wait_ge(loaded, 64)

            def turn(b, r):
                pe.wait_ge(xs_ready, b + 1)
                for t in range(TQ):
                    ins = nc.tensor.transpose(psT[r][:, t, :], xs[:, r, t, :], s.ident[:, :])
                ins.then_inc(turned, 1)

            def score(b, r):
                pe.wait_ge(xT_ready, b + 1)
                for t in range(TQ):
                    ins = nc.tensor.matmul(psL[r][:, t, :], xT[:, r, t, :], sel_w[:, :], start=True, stop=True)
                ins.then_inc(scored, 1)

            for r in range(2):
                turn(r, r)
            for r in range(2):
                score(r, r)
                turn(2 + r, r)
            with pe.Fori(1, HB - 1) as i:
                for r in range(2):
                    pe.wait_ge(raised, i * 2)
                    score(i * 2 + r, r)
                    turn(i * 2 + r + 2, r)
            for r in range(2):
                pe.wait_ge(raised, B - 2)
                score(B - 2 + r, r)
            pe.wait_ge(picked, 1)
            flat_picks = flat(picks[:, :, :])
            for n in range(4):
                nc.tensor.matmul(ps[:, n, :], tri[:, :], flat_picks[:, n * 512:(n + 1) * 512], start=True, stop=True)
            for n in range(4):
                ins = nc.tensor.matmul(ps[:, 4 + n, :], ones[:, :], flat_picks[:, n * 512:(n + 1) * 512], start=True, stop=True)
            ins.then_inc(counted, 1)

        @block.scalar
        def _(act):
            def block_of_four(b, r, first):
                act.wait_ge(turned, b + 1)
                if not first:
                    act.wait_ge(scored, b - 1)
                nc.scalar.activation(xT[:, r, :, :], psT[r], ACT.Copy).then_inc(xT_ready, 1)
                act.wait_ge(scored, b + 1)
                nc.scalar.activation(sel[:, bass.ds(b * TQ, TQ), :], psL[r][:, :, 0:E1], ACT.Exp, scale=-1.0).then_inc(raised, 1)

            for r in range(2):
                block_of_four(r, r, True)
            with act.Fori(1, HB) as i:
                for r in range(2):
                    block_of_four(i * 2 + r, r, False)


def phase_experts1(nc, d, s):
    with ExitStack() as ctx:
        k = Scope(nc, ctx, "x")
        x, o = (k.sb(n, [P, 4, 4, D]) for n in ("x", "o"))
        w = k.sb("w", [P, 4, 4, 2 * P])
        xT, hT = (k.sb(n, [P, 2, 4, P]) for n in ("xT", "hT"))
        psX, psH, psO = (k.ps(n, [P, 2, 4, P]) for n in ("psX", "psH", "psO"))
        x_turned, xT_ready, hidden, hT_ready, outed, o_ready = k.sems("x_turned xT_ready hidden hT_ready outed o_ready")
        x_in, w_in, o_out = k.sems("x_in0 x_in1 x_in2 x_in3"), k.sems("w_in0 w_in1 w_in2 w_in3"), k.sems("o_out0 o_out1 o_out2 o_out3")
        block = ctx.enter_context(nc.Block())
        rows_in = d["rows1"].rearrange("(g t p) e -> g p t e", t=4, p=P)
        rows_out = d["rows1o"].rearrange("(g t p) e -> g p t e", t=4, p=P)
        QG = GR // 4

        def run(eng, stage):
            for r in range(4):
                stage(0, r)
            with eng.Fori(1, QG) as i:
                for r in range(4):
                    stage(i, r)

        @block.sync
        def _(sp):
            def load(i, r):
                g = i * 4 + r
                if at_least(i, 1):
                    sp.wait_ge(outed, g - 3)
                for t in range(4):
                    e = sp.value_load(s.tile_expert[0:1, bass.ds(g * 4 + t, 1)], min_val=0, max_val=E1 - 1)
                    sp.dma_start(w[:, r, t, :], d["keys_values"][bass.ds(e, 1)].rearrange("a p h -> (a p) h")).then_inc(w_in[r], 16)

            run(sp, load)

        @block.gpsimd
        def _(pool):
            def load(i, r):
                if at_least(i, 1):
                    pool.wait_ge(x_turned, i * 4 + r - 3)
                pool.dma_start(x[:, r, :, :], rows_in[bass.ds(i * 4 + r, 1)].rearrange("a p t e -> (a p) t e")).then_inc(x_in[r], 16)

            def store(i, r):
                pool.wait_ge(o_ready, i * 4 + r + 1)
                pool.dma_start(rows_out[bass.ds(i * 4 + r, 1)].rearrange("a p t e -> (a p) t e"), o[:, r, :, :]).then_inc(o_out[r], 16)

            for r in range(4):
                load(0, r)
            with pool.Fori(1, QG) as i:
                for r in range(4):
                    load(i, r)
                    store(i - 1, r)
            for r in range(4):
                store(QG - 1, r)
            for r in range(4):
                pool.wait_ge(o_out[r], QG * 16)

        @block.tensor
        def _(pe):
            def turn(i, r):
                g = i * 4 + r
                pe.wait_ge(x_in[r], i * 16 + 16)
                if at_least(g, 2):
                    pe.wait_ge(xT_ready, g - 1)
                for t in range(4):
                    ins = nc.tensor.transpose(psX[:, r % 2, t, :], x[:, r, t, :], s.ident[:, :])
                ins.then_inc(x_turned, 1)

            def first(i, r):
                g = i * 4 + r
                pe.wait_ge(xT_ready, g + 1)
                pe.wait_ge(w_in[r], i * 64 + 64)
                if at_least(g, 2):
                    pe.wait_ge(hT_ready, g - 1)
                for t in range(4):
                    ins = nc.tensor.matmul(psH[:, r % 2, t, :], w[:, r, t, 0:P], xT[:, r % 2, t, :], start=True, stop=True)
                ins.then_inc(hidden, 1)

            def second(i, r):
                g = i * 4 + r
                pe.wait_ge(hT_ready, g + 1)
                if at_least(g, 2):
                    pe.wait_ge(o_ready, g - 1)
                for t in range(4):
                    ins = nc.tensor.matmul(psO[:, r % 2, t, :], hT[:, r % 2, t, :], w[:, r, t, P:2 * P], start=True, stop=True)
                ins.then_inc(outed, 1)

            def stage(i, r):
                if not isinstance(i, int) or i < QG - 1 or r < 3:
                    turn(i + (r + 1) // 4, (r + 1) % 4)
                first(i, r)
                if r or at_least(i, 1):
                    second(i if r else i - 1, (r + 3) % 4)

            turn(0, 0)
            for r in range(4):
                stage(0, r)
            with pe.Fori(1, QG - 1) as i:
                for r in range(4):
                    stage(i, r)
            for r in range(4):
                stage(QG - 1, r)
            second(QG - 1, 3)

        @block.scalar
        def _(act):
            def turned(i, r):
                g = i * 4 + r
                act.wait_ge(x_turned, g + 1)
                if at_least(g, 2):
                    act.wait_ge(hidden, g - 1)
                nc.scalar.activation(xT[:, r % 2, :, :], psX[:, r % 2, :, :], ACT.Copy).then_inc(xT_ready, 1)

            def out(i, r):
                g = i * 4 + r
                act.wait_ge(outed, g + 1)
                if at_least(g, 4):
                    act.wait_ge(o_out[r], i * 16)
                nc.scalar.activation(o[:, r, :, :], psO[:, r % 2, :, :], ACT.Copy).then_inc(o_ready, 1)

            def stage(i, r):
                if not isinstance(i, int) or i < QG - 1 or r < 3:
                    turned(i + (r + 1) // 4, (r + 1) % 4)
                if r or at_least(i, 1):
                    out(i if r else i - 1, (r + 3) % 4)

            turned(0, 0)
            for r in range(4):
                stage(0, r)
            for r in range(4):
                stage(1, r)
            with act.Fori(2, QG - 1) as i:
                for r in range(4):
                    stage(i, r)
            for r in range(4):
                stage(QG - 1, r)
            out(QG - 1, 3)

        @block.vector
        def _(dve):
            def hide(i, r):
                g = i * 4 + r
                dve.wait_ge(hidden, g + 1)
                if at_least(g, 2):
                    dve.wait_ge(outed, g - 1)
                nc.vector.tensor_scalar(hT[:, r % 2, :, :], psH[:, r % 2, :, :], 0.0, None, ALU.max).then_inc(hT_ready, 1)

            run(dve, hide)


def phase_final(nc, d, s):
    with ExitStack() as ctx:
        k = Scope(nc, ctx, "z")
        x = k.sb("x", [P, NT, D])
        loaded, multiplied, ready, stored = k.sems("loaded multiplied ready stored")
        block = ctx.enter_context(nc.Block())

        def cut(ap, b):
            return ap[:, b * TQ:(b + 1) * TQ, :]

        @block.sync
        def _(sp):
            sp.dma_start(x[:, :, :], d["x1"].rearrange("b (q p) e -> p (b q) e", p=P)).then_inc(loaded, 16)
            for b in range(B):
                sp.wait_ge(ready, b + 1)
                sp.dma_start(d["out"][b].rearrange("(q p) e -> p q e", p=P), cut(x, b)).then_inc(stored, 16)
            sp.wait_ge(stored, 16 * B)

        @block.vector
        def _(dve):
            for b in range(B):
                nc.vector.tensor_tensor(cut(s.g1, b), cut(s.g1, b), cut(s.s1, b), ALU.mult).then_inc(multiplied, 1)
                if b == 0:
                    dve.wait_ge(loaded, 16)
                dve.wait_ge(multiplied, b + 1)
                nc.vector.tensor_tensor(cut(x, b), cut(x, b), cut(s.g1, b), ALU.add).then_inc(ready, 1)


class Shared:
    pass


def phase_start(nc, d, s, k):
    loaded, = k.sems("ident_loaded")
    with nc.Block() as block:
        @block.sync
        def _(sp):
            sp.dma_start(s.ident[:, :], d["ident"]).then_inc(loaded, 16)
            sp.wait_ge(loaded, 16)


def phase_store(nc, k, name, src, dst):
    stored, = k.sems(name)
    with nc.Block() as block:
        @block.sync
        def _(sp):
            sp.dma_start(dst.rearrange("b (q p) e -> p (b q) e", p=P), src).then_inc(stored, 16)
            sp.wait_ge(stored, 16)


def program(nc, d):
    def dram(name, shape, dt=F32):
        d[name] = nc.dram_tensor(name, shape, dt).ap()

    dram("lnp", (2, 3, 4, L, DI), BF16)
    dram("hdp", (2, 6, 4, L + 1, DI), BF16)
    dram("st0", (B, L + 1, 6 * NS), BF16)
    dram("st1", (B, L, 6 * NS), BF16)
    dram("y", (B, L, DI))
    dram("hdx", (B, L, DI))
    dram("z", (B, L, DI))
    dram("xin", (SLOTS, D))
    dram("eout", (SLOTS, D))
    dram("x1", (B, L, D))
    dram("qk9", (2, B, 9, DK, NH, L), BF16)
    dram("rows1", (SLOTS1, D))
    dram("rows1o", (SLOTS1, D))
    dram("expert_of", (2 * P,), I32)
    s = Shared()
    Scope.taken = []
    with ExitStack() as whole:
        k = Scope(nc, whole, "s")
        s.ident, s.eps, s.rstd = k.sb("ident", [P, P]), k.sb("eps", [P, 1]), k.sb("rstd", [P, NT])
        s.xc = k.sb("xc", [P, NT, D])
        phase_start(nc, d, s, k)
        with ExitStack() as layer0:
            k0 = Scope(nc, layer0, "s0")
            s.g0 = k0.sb("g0", [P, NT, D])
            s.kappa = k0.sb("kappa", [P, TQ, B])
            with ExitStack() as before_output:
                k1 = Scope(nc, before_output, "s1")
                s.bcr = k1.sb("bcr", [P, NT, WC - 3 * DI])
                with ExitStack() as projections:
                    k2 = Scope(nc, projections, "s2")
                    s.xi, s.pre = k2.sb("xi", [P, NT, DI]), k2.sb("pre", [P, NT, DI])
                    with ExitStack() as tokens:
                        k3 = Scope(nc, tokens, "s3")
                        s.zp = k3.sb("zp", [P, NT, DI])
                        s.place, s.fetch = k3.sb("place", [P, NT, 2], U32), k3.sb("fetch", [P, NT, 2], U32)
                        s.gate = k3.sb("gate", [P, NT, 2])
                        phase_norm(nc, d, s, "n0", d["x"], False)
                        phase_project(nc, d, s)
                        phase_route0(nc, d, s)
                        phase_scatter(nc, d, s, "d0", d["xin"], 2, SLOTS, SLOTS)
                        phase_experts0(nc, d, s)
                        phase_gather(nc, d, s, "h0", d["eout"], 2, s.gate, s.g0)
                        phase_store(nc, k3, "z_stored", s.zp[:, :, :], d["z"])
                    phase_steps(nc, d, s)
                    phase_store(nc, k2, "hdx_stored", s.xi[:, :, :], d["hdx"])
                k4 = Scope(nc, before_output, "s4")
                s.cos_c, s.sin_c = k4.sb("cos_c", [P, L]), k4.sb("sin_c", [P, L])
                s.c_col = k4.sb("c_col", [P, 2, L])
                s.marg = k4.sb("marg", [108, 2, CH, 2, DI], BF16)
                phase_rotation(nc, d, s)
                phase_scan(nc, d, s)
            phase_output0(nc, d, s)
        Scope.clear_all(nc)
        s.s1 = k.sb("s1", [P, NT, D])
        phase_norm(nc, d, s, "n1", None, True)
        s.place, s.chosen = k.sb("place1", [P, NT, K1], U32), k.sb("chosen", [P, NT, K1])
        s.fetch = s.place
        s.tile_expert = k.sb("tile_expert", [1, 2 * P], I32)
        phase_route1(nc, d, s)
        with ExitStack() as attention:
            k6 = Scope(nc, attention, "s6")
            s.v, s.o = k6.sb("v", [P, NT, D]), k6.sb("o", [P, NT, D])
            phase_qkv(nc, d, s)
            phase_attention(nc, d, s)
            phase_attention_out(nc, d, s)
        s.g1 = k.sb("g1", [P, NT, D])
        phase_experts1(nc, d, s)
        phase_gather(nc, d, s, "h1", d["rows1o"], K1, s.chosen, s.g1)
        phase_final(nc, d, s)


def lay_out(inputs):
    w = {name: np.asarray(a) for name, a in inputs.items()}
    state = np.arange(P) % NS
    rows = lambda a: np.tile(a, (P, 1))
    f = {"x": w["L0_attn_x"], "ident": np.eye(P, dtype=np.float32)}
    f["wcat"] = np.concatenate([w["L0_attn_W_in"].T, w["L0_attn_W_dt"].T, w["L0_attn_W_B"].T, w["L0_attn_W_C"].T, w["L0_ffn_w_router"]], 1)
    f["b_dt"], f["dt_bias"] = rows(w["L0_attn_b_dt"]), rows(w["L0_attn_dt_bias"])
    freq = w["L0_attn_rope_freq"]
    f["freq"], f["freq_col"] = rows(freq), np.tile(freq, 2 * 4)[:, None]
    f["sign_col"] = np.where(state < HALF, 1.0, -1.0)[:, None]
    f["steps"] = np.arange(L).reshape(TQ, P).T
    f["steps_row"] = rows(np.arange(L))
    f["alog"] = np.tile(w["L0_attn_A_log"].T, (3, 1))
    at = np.arange(P)
    group = at // NS
    same = group[:, None] == group[None]
    f["eye_j"] = np.stack([np.eye(P), same & ((at[:, None] + HALF) % NS == state[None])], 1)
    f["mask4"] = group[:, None] == np.arange(4)[None]
    r = np.arange(3 * NS + 12)
    f["sel"] = np.where(r[:, None] < 3 * NS, r[:, None] % NS == state[None], (r[:, None] - 3 * NS) % 4 == group[None])
    f["tri"] = at[:, None] <= at[None]
    f["number"] = np.tile(np.arange(E0), (P, NT, 1))
    f["offset"] = np.broadcast_to((np.arange(NT) // (NT // G0) * E0 * C0)[None, :, None, None] + (np.arange(E0) * C0), (P, NT, 2, E0))
    f["wi"], f["wo"] = w["L0_ffn_wi"], w["L0_ffn_wo"]
    f["ln_w"], f["ln_b"] = rows(w["L0_attn_ln_w"]), rows(w["L0_attn_ln_b"])
    f["wout"] = w["L0_attn_W_out"].T
    q, key, v, o = (w["L1_attn_W_" + c].T for c in "qkvo")
    order = at % NH * DK + at // NH
    f["w_qkv"], f["w_o"] = np.stack([q[:, order], q[:, order ^ 1], key[:, order], key[:, order ^ 1], v], 1), o
    theta = np.float32(10000.0) ** (-2.0 * np.arange(DK // 2, dtype=np.float32) / np.float32(DK))
    angle = np.minimum(np.arange(L), 255).astype(np.float32)[:, None] * theta[None].astype(np.float32)
    pair = at // NH // 2
    f["rope_cos"] = np.cos(angle)[:, pair].T
    f["rope_sin"] = (np.sin(angle)[:, pair] * np.where(at // NH % 2 == 0, -1, 1)).T
    f["mask"] = np.stack([np.where(at[None] > at[:, None], NEG, 0), np.where(at[None] < at[:, None], NEG, 0)], 1)
    f["sel_w"] = np.tile(w["L1_ffn_expert_sel"].T, (1, 2))
    f["number1"] = rows(np.arange(E1))
    f["tile_no"] = 2 * at[:, None] + np.arange(2)
    f["keys_values"] = np.concatenate([w["L1_ffn_keys"], w["L1_ffn_values"]], 2)
    return {name: np.ascontiguousarray(a, dtype=np.float32) for name, a in f.items()}


def kernel(**inputs):
    import concourse.bacc as bacc
    from concourse.bass_utils import run_bass_kernel_spmd

    arrays = lay_out(inputs)
    nc = bacc.Bacc("TRN2", target_bir_lowering=False, num_devices=1)
    d = {name: nc.dram_tensor(name, a.shape, F32, kind="ExternalInput").ap() for name, a in arrays.items()}
    d["out"] = nc.dram_tensor("out", (B, L, D), F32, kind="ExternalOutput").ap()
    program(nc, d)
    r = run_bass_kernel_spmd(nc, [arrays], core_ids=[0])
    return r.results[0]["out"]
```

```python
import numpy as np
from contextlib import ExitStack
import concourse.bass as bass
from concourse import mybir

F32 = mybir.dt.float32
BF16 = mybir.dt.bfloat16
I32 = mybir.dt.int32
U32 = mybir.dt.uint32
ALU = mybir.AluOpType
ACT = mybir.ActivationFunctionType
AX = mybir.AxisListType

P = 128
B, L, D = 8, 512, 128
T = B * L
NT = T // P
TQ = L // P
DI, NS = 256, 32
HALF = NS // 2
E0, C0, F0, G0 = 8, 80, 512, 2
WC = 2 * DI + DI + 2 * NS + E0
E1, K1 = 64, 4
TILES1 = T * K1 // P + E1
GR = TILES1 // 4
SLOTS1 = TILES1 * P
EPS = 1e-5
CH = 16
BODY = 2 * CH
NB = L // BODY
FILL = SLOTS1 // P // NB
LN2 = float(np.log(2.0))
TINY = 2.0 ** -60
LOG_TINY = 60.0 * LN2


class Tally:

    def __init__(self, eng, sem, base=0):
        self.eng, self.sem, self.base, self.n = eng, sem, base, 0

    def mark(self, ins):
        self.n += 1
        ins.then_inc(self.sem, 1)
        return self.n

    def settle(self):
        self.eng.wait_ge(self.sem, self.base + self.n)

    def __call__(self, ins):
        self.mark(ins)
        self.settle()

    def alternate(self, ins):
        self.mark(ins)
        if self.n > 1:
            self.eng.wait_ge(self.sem, self.base + (self.n - 1))


class Scope:
    taken = []

    def __init__(self, nc, ctx, tag):
        self.nc, self.ctx, self.tag = nc, ctx, tag

    def sb(self, name, shape, dt=F32):
        return self.ctx.enter_context(self.nc.sbuf_tensor(f"{self.tag}_{name}", shape, dt))

    def ps(self, name, shape, dt=F32):
        return self.ctx.enter_context(self.nc.psum_tensor(f"{self.tag}_{name}", shape, dt))

    def sems(self, names):
        new = [self.nc.alloc_semaphore(f"{self.tag}_{n}") for n in names.split()]
        Scope.taken.extend(new)
        return new

    @staticmethod
    def clear_all(nc):
        nc.clear_and_free_semaphores(Scope.taken)
        Scope.taken = []
        nc.all_engine_barrier()


def at_least(n, low):
    return not isinstance(n, int) or n >= low


def over(ap, n):
    return ap.unsqueeze(2).to_broadcast([ap.shape[0], ap.shape[1], n])


def phase_norm(nc, d, s, tag, source, scaled):
    with ExitStack() as ctx:
        k = Scope(nc, ctx, tag)
        sq = k.sb("sq", [P, NT, D])
        mean = k.sb("mean", [P, NT])
        var = k.sb("var", [P, NT])
        std = k.sb("std", [P, NT])
        dv, centred, squared, var_ready, std_ready = k.sems("dv centred squared var_ready std_ready")
        loaded = k.sems("loaded0 loaded1 loaded2 loaded3")
        block = ctx.enter_context(nc.Block())
        CUTS = 4
        cut = [slice(c * NT // CUTS, (c + 1) * NT // CUTS) for c in range(CUTS)]

        @block.sync
        def _(sp):
            if source is not None:
                tiles = source.rearrange("b (q p) e -> p (b q) e", p=P)
                for c in range(CUTS):
                    sp.dma_start(s.xc[:, cut[c], :], tiles[:, cut[c], :]).then_inc(loaded[c], 16)

        @block.vector
        def _(dve):
            step = Tally(dve, dv)
            step.mark(nc.vector.memset(s.eps[:, :], EPS))
            for c in range(CUTS):
                x = s.xc[:, cut[c], :]
                if source is not None:
                    dve.wait_ge(loaded[c], 16)
                step(nc.vector.tensor_reduce(mean[:, cut[c]], x, AX.X, ALU.add))
                step(nc.vector.tensor_scalar(mean[:, cut[c]], mean[:, cut[c]], 1.0 / D, None, ALU.mult))
                nc.vector.tensor_tensor(x, x, over(mean[:, cut[c]], D), ALU.subtract).then_inc(centred, 1)
            for c in range(CUTS):
                dve.wait_ge(squared, c + 1)
                step.mark(nc.vector.tensor_reduce(var[:, cut[c]], sq[:, cut[c], :], AX.X, ALU.add))
            step.settle()
            nc.vector.tensor_scalar(var[:, :], var[:, :], 1.0 / D, None, ALU.mult).then_inc(var_ready, 1)
            dve.wait_ge(std_ready, 1)
            step(nc.vector.reciprocal(s.rstd[:, :], std[:, :]))
            if scaled:
                step(nc.vector.tensor_tensor(s.xc[:, :, :], s.xc[:, :, :], over(s.rstd[:, :], D), ALU.mult))

        @block.scalar
        def _(act):
            for c in range(CUTS):
                act.wait_ge(centred, c + 1)
                nc.scalar.activation(sq[:, cut[c], :], s.xc[:, cut[c], :], ACT.Square).then_inc(squared, 1)
            act.wait_ge(var_ready, 1)
            nc.scalar.activation(std[:, :], var[:, :], ACT.Sqrt, bias=s.eps[:, 0:1]).then_inc(std_ready, 1)


def phase_project(nc, d, s, ctx, block):
    k = Scope(nc, ctx, "p")
    wcat = k.sb("wcat", [P, WC])
    bias = k.sb("bias", [P, DI])
    bias2 = k.sb("bias2", [P, DI])
    xs = k.sb("xs", [P, 2, P])
    xT = k.sb("xT", [P, 2, P])
    psT = k.ps("psT", [P, 2, 512])
    ps1 = k.ps("ps1", [P, 2, 512])
    ps2 = k.ps("ps2", [P, 2, 512])
    loaded, dv, xs_ready, turned, xT_ready, projected, read_act, read_dve = k.sems(
        "loaded dv xs_ready turned xT_ready projected read_act read_dve")

    @block.sync
    def _(sp):
        sp.dma_start(wcat[:, :], d["wcat"]).then_inc(loaded, 16)
        sp.dma_start(bias[:, :], d["b_dt"]).then_inc(loaded, 16)
        sp.dma_start(bias2[:, :], d["dt_bias"]).then_inc(loaded, 16)

    @block.vector
    def _(dve):
        step = Tally(dve, dv)
        dve.wait_ge(loaded, 48)
        step(nc.vector.tensor_tensor(bias[:, :], bias[:, :], bias2[:, :], ALU.add))

        def normalise(n, r):
            nc.vector.tensor_scalar(xs[:, r, :], s.xc[:, bass.ds(n, 1), :].rearrange("p a e -> p (a e)"),
                                    s.rstd[:, bass.ds(n, 1)], None, ALU.mult).then_inc(xs_ready, 1)

        def take(n, r):
            dve.wait_ge(projected, n + 1)
            nc.vector.tensor_tensor(s.pre[:, bass.ds(n, 1), :].rearrange("p a e -> p (a e)"),
                                    ps2[:, r, 0:DI], bias[:, :], ALU.add)
            nc.vector.tensor_copy(s.bcr[:, bass.ds(n, 1), :].rearrange("p a e -> p (a e)"),
                                  ps2[:, r, DI:WC - 2 * DI]).then_inc(read_dve, 1)

        normalise(0, 0)
        normalise(1, 1)
        with dve.Fori(0, NT // 2 - 1) as pair:
            for r in range(2):
                n = pair * 2
                dve.wait_ge(turned, n + r + 1)
                normalise(n + r + 2, r)
                take(n + r, r)
        for r in range(2):
            take(NT - 2 + r, r)

    @block.tensor
    def _(pe):
        pe.wait_ge(loaded, 48)

        def turn(n, r):
            pe.wait_ge(xs_ready, n + 1)
            nc.tensor.transpose(psT[:, r, 0:P], xs[:, r, :], s.ident[:, :]).then_inc(turned, 1)

        def tile(n, r, first, last=False):
            if not last:
                turn(n + 1, 1 - r)
            pe.wait_ge(xT_ready, n + 1)
            if not first:
                pe.wait_ge(read_act, n - 1)
                pe.wait_ge(read_dve, n - 1)
            nc.tensor.matmul(ps1[:, r, :], xT[:, r, :], wcat[:, 0:512], start=True, stop=True)
            nc.tensor.matmul(ps2[:, r, 0:WC - 512], xT[:, r, :], wcat[:, 512:WC], start=True, stop=True).then_inc(projected, 1)

        turn(0, 0)
        for r in range(2):
            tile(r, r, True)
        with pe.Fori(1, NT // 2 - 1) as pair:
            for r in range(2):
                tile(pair * 2 + r, r, False)
        for r in range(2):
            tile(NT - 2 + r, r, False, r == 1)

    @block.scalar
    def _(act):
        def take(n, r):
            act.wait_ge(turned, n + 1)
            nc.scalar.activation(xT[:, r, :], psT[:, r, 0:P], ACT.Copy).then_inc(xT_ready, 1)

        take(0, 0)
        def tile(n, r, last=False):
            if not last:
                take(n + 1, 1 - r)
            act.wait_ge(projected, n + 1)
            one = bass.ds(n, 1)
            nc.scalar.activation(flat(s.xi[:, one, :]), ps1[:, r, 0:DI], ACT.Copy)
            nc.scalar.activation(flat(s.zp[:, one, :]), ps1[:, r, DI:2 * DI], ACT.Copy).then_inc(read_act, 1)

        with act.Fori(0, NT // 2 - 1) as pair:
            for r in range(2):
                tile(pair * 2 + r, r)
        for r in range(2):
            tile(NT - 2 + r, r, r == 1)

def flat(ap):
    return ap.rearrange("p a e -> p (a e)")

TWO_PI = 2.0 * float(np.pi)
C1 = 6.28125
C2 = float(np.array([np.float32(TWO_PI - C1).view(np.uint32) & 0xFFFFF000], np.uint32).view(np.float32)[0])
C3 = float(TWO_PI - C1 - C2)
ROUND = 1.5 * 2.0 ** 23
PI_IN = 3.1415925


def phase_steps(nc, d, s):
    with ExitStack() as ctx:
        k = Scope(nc, ctx, "t")
        W = TQ * DI
        ab, ex, lg, lg2, u1, mm, dt, shift = (k.sb(n, [P, W]) for n in ("ab", "ex", "lg", "lg2", "u1", "mm", "dt", "shift"))
        lnd = k.sb("lnd", [P, 2, W])
        res = k.sb("res", [P, 2, W])
        lparts = k.sb("lparts", [P, 2, 3, W], BF16)
        hparts = k.sb("hparts", [P, 2, 3, W], BF16)
        zero = k.sb("zero", [P, DI], BF16)
        xs = k.sb("xs", [P, TQ, D])
        idx = k.sb("idx", [P, TQ, 2, 1], U32)
        (dv, exp_ready, log_ready, clamped, log2_ready, lnd_ready, hdx_ready, high_ready, rest_ready,
         mid_ready, low_ready, slot_free, stored, zeroed, kept, brought, passed) = k.sems(
            "dv exp_ready log_ready clamped log2_ready lnd_ready hdx_ready high_ready rest_ready "
            "mid_ready low_ready slot_free stored zeroed kept brought passed")
        sent = k.sems("sent0 sent1 sent2 sent3")
        block = ctx.enter_context(nc.Block())
        per_b = 6

        def rows(ap, b):
            return flat(ap[:, bass.ds(b * TQ, TQ), :])

        @block.sync
        def _(sp):
            sp.wait_ge(zeroed, 1)
            for h in range(2):
                sp.dma_start(d["hdp"][h, :, :, 0, :].rearrange("c f e -> (c f) e"), zero[0:24, :]).then_inc(stored, 16)
            sp.dma_start(d["z"].rearrange("b (q p) e -> p (b q) e", p=P), s.zp[:, :, :]).then_inc(kept, 16)
            with sp.Fori(0, 2) as h:
                for f in range(4):
                    r = f % 2
                    sp.wait_ge(hdx_ready, h * 4 + f + 1)
                    sp.dma_start(d["hdx"][bass.ds(h * 4 + f, 1)].rearrange("a (q p) e -> p (a q) e", p=P),
                                 s.xi[:, bass.ds((h * 4 + f) * TQ, TQ), :]).then_inc(kept, 16)
                    sp.wait_ge(low_ready, (h * 4 + f) * 2 + 2)
                    for c in range(3):
                        sp.dma_start(d["lnp"][bass.ds(h, 1), c, f].rearrange("h (q p) e -> p (h q) e", p=P),
                                     lparts[:, r, c, :].rearrange("p (q e) -> p q e", e=DI)).then_inc(stored, 16)
                    for c, part in enumerate((0, 1, 2, 0, 1, 0)):
                        sp.dma_start(d["hdp"][bass.ds(h, 1), c, f, 1:, :].rearrange("h (q p) e -> p (h q) e", p=P),
                                     hparts[:, r, part, :].rearrange("p (q e) -> p q e", e=DI)).then_inc(stored, 16)
                    sp.wait_ge(stored, (h * 4 + f) * 144 + 176)
                    sp.sem_inc(slot_free, 1)
            sp.wait_ge(stored, 16 * (2 + 9 * B))
            sp.wait_ge(kept, 16 * (1 + B))

        @block.vector
        def _(dve):
            def lower(b, r):
                for i, parts in enumerate((hparts, lparts)):
                    dve.wait_ge(mid_ready, b * 2 + i + 1)
                    nc.vector.tensor_tensor(parts[:, r, 2, :], res[:, i, :], parts[:, r, 1, :], ALU.subtract).then_inc(low_ready, 1)

            def sequence(b, r):
                step = Tally(dve, dv, b * per_b)
                pre = rows(s.pre, b)
                if at_least(b, 1):
                    dve.wait_ge(lnd_ready, b)
                step.mark(nc.vector.scalar_tensor_tensor(ab[:, :], pre, -1.0, pre, ALU.mult, ALU.max))
                step.mark(nc.vector.tensor_scalar(shift[:, :], pre, LOG_TINY, 0.0, ALU.add, ALU.min))
                dve.wait_ge(exp_ready, b + 1)
                step(nc.vector.tensor_scalar(u1[:, :], ex[:, :], 1.0, -1.0, ALU.add, ALU.add))
                step(nc.vector.tensor_tensor(u1[:, :], ex[:, :], u1[:, :], ALU.subtract))
                dve.wait_ge(log_ready, b + 1)
                step(nc.vector.tensor_tensor(u1[:, :], lg[:, :], u1[:, :], ALU.add))
                step(nc.vector.scalar_tensor_tensor(dt[:, :], pre, 0.0, u1[:, :], ALU.max, ALU.add))
                assert step.n == per_b
                nc.vector.tensor_scalar(mm[:, :], dt[:, :], TINY, None, ALU.max).then_inc(clamped, 1)
                xi = rows(s.xi, b)
                nc.vector.scalar_tensor_tensor(xi, dt[:, :], 0.5, xi, ALU.mult, ALU.mult).then_inc(hdx_ready, 1)
                if at_least(b, 1):
                    lower(b - 1, 1 - r)
                dve.wait_ge(log2_ready, b + 1)
                if at_least(b, 1):
                    dve.wait_ge(low_ready, b * 2)
                nc.vector.tensor_tensor(lnd[:, r, :], lg2[:, :], shift[:, :], ALU.add).then_inc(lnd_ready, 1)

            for r in range(2):
                sequence(r, r)
            with dve.Fori(1, B // 2) as pair:
                for r in range(2):
                    sequence(pair * 2 + r, r)
            lower(B - 1, 1)

        @block.scalar
        def _(act):
            def sequence(b, r):
                act.wait_ge(dv, b * per_b + 1)
                nc.scalar.activation(ex[:, :], ab[:, :], ACT.Exp, scale=-1.0).then_inc(exp_ready, 1)
                act.wait_ge(exp_ready, b + 1)
                nc.scalar.activation(lg[:, :], ex[:, :], ACT.Ln, bias=1.0).then_inc(log_ready, 1)
                if at_least(b, 1):
                    middle(b - 1, 1 - r)
                act.wait_ge(clamped, b + 1)
                nc.scalar.activation(lg2[:, :], mm[:, :], ACT.Ln).then_inc(log2_ready, 1)
                act.wait_ge(slot_free, b + 1)
                act.wait_ge(hdx_ready, b + 1)
                nc.scalar.activation(hparts[:, r, 0, :], rows(s.xi, b), ACT.Copy).then_inc(high_ready, 1)
                act.wait_ge(lnd_ready, b + 1)
                nc.scalar.activation(lparts[:, r, 0, :], lnd[:, r, :], ACT.Copy).then_inc(high_ready, 1)

            def middle(b, r):
                for i, parts in enumerate((hparts, lparts)):
                    act.wait_ge(rest_ready, b * 2 + i + 1)
                    nc.scalar.activation(parts[:, r, 1, :], res[:, i, :], ACT.Copy).then_inc(mid_ready, 1)

            act.sem_inc(slot_free, 2)
            for r in range(2):
                sequence(r, r)
            with act.Fori(1, B // 2) as pair:
                for r in range(2):
                    sequence(pair * 2 + r, r)
            middle(B - 1, 1)

        @block.gpsimd
        def _(pool):
            nc.gpsimd.memset(zero[:, :], 0.0).then_inc(zeroed, 1)

            def send(b, q):
                tile = bass.ds(b * TQ + q, 1)
                if at_least(b, 1):
                    pool.wait_ge(sent[q], b * 32)
                nc.gpsimd.tensor_copy(idx[:, q, :, :].rearrange("p c a -> p (c a)"), flat(s.place[:, tile, :])).then_inc(brought, 1)
                nc.gpsimd.tensor_tensor(xs[:, q:q + 1, :], s.xc[:, tile, :], over(s.rstd[:, tile], D), ALU.mult).then_inc(brought, 1)
                pool.wait_ge(brought, b * 8 + (2 * q + 2))
                pool.sem_inc(passed, 1)
                for c in range(2):
                    nc.gpsimd.indirect_dma_start(
                        out=d["xin"], out_offset=bass.IndirectOffsetOnAxis(ap=idx[:, q, c, :], axis=0),
                        in_=xs[:, q, :], in_offset=None, bounds_check=SLOTS - 1, oob_is_err=False).then_inc(sent[q], 16)

            def sequence(b, r):
                whole = (rows(s.xi, b), lnd[:, r, :])
                if at_least(b, 1):
                    pool.wait_ge(low_ready, b * 2)
                for i, parts in enumerate((hparts, lparts)):
                    pool.wait_ge(high_ready, b * 2 + i + 1)
                    nc.gpsimd.tensor_tensor(res[:, i, :], whole[i], parts[:, r, 0, :], ALU.subtract).then_inc(rest_ready, 1)
                for q in range(TQ):
                    send(b, q)

            for r in range(2):
                sequence(r, r)
            with pool.Fori(1, B // 2) as pair:
                for r in range(2):
                    sequence(pair * 2 + r, r)
            for q in range(TQ):
                pool.wait_ge(sent[q], B * 32)


def split3(nc, dve, step, x, parts, rest):
    step(nc.vector.tensor_copy(parts[0], x))
    step(nc.vector.tensor_tensor(rest, x, parts[0], ALU.subtract))
    step(nc.vector.tensor_copy(parts[1], rest))
    step(nc.vector.tensor_tensor(parts[2], rest, parts[1], ALU.subtract))


def phase_angles(nc, d, s, ctx, block):
    k = Scope(nc, ctx, "w")
    freq, freq_col, sign_col = k.sb("freq", [P, HALF]), k.sb("freq_col", [P, 1]), k.sb("sign_col", [P, 1])
    steps, steps_row = k.sb("steps", [P, TQ]), k.sb("steps_row", [P, L])
    angle, angle_c = k.sb("angle", [P, TQ, HALF]), k.sb("angle_c", [P, L])
    turns = k.sb("turns", [P, 2, L])
    loaded, own, angles_ready, sines_ready = k.sems("loaded own angles_ready sines_ready")

    @block.sync
    def _(sp):
        for dst, name in ((freq[:, :], "freq"), (freq_col[:, :], "freq_col"), (sign_col[:, :], "sign_col"),
                          (steps[:, :], "steps"), (steps_row[:, :], "steps_row")):
            sp.dma_start(dst, d[name]).then_inc(loaded, 16)

    @block.gpsimd
    def _(pool):
        g = nc.gpsimd
        step = Tally(pool, own)
        pool.wait_ge(loaded, 80)
        step(g.tensor_tensor(angle[:, :, :], over(steps[:, :], HALF), freq[:, :].unsqueeze(1).to_broadcast([P, TQ, HALF]), ALU.mult))
        step(g.tensor_scalar(angle_c[:, :], steps_row[:, :], freq_col[:, 0:1], None, ALU.mult))

        def reduce(ang, out, n, quarter):
            turn, whole = turns[:, 0, 0:n], turns[:, 1, 0:n]
            step(g.tensor_scalar(turn, ang, 1.0 / TWO_PI, 0.25 * quarter, ALU.mult, ALU.add))
            step(g.tensor_scalar(turn, turn, ROUND, -ROUND, ALU.add, ALU.add))
            for part, start in ((C1, ang), (C2, out), (C3, out)):
                step(g.tensor_scalar(whole, turn, -part, None, ALU.mult))
                step(g.tensor_tensor(out, start, whole, ALU.add))
            step(g.tensor_scalar(out, out, quarter * TWO_PI / 4, PI_IN, ALU.add, ALU.min))
            step(g.tensor_scalar(out, out, -PI_IN, None, ALU.max))

        small = flat(angle[:, :, :])
        reduce(small, flat(s.cos_t[:, :, :]), TQ * HALF, 1)
        reduce(small, flat(s.sin_t[:, :, :]), TQ * HALF, 0)
        reduce(angle_c[:, :], s.cos_c[:, :], L, 1)
        reduce(angle_c[:, :], s.sin_c[:, :], L, 0)
        pool.sem_inc(angles_ready, 1)
        pool.wait_ge(sines_ready, 1)
        step(g.tensor_scalar(s.sin_c[:, :], s.sin_c[:, :], sign_col[:, 0:1], None, ALU.mult))

    @block.scalar
    def _(act):
        act.wait_ge(angles_ready, 1)
        nc.scalar.activation(s.cos_t[:, :, :], s.cos_t[:, :, :], ACT.Sin)
        nc.scalar.activation(s.sin_t[:, :, :], s.sin_t[:, :, :], ACT.Sin)
        nc.scalar.activation(s.cos_c[:, :], s.cos_c[:, :], ACT.Sin)
        nc.scalar.activation(s.sin_c[:, :], s.sin_c[:, :], ACT.Sin).then_inc(sines_ready, 1)


def phase_rotation(nc, d, s, ctx, block):
    k = Scope(nc, ctx, "r")
    turned_b, turned_c = (k.sb(n, [P, TQ, B, NS]) for n in ("turned_b", "turned_c"))
    prod = k.sb("prod", [P, TQ, B, HALF])
    plain_b = k.sb("plain_b", [P, TQ, B, NS])
    cb = k.sb("cb", [P, TQ, B, NS])
    rest = k.sb("rest", [P, TQ, B, NS])
    parts = k.sb("parts", [P, 3, TQ, B, NS], BF16)
    stack = k.sb("stack", [P, 2, TQ, B, 6, NS], BF16)
    zero = k.sb("zero", [P, 6 * NS], BF16)
    alog = k.sb("alog", [3 * NS, DI])
    alog_rest = k.sb("alog_rest", [3 * NS, DI])
    alog_parts = k.sb("alog_parts", [3 * NS, 3, DI], BF16)
    psT = k.ps("psT", [P, 2, L])
    loaded, dv, turned_ready, columns_ready, stacked, stored, alog_split = k.sems(
        "loaded dv turned_ready columns_ready stacked stored alog_split")

    @block.sync
    def _(sp):
        sp.dma_start(alog[:, :], d["alog"]).then_inc(loaded, 16)

    @block.gpsimd
    def _(pool):
        pool.wait_ge(alog_split, 1)
        for c in range(3):
            lo, hi = c * NS, (c + 1) * NS
            src = alog_parts[lo:hi, c, :].unsqueeze(1).to_broadcast([NS, 2 * CH * 2, DI])
            pool.dma_start(s.marg[lo:hi, :, :, :, :].rearrange("r a u h e -> r (a u h) e"), src).then_inc(stored, 16)
        for wiped in (s.mv[:, :, :, :, :], s.st[:, :, :, :], s.zeros[:, :, :]):
            nc.gpsimd.memset(wiped, 0.0)
        for term in range(2):
            pool.wait_ge(stacked, term + 1)
            for b in range(B):
                dst = d["st0"][b, 1:] if term == 0 else d["st1"][b]
                pool.dma_start(dst.rearrange("(q p) e -> p q e", p=P),
                             stack[:, term, :, b, :, :].rearrange("p q c n -> p q (c n)")).then_inc(stored, 16)
        pool.dma_start(d["st0"][:, 0, :], zero[0:B, :]).then_inc(stored, 16)
        pool.wait_ge(stored, 16 * (2 * B + 4))

    @block.vector
    def _(dve):
        step = Tally(dve, dv)
        step.mark(nc.vector.memset(zero[:, :], 0.0))
        dve.wait_ge(loaded, 16)
        pieces = [alog_parts[:, c, :] for c in range(3)]
        split3(nc, dve, step, alog[:, :], pieces, alog_rest[:, :])
        nc.vector.engine_nop().then_inc(alog_split, 1)
        view = s.bcr[:, :, :].rearrange("p (b q) n -> p q b n", q=TQ)
        full = [P, TQ, B, HALF]

        def turn(src, dst, back):
            re, im = src[:, :, :, 0:HALF], src[:, :, :, HALF:NS]
            cos = s.cos_t[:, :, :].unsqueeze(2).to_broadcast(full)
            sin = s.sin_t[:, :, :].unsqueeze(2).to_broadcast(full)
            for a, b, lo, op in ((re, im, 0, ALU.add if back else ALU.subtract),
                                 (im, re, HALF, ALU.subtract if back else ALU.add)):
                out = dst[:, :, :, lo:lo + HALF]
                for q in range(TQ):
                    step.mark(nc.vector.tensor_tensor(out[:, q], a[:, q], cos[:, q], ALU.mult))
                    step(nc.vector.tensor_tensor(prod[:, q], b[:, q], sin[:, q], ALU.mult))
                step(nc.vector.tensor_tensor(out, out, prod[:, :, :, :], op))

        turn(view[:, :, :, 0:NS], turned_b, False)
        turn(view[:, :, :, NS:2 * NS], turned_c, True)
        nc.vector.engine_nop().then_inc(turned_ready, 1)
        step(nc.vector.tensor_copy(plain_b[:, :, :, :], view[:, :, :, 0:NS]))
        step(nc.vector.tensor_tensor(cb[:, :, :, :], turned_c[:, :, :, :], plain_b[:, :, :, :], ALU.mult))
        step(nc.vector.tensor_reduce(s.kappa[:, :, :], cb[:, :, :, :], AX.X, ALU.add))
        for term, src in enumerate((turned_b, plain_b)):
            m = "p q b n -> p (q b) n"
            p3 = [parts[:, c, :, :, :].rearrange(m) for c in range(3)]
            split3(nc, dve, step, src[:, :, :, :].rearrange(m), p3, rest[:, :, :, :].rearrange(m))
            st = stack[:, term, :, :, :, :].rearrange("p q b c n -> p (q b) c n")
            for lo, hi, c in ((0, 3, 0), (3, 5, 1), (5, 6, 2)):
                step(nc.vector.tensor_copy(st[:, :, lo:hi, :],
                                           p3[c].unsqueeze(2).to_broadcast([P, TQ * B, hi - lo, NS])))
            nc.vector.engine_nop().then_inc(stacked, 1)
        dve.wait_ge(columns_ready, 2)
        for h in range(2):
            step.mark(nc.vector.tensor_copy(s.c_col[:, h, :], psT[:, h, :]))

    def columns(pe):
        pe.wait_ge(turned_ready, 1)
        for h in range(2):
            for q in range(TQ):
                last = nc.tensor.transpose(psT[:, h, q * P:(q + 1) * P],
                                           turned_c[:, q, 4 * h:4 * h + 4, :].rearrange("p f n -> p (f n)"), s.ident[:, :])
            last.then_inc(columns_ready, 1)

    return columns

AHEAD = 2


def phase_scan(nc, d, s):
    with ExitStack() as ctx:
        k = Scope(nc, ctx, "c")
        sel = k.sb("sel", [108, P], BF16)
        sel_f = k.sb("sel_f", [108, P])
        eye_j = k.sb("eye_j", [P, 2, P])
        mask4 = k.sb("mask4", [P, 4])
        got = k.sb("got", [P, 2, D])
        idx = k.sb("idx", [P, 2, 1], U32)
        half_ln2 = k.sb("half_ln2", [P, 1])
        mv, st, zeros = s.mv, s.st, s.zeros
        rot = k.sb("rot", [P, 2, 8, P])
        tmp = k.sb("tmp", [P, 8, P])
        cy = k.sb("cy", [P, 2, 8, 2, 32])
        a = k.sb("a", [P, 4, 512])
        aq = k.sb("aq", [P, 4, 512])
        yb = k.sb("yb", [P, 2, CH, P])
        args = k.ps("args", [P, 2, 512])
        q = k.ps("q", [P, 2, 2, 512])
        ys = k.ps("ys", [P, 2, 4, P])
        (loaded, picked, dv, arg_loaded0, arg_loaded1, mv_loaded0, mv_loaded1, arg_ready, mv_used, decay_ready, q_ready, aq_ready, rot_ready,
         y_ready, y_banks, y_stored0, y_stored1, pl, filled, brought, passed, arrived, mix, mixed) = k.sems(
            "loaded picked dv arg_loaded0 arg_loaded1 mv_loaded0 mv_loaded1 arg_ready mv_used decay_ready q_ready aq_ready rot_ready "
            "y_ready y_banks y_stored0 y_stored1 pl filled brought passed arrived mix mixed")
        arg_loaded, mv_loaded = (arg_loaded0, arg_loaded1), (mv_loaded0, mv_loaded1)
        y_stored = (y_stored0, y_stored1)
        block = ctx.enter_context(nc.Block())
        y_out = d["y"].rearrange("(h f) l (g e) -> h g f l e", h=2, g=2)
        n_arg, n_mv = 2, 4 + 16

        @block.sync
        def _(sp):
            sp.dma_start(sel_f[:, :], d["sel"]).then_inc(loaded, 16)
            sp.dma_start(eye_j[:, :, :], d["eye_j"]).then_inc(loaded, 16)
            sp.dma_start(mask4[:, :], d["mask4"]).then_inc(loaded, 16)

            def load(c, slot):
                u0 = c * CH
                for h in range(2):
                    sp.dma_start(s.marg[96:108, slot, :, h, :],
                                 d["lnp"][h, :, :, bass.ds(u0, CH), :].rearrange("c f u e -> (c f) u e")).then_inc(arg_loaded[slot], 16)
                for h in range(2):
                    for term in range(2):
                        lo = h * 48 + term * 24
                        sp.dma_start(mv[lo:lo + 24, slot, :, h, :],
                                     d["hdp"][h, :, :, bass.ds(u0 + term, CH), :].rearrange("c f u e -> (c f) u e")).then_inc(mv_loaded[slot], 16)
                        src = d["st0"] if term == 0 else d["st1"]
                        for f in range(4):
                            sp.dma_start(st[lo + f:lo + 24:4, slot, :, f * NS:(f + 1) * NS],
                                         src[h * 4 + f, bass.ds(u0, CH), :].rearrange("u (c n) -> c u n", n=NS)).then_inc(mv_loaded[slot], 16)

            def store(c, slot):
                sp.wait_ge(y_banks, (c + 1) * (CH // 4) + 2)
                for j in range(4):
                    h, g = divmod(j, 2)
                    sp.dma_start(y_out[h, g, :, bass.ds(c * CH, CH), :], yb[32 * j:32 * j + 4, slot, :, :]).then_inc(y_stored[slot], 16)

            for slot in range(2):
                load(slot, slot)
            wiped = d["rows1"].rearrange("(n p j) e -> n p j e", p=P, j=FILL)
            sp.dma_start(wiped[0], zeros[:, :, :]).then_inc(filled, 16)
            with sp.Fori(0, NB - 1) as i:
                sp.dma_start(wiped[bass.ds(i + 1, 1)].rearrange("a p j e -> (a p) j e"), zeros[:, :, :]).then_inc(filled, 16)
                for slot in range(2):
                    c = i * 2 + slot
                    sp.wait_ge(arg_ready, (c + 1) * CH)
                    sp.wait_ge(mv_used, c + 1)
                    load(c + 2, slot)
                    store(c, slot)
            for slot in range(2):
                store(2 * NB - 2 + slot, slot)
                sp.wait_ge(y_stored[slot], (NB + 1) * 64)
            sp.wait_ge(filled, NB * 16)

        @block.tensor
        def _(pe):
            pe.wait_ge(picked, 1)

            def argument(i, j):
                slot, u = j // CH % 2, j % CH
                if u == 0:
                    pe.wait_ge(arg_loaded[slot], (i + j // BODY + 1) * 16 * n_arg)
                nc.tensor.matmul(args[:, j % 2, :], sel[:, :], flat(s.marg[:, slot, u]), start=True, stop=True).then_inc(arg_ready, 1)

            def inputs(i, j, only=False):
                slot, u = j // CH % 2, j % CH
                if u == 0:
                    pe.wait_ge(mv_loaded[slot], (i + j // BODY + 1) * 16 * n_mv)
                for h in range(2):
                    ins = nc.tensor.matmul(q[:, j % 2, h, 0:DI], st[:, slot, u, :], mv[:, slot, u, h, :], start=True, stop=only)
                if u == CH - 1:
                    ins.then_inc(mv_used, 1)
                return ins

            def body(i, last):
                for j in range(BODY):
                    end = last and j == BODY - 1
                    if j % 8 == 0:
                        pe.wait_ge(rot_ready, i * (BODY // 8) + j // 8 + 1)
                    slot, v = j // 8 % 2, j % 8
                    for h in range(2):
                        cols = slice(h * DI, (h + 1) * DI)
                        pe.wait_ge(aq_ready, i * (2 * BODY) + 2 * j + h + 1)
                        if not end:
                            nc.tensor.matmul(q[:, (j + 1) % 2, h, 0:DI], rot[:, slot, v, :], aq[:, j % 4, cols],
                                             start=False, stop=True).then_inc(q_ready, 1)
                    if j % 4 == 0:
                        pe.wait_ge(y_banks, i * (BODY // 4) + j // 4 + 1)
                    for g in range(4):
                        ins = nc.tensor.matmul(ys[32 * g:32 * g + 32, j // 4 % 2, j % 4, :], cy[:, slot, v, g // 2, :],
                                               aq[:, j % 4, g * P:(g + 1) * P], start=True, stop=True)
                    if j % 4 == 3:
                        ins.then_inc(y_ready, 1)
                    if not (last and j >= BODY - AHEAD):
                        argument(i, j + AHEAD)
                    if not (last and j >= BODY - 2):
                        ins = inputs(i, j + 2)

            for j in range(AHEAD):
                argument(0, j)
            inputs(0, 0, only=True).then_inc(q_ready, 2)
            inputs(0, 1)
            with pe.Fori(0, NB - 1) as i:
                body(i, False)
            body(NB - 1, True)

        @block.vector
        def _(dve):
            step = Tally(dve, dv)
            step.mark(nc.vector.memset(half_ln2[:, :], LN2 / 2))
            dve.wait_ge(loaded, 48)
            nc.vector.tensor_copy(sel[:, :], sel_f[:, :]).then_inc(picked, 1)
            with dve.Fori(0, NB) as i:
                for j in range(BODY):
                    dve.wait_ge(decay_ready, i * BODY + j + 1)
                    for h in range(2):
                        cols = slice(h * DI, (h + 1) * DI)
                        dve.wait_ge(q_ready, i * (2 * BODY) + 2 * j + h + 1)
                        nc.vector.tensor_tensor(aq[:, j % 4, cols], q[:, j % 2, h, 0:DI], a[:, j % 4, cols],
                                                ALU.mult).then_inc(aq_ready, 1)

        @block.scalar
        def _(act):
            act.sem_inc(y_banks, 2)
            act.sem_inc(y_stored0, 64)
            act.sem_inc(y_stored1, 64)
            act.wait_ge(picked, 1)

            def decay(i, m):
                act.wait_ge(arg_ready, i * BODY + m + 1)
                nc.scalar.activation(a[:, m % 4, :], args[:, m % 2, :], ACT.Tanh, bias=half_ln2[:, 0:1],
                                     scale=-0.5).then_inc(decay_ready, 1)

            def copy_out(i, n):
                slot = n * 4 // CH
                if n * 4 % CH == 0:
                    act.wait_ge(y_stored[slot], (i + 1) * 64)
                act.wait_ge(y_ready, i * (BODY // 4) + n + 1)
                u = n * 4 % CH
                nc.scalar.activation(yb[:, slot, u:u + 4, :], ys[:, n % 2, :, :], ACT.Copy).then_inc(y_banks, 1)

            def body(i, last):
                for m in range(BODY):
                    if not (last and m >= BODY - AHEAD):
                        decay(i, m + AHEAD)
                    if m % 4 == 3:
                        copy_out(i, m // 4)

            decay(0, 0)
            decay(0, 1)
            with act.Fori(0, NB - 1) as i:
                body(i, False)
            body(NB - 1, True)

        @block.gpsimd
        def _(pool):
            own = Tally(pool, pl)
            own(nc.gpsimd.memset(cy[:, :, :, :, :], 0.0))
            pool.wait_ge(loaded, 48)

            def build(g, slot, base):
                own = Tally(pool, pl, base)
                t = bass.ds(g * 8, 8)
                wide = [P, 8, P]
                own.mark(nc.gpsimd.tensor_tensor(rot[:, slot, :, :], eye_j[:, 0, :].unsqueeze(1).to_broadcast(wide),
                                                 over(s.cos_c[:, t], P), ALU.mult))
                own(nc.gpsimd.tensor_tensor(tmp[:, :, :], eye_j[:, 1, :].unsqueeze(1).to_broadcast(wide),
                                            over(s.sin_c[:, t], P), ALU.mult))
                own(nc.gpsimd.tensor_tensor(rot[:, slot, :, :], rot[:, slot, :, :], tmp[:, :, :], ALU.add))
                for h in range(2):
                    ins = nc.gpsimd.tensor_tensor(cy[:, slot, :, h, 0:4], mask4[:, :].unsqueeze(1).to_broadcast([P, 8, 4]),
                                                  over(s.c_col[:, h, t], 4), ALU.mult)
                ins.then_inc(rot_ready, 1)

            def fetch(t):
                nc.gpsimd.tensor_copy(idx[:, :, :].rearrange("p c a -> p (c a)"), flat(s.fetch[:, bass.ds(t, 1), :])).then_inc(brought, 1)
                pool.wait_ge(brought, t + 1)
                pool.sem_inc(passed, 1)
                for c in range(2):
                    nc.gpsimd.indirect_dma_start(
                        out=got[:, c, :], out_offset=None, in_=d["eout"],
                        in_offset=bass.IndirectOffsetOnAxis(ap=idx[:, c, :], axis=0)).then_inc(arrived, 16)

            def combine(t):
                own = Tally(pool, mix, t * 2)
                one = bass.ds(t, 1)
                pool.wait_ge(arrived, t * 32 + 32)
                own.mark(nc.gpsimd.tensor_tensor(s.g0[:, one, :], got[:, 0:1, :], over(s.gate[:, one, 0], D), ALU.mult))
                own(nc.gpsimd.tensor_tensor(got[:, 1:2, :], got[:, 1:2, :], over(s.gate[:, one, 1], D), ALU.mult))
                pool.sem_inc(passed, 1)
                nc.gpsimd.tensor_tensor(s.g0[:, one, :], s.g0[:, one, :], got[:, 1:2, :], ALU.add).then_inc(mixed, 1)

            def tile_apart(t):
                fetch(t)
                combine(t)

            build(0, 0, 1)
            build(1, 1, 4)
            tile_apart(0)
            with pool.Fori(0, L // 16 - 1) as i:
                pool.wait_ge(mixed, i + 1)
                fetch(i + 1)
                for slot in range(2):
                    g = i * 2 + slot
                    pool.wait_ge(y_ready, g * 2 + 2)
                    build(g + 2, slot, g * 3 + 7)
                combine(i + 1)

SLOTS = G0 * E0 * C0
SKIP = 8192.0


def phase_route0(nc, d, s):
    with ExitStack() as ctx:
        k = Scope(nc, ctx, "g")
        W = NT * E0
        logits = s.bcr[:, :, 2 * NS:2 * NS + E0]
        prob, hit, cand, number = (k.sb(n, [P, NT, E0]) for n in ("prob", "hit", "cand", "number"))
        best, first = k.sb("best", [P, 2, NT]), k.sb("first", [P, NT])
        total, inv = k.sb("total", [P, NT]), k.sb("inv", [P, NT])
        pick = k.sb("pick", [P, NT, 2, E0])
        pick_b = k.sb("pick_b", [P, NT, 2, E0], BF16)
        tri_f, tri = k.sb("tri_f", [P, P]), k.sb("tri", [P, P], BF16)
        ones = k.sb("ones", [P, P], BF16)
        count = k.sb("count", [P, NT, 2, E0])
        pos = k.sb("pos", [P, NT, 2, E0])
        offset = k.sb("offset", [P, NT, 2, E0])
        rank, slot, kept, lost = (k.sb(n, [P, NT, 2]) for n in ("rank", "slot", "kept", "lost"))
        zeros = k.sb("zeros", [P, SLOTS // P, D])
        psC = k.ps("psC", [P, NT, 2, E0])
        psS = k.ps("psS", [P, NT, 2, E0])
        loaded, dv, shifted, raised, picked, counted, cleared, filled = k.sems("loaded dv shifted raised picked counted cleared filled")
        block = ctx.enter_context(nc.Block())

        @block.sync
        def _(sp):
            sp.dma_start(tri_f[:, :], d["tri"]).then_inc(loaded, 16)
            sp.dma_start(number[:, :, :], d["number"]).then_inc(loaded, 16)
            sp.dma_start(offset[:, :, :, :], d["offset"]).then_inc(loaded, 16)
            sp.wait_ge(cleared, 1)
            sp.dma_start(d["xin"].rearrange("(p j) e -> p j e", p=P), zeros[:, :, :]).then_inc(filled, 16)
            sp.wait_ge(filled, 16)

        @block.vector
        def _(dve):
            v = nc.vector
            step = Tally(dve, dv)
            v.memset(zeros[:, :, :], 0.0).then_inc(cleared, 1)
            step.mark(v.memset(ones[:, :], 1.0))
            dve.wait_ge(loaded, 48)
            step.mark(v.tensor_copy(tri[:, :], tri_f[:, :]))
            step(v.tensor_reduce(first[:, :], logits, AX.X, ALU.max))
            v.tensor_tensor(prob[:, :, :], logits, over(first[:, :], E0), ALU.subtract).then_inc(shifted, 1)
            dve.wait_ge(raised, 1)
            step(v.tensor_reduce(total[:, :], prob[:, :, :], AX.X, ALU.add))
            step(v.reciprocal(inv[:, :], total[:, :]))
            step(v.tensor_tensor(prob[:, :, :], prob[:, :, :], over(inv[:, :], E0), ALU.mult))
            for c in range(2):
                one = pick[:, :, c, :]
                step(v.tensor_reduce(best[:, c, :], prob[:, :, :], AX.X, ALU.max))
                step(v.tensor_tensor(hit[:, :, :], prob[:, :, :], over(best[:, c, :], E0), ALU.is_lt))
                step(v.scalar_tensor_tensor(cand[:, :, :], hit[:, :, :], float(E0), number[:, :, :], ALU.mult, ALU.add))
                step(v.tensor_reduce(first[:, :], cand[:, :, :], AX.X, ALU.min))
                step(v.tensor_tensor(one, number[:, :, :], over(first[:, :], E0), ALU.is_equal))
                if c == 0:
                    step(v.scalar_tensor_tensor(prob[:, :, :], one, -2.0, prob[:, :, :], ALU.mult, ALU.add))
            v.tensor_copy(pick_b[:, :, :, :], pick[:, :, :, :]).then_inc(picked, 1)
            dve.wait_ge(counted, 1)
            per_group = NT // G0
            tiles = [ap[:, :, :, :].rearrange("p (g t) c e -> p t g (c e)", g=G0) for ap in (count, psS)]
            step(v.memset(tiles[0][:, 0], 0.0))
            for t in range(1, per_group):
                step(v.tensor_tensor(tiles[0][:, t], tiles[0][:, t - 1], tiles[1][:, t - 1], ALU.add))
            step(v.tensor_tensor(pos[:, :, :, :], count[:, :, :, :], psC[:, :, :, :], ALU.add))
            for g in range(G0):
                last = (g + 1) * per_group - 1
                step(v.tensor_tensor(hit[:, 0, :], count[:, last, 0, :], psS[:, last, 0, :], ALU.add))
                sec = pos[:, g * per_group:(g + 1) * per_group, 1, :]
                step(v.tensor_tensor(sec, sec, hit[:, 0, :].unsqueeze(1).to_broadcast([P, per_group, E0]), ALU.add))
            step(v.tensor_scalar(pos[:, :, :, :], pos[:, :, :, :], -1.0, None, ALU.add))
            step(v.tensor_tensor(count[:, :, :, :], pos[:, :, :, :], pick[:, :, :, :], ALU.mult))
            step(v.tensor_reduce(rank[:, :, :], count[:, :, :, :], AX.X, ALU.add))
            step(v.tensor_tensor(pos[:, :, :, :], pos[:, :, :, :], offset[:, :, :, :], ALU.add))
            step(v.tensor_tensor(count[:, :, :, :], pos[:, :, :, :], pick[:, :, :, :], ALU.mult))
            step(v.tensor_reduce(slot[:, :, :], count[:, :, :, :], AX.X, ALU.add))
            step(v.tensor_scalar(kept[:, :, :], rank[:, :, :], float(C0), None, ALU.is_lt))
            step(v.tensor_scalar(lost[:, :, :], kept[:, :, :], -SKIP, SKIP, ALU.mult, ALU.add))
            step(v.tensor_tensor(lost[:, :, :], lost[:, :, :], slot[:, :, :], ALU.add))
            step(v.tensor_copy(s.place[:, :, :], lost[:, :, :]))
            step(v.tensor_tensor(slot[:, :, :], slot[:, :, :], kept[:, :, :], ALU.mult))
            step(v.tensor_copy(s.fetch[:, :, :], slot[:, :, :]))
            step(v.tensor_tensor(s.gate[:, :, :], kept[:, :, :], best[:, :, :].rearrange("p c t -> p t c"), ALU.mult))

        @block.scalar
        def _(act):
            act.wait_ge(shifted, 1)
            nc.scalar.activation(prob[:, :, :], prob[:, :, :], ACT.Exp).then_inc(raised, 1)
            nc.scalar.activation(s.zp[:, :, :], s.zp[:, :, :], ACT.Silu).then_inc(raised, 1)

        @block.tensor
        def _(pe):
            pe.wait_ge(picked, 1)
            rhs = pick_b[:, :, :, :].rearrange("p t c e -> p (t c e)")
            nc.tensor.matmul(psC[:, :, :, :].rearrange("p t c e -> p (t c e)"), tri[:, :], rhs, start=True, stop=True)
            nc.tensor.matmul(psS[:, :, :, :].rearrange("p t c e -> p (t c e)"), ones[:, :], rhs, start=True, stop=True).then_inc(counted, 1)


def phase_experts0(nc, d, s, ctx, block):
    k = Scope(nc, ctx, "e")
    FC = F0 // P
    R = G0 * C0
    x = k.sb("x", [C0, 2, G0, D])
    wi = k.sb("wi", [P, 2, F0])
    wo = k.sb("wo", [P, 2, FC, D])
    xT = k.sb("xT", [P, 2, R])
    hT = k.sb("hT", [P, 2, FC, R])
    o = k.sb("o", [C0, 2, G0, D])
    psX = k.ps("psX", [P, 1, 512])
    psH = k.ps("psH", [P, 4, 512])
    psO = k.ps("psO", [P, G0, 2 * D])
    ld0, ld1, turned, xT_ready, hid, h_ready, outed, o_ready, st0, st1 = k.sems("ld0 ld1 turned xT_ready hid h_ready outed o_ready st0 st1")
    ld, st = (ld0, ld1), (st0, st1)
    rows_in = d["xin"].rearrange("(g e c) h -> e c g h", g=G0, e=E0)
    rows_out = d["eout"].rearrange("(g e c) h -> e c g h", g=G0, e=E0)
    wo_v = d["wo"].rearrange("e (f p) h -> e p f h", p=P)

    @block.sync
    def _(sp):
        def load(e, r):
            one = bass.ds(e, 1)
            sp.dma_start(x[:, r, :, :], rows_in[one].rearrange("a c g h -> c (a g) h")).then_inc(ld[r], 16)
            sp.dma_start(wi[:, r, :], d["wi"][one].rearrange("a h f -> h (a f)")).then_inc(ld[r], 16)
            sp.dma_start(wo[:, r, :, :], wo_v[one].rearrange("a p f h -> p (a f) h")).then_inc(ld[r], 16)

        def store(e, r):
            sp.wait_ge(o_ready, e + 1)
            sp.dma_start(rows_out[bass.ds(e, 1)].rearrange("a c g h -> c (a g) h"), o[:, r, :, :]).then_inc(st[r], 16)

        for r in range(2):
            sp.sem_inc(st[r], 16)
            load(r, r)
        with sp.Fori(0, E0 // 2 - 1) as i:
            for r in range(2):
                store(i * 2 + r, r)
                load(i * 2 + r + 2, r)
        for r in range(2):
            store(E0 - 2 + r, r)
            sp.wait_ge(st[r], E0 // 2 * 16 + 16)

    @block.tensor
    def _(pe):
        def expert(i, r):
            e = i * 2 + r
            pe.wait_ge(ld[r], (i + 1) * 48)
            for g in range(G0):
                ins = nc.tensor.transpose(psX[:, 0, g * C0:(g + 1) * C0], x[:, r, g, :], s.ident[0:C0, 0:C0])
            ins.then_inc(turned, 1)
            pe.wait_ge(xT_ready, e + 1)
            if at_least(e, 1):
                pe.wait_ge(h_ready, e * FC)
            for f in range(FC):
                nc.tensor.matmul(psH[:, f, 0:R], wi[:, r, f * P:(f + 1) * P], xT[:, r, :], start=True, stop=True).then_inc(hid, 1)
            pe.wait_ge(h_ready, e * FC + FC)
            if at_least(e, 1):
                pe.wait_ge(o_ready, e)
            for g in range(G0):
                for f in range(FC):
                    ins = nc.tensor.matmul(psO[0:C0, g, 0:D], hT[:, r, f, g * C0:(g + 1) * C0], wo[:, r, f, :],
                                           start=f == 0, stop=f == FC - 1)
            ins.then_inc(outed, 1)

        for r in range(2):
            expert(0, r)
        with pe.Fori(1, E0 // 2) as i:
            for r in range(2):
                expert(i, r)

    @block.scalar
    def _(act):
        with act.Fori(0, E0 // 2) as i:
            for r in range(2):
                e = i * 2 + r
                act.wait_ge(turned, e + 1)
                nc.scalar.activation(xT[:, r, :], psX[:, 0, 0:R], ACT.Copy).then_inc(xT_ready, 1)
                for f in range(FC):
                    act.wait_ge(hid, e * FC + f + 1)
                    nc.scalar.activation(hT[:, r, f, :], psH[:, f, 0:R], ACT.Relu).then_inc(h_ready, 1)
                act.wait_ge(st[r], i * 16 + 16)
                act.wait_ge(outed, e + 1)
                nc.scalar.activation(o[:, r, :, :], psO[0:C0, :, 0:D], ACT.Copy).then_inc(o_ready, 1)

NH, DK = 16, 8
HG = 4
UN = B * NH // HG
KR = 9 * DK
NEG = -1e30
INV_SQRT_DK = float(1.0 / np.sqrt(np.float32(DK)))


def phase_output0(nc, d, s):
    RING = 4
    with ExitStack() as ctx:
        k = Scope(nc, ctx, "o")
        lnw, lnb = k.sb("lnw", [P, DI]), k.sb("lnb", [P, DI])
        wout = k.sb("wout", [P, 2, D])
        y, hd, z = (k.sb(n, [P, RING, TQ, DI]) for n in ("y", "hd", "z"))
        x = k.sb("x", [P, 4, TQ, D])
        sq = k.sb("sq", [P, 2, TQ, DI])
        mean, var, std, inv = (k.sb(n, [P, 2, TQ]) for n in ("mean", "var", "std", "inv"))
        yT = k.sb("yT", [P, 2, TQ, P])
        sg = k.sb("sg", [P, TQ, D])
        psT = k.ps("psT", [P, 2, 2, TQ, P])
        psO = k.ps("psO", [P, 2, TQ, D])
        (loaded, dv, centred, squared, var_ready, std_ready, scaled, shifted, turned, yT_ready, outed, x_ready, stored, activated) = k.sems(
            "loaded dv centred squared var_ready std_ready scaled shifted turned yT_ready outed x_ready stored activated")
        arrived = k.sems("in0 in1 in2 in3")
        x_arrived = k.sems("x0 x1 x2 x3")
        block = ctx.enter_context(nc.Block())

        @block.sync
        def _(sp):
            sp.dma_start(lnw[:, :], d["ln_w"]).then_inc(loaded, 16)
            sp.dma_start(lnb[:, :], d["ln_b"]).then_inc(loaded, 16)
            sp.dma_start(wout[:, :, :], d["wout"].rearrange("(c p) o -> p c o", p=P)).then_inc(loaded, 16)
            for b in range(B):
                if b >= RING:
                    sp.wait_ge(turned, (b - RING + 1) * 2)
                for dst, name in ((y, "y"), (hd, "hdx"), (z, "z")):
                    sp.dma_start(dst[:, b % RING, :, :], d[name][b].rearrange("(q p) e -> p q e", p=P)).then_inc(arrived[b % RING], 16)
                if b >= 4:
                    sp.wait_ge(x_ready, b - 3)
                sp.dma_start(x[:, b % 4, :, :], d["x"][b].rearrange("(q p) e -> p q e", p=P)).then_inc(x_arrived[b % 4], 16)
            for b in range(B):
                sp.wait_ge(x_ready, b + 1)
                sp.dma_start(d["x1"][b].rearrange("(q p) e -> p q e", p=P), s.xc[:, b * TQ:(b + 1) * TQ, :]).then_inc(stored, 16)
            sp.wait_ge(stored, 16 * B)

        @block.vector
        def _(dve):
            v = nc.vector
            step = Tally(dve, dv)

            def centre(b):
                r, f = b % RING, b % 2
                yb = y[:, r]
                dve.wait_ge(arrived[r], (b // RING + 1) * 48)
                for q in range(TQ):
                    step.mark(v.scalar_tensor_tensor(yb[:, q, :], hd[:, r, q, :], s.kappa[:, q, b:b + 1], yb[:, q, :], ALU.mult, ALU.add))
                step.settle()
                step(v.tensor_tensor(yb, yb, z[:, r], ALU.mult))
                step(v.tensor_reduce(mean[:, f, :], yb, AX.X, ALU.add))
                step(v.tensor_scalar(mean[:, f, :], mean[:, f, :], 1.0 / DI, None, ALU.mult))
                v.tensor_tensor(yb, yb, over(mean[:, f, :], DI), ALU.subtract).then_inc(centred, 1)

            def scale(b):
                r, f = b % RING, b % 2
                dve.wait_ge(squared, b + 1)
                step(v.tensor_reduce(var[:, f, :], sq[:, f], AX.X, ALU.add))
                v.tensor_scalar(var[:, f, :], var[:, f, :], 1.0 / DI, None, ALU.mult).then_inc(var_ready, 1)
                dve.wait_ge(std_ready, b + 1)
                step(v.reciprocal(inv[:, f, :], std[:, f, :]))
                v.tensor_tensor(y[:, r], y[:, r], over(inv[:, f, :], DI), ALU.mult).then_inc(scaled, 1)

            def add(b):
                dve.wait_ge(outed, b + 1)
                rows = slice(b * TQ, (b + 1) * TQ)
                if b == 0:
                    dve.wait_ge(activated, 1)
                else:
                    dve.wait_ge(x_ready, b)
                step(v.tensor_tensor(sg[:, :, :], psO[:, b % 2, :, :], s.g0[:, rows, :], ALU.mult))
                dve.wait_ge(x_arrived[b % 4], (b // 4 + 1) * 16)
                v.tensor_tensor(s.xc[:, rows, :], sg[:, :, :], x[:, b % 4, :, :], ALU.add).then_inc(x_ready, 1)

            dve.wait_ge(loaded, 48)
            for b in range(B + 3):
                if b < B:
                    centre(b)
                if 1 <= b <= B:
                    scale(b - 1)
                if b >= 3:
                    add(b - 3)

        @block.gpsimd
        def _(pool):
            pool.wait_ge(loaded, 48)
            wide = [P, TQ, DI]
            for b in range(B):
                r = b % RING
                pool.wait_ge(scaled, b + 1)
                nc.gpsimd.tensor_tensor(z[:, r], y[:, r], lnw[:, :].unsqueeze(1).to_broadcast(wide), ALU.mult).then_inc(shifted, 1)
                pool.wait_ge(shifted, b * 2 + 1)
                nc.gpsimd.tensor_tensor(hd[:, r], z[:, r], lnb[:, :].unsqueeze(1).to_broadcast(wide), ALU.add).then_inc(shifted, 1)

        @block.tensor
        def _(pe):
            pe.wait_ge(loaded, 48)
            for b in range(B):
                r = b % 2
                pe.wait_ge(shifted, b * 2 + 2)
                for c in range(2):
                    for q in range(TQ):
                        ins = nc.tensor.transpose(psT[:, r, c, q, :], hd[:, b % RING, q, c * P:(c + 1) * P], s.ident[:, :])
                    ins.then_inc(turned, 1)
                pe.wait_ge(yT_ready, b * 2 + 2)
                if b >= 2:
                    pe.wait_ge(x_ready, b - 1)
                for q in range(TQ):
                    for c in range(2):
                        ins = nc.tensor.matmul(psO[:, r, q, :], yT[:, c, q, :], wout[:, c, :], start=c == 0, stop=c == 1)
                ins.then_inc(outed, 1)

        @block.scalar
        def _(act):
            def square(b):
                act.wait_ge(centred, b + 1)
                nc.scalar.activation(sq[:, b % 2], y[:, b % RING], ACT.Square).then_inc(squared, 1)

            nc.scalar.activation(s.g0[:, :, :], s.g0[:, :, :], ACT.Silu).then_inc(activated, 1)
            def take(b):
                for c in range(2):
                    act.wait_ge(turned, b * 2 + c + 1)
                    if b >= 1:
                        act.wait_ge(outed, b)
                    nc.scalar.activation(yT[:, c, :, :], psT[:, b % 2, c, :, :], ACT.Copy).then_inc(yT_ready, 1)

            for b in range(B + 2):
                if b < B:
                    square(b)
                if b >= 2:
                    take(b - 2)
                if 1 <= b <= B:
                    act.wait_ge(var_ready, b)
                    nc.scalar.activation(std[:, (b - 1) % 2, :], var[:, (b - 1) % 2, :], ACT.Sqrt, bias=s.eps[:, 0:1]).then_inc(std_ready, 1)


PER_PAIR = 2 * (4 + 2 + K1 * 7 - 1)


def phase_qkv(nc, d, s):
    with ExitStack() as ctx:
        k = Scope(nc, ctx, "q")
        w = k.sb("w", [P, 5, D])
        cos, sin = k.sb("cos", [P, L]), k.sb("sin", [P, L])
        xs = k.sb("xs", [P, 2, TQ, D])
        xT = k.sb("xT", [P, 2, L])
        prod = k.sb("prod", [P, 2, L])
        qk = k.sb("qk", [P, 2, 2, L])
        rest = k.sb("rest", [P, 2, 2, L])
        parts = k.sb("parts", [P, 2, 2, 3, L], BF16)
        sel_w = k.sb("sel_w", [P, 2 * E1])
        sel, low_no = (k.sb(n, [P, 2, TQ, E1]) for n in ("sel", "low_no"))
        best, first = k.sb("best", [P, 2, TQ]), k.sb("first", [P, 2, TQ])
        psL = k.ps("psL", [P, TQ, 2 * E1])
        psT = k.ps("psT", [P, 2, TQ, P])
        psP = k.ps("psP", [P, 4, L])
        psV = k.ps("psV", [P, TQ, D])
        (loaded, dv, xs_ready, turned, xT_ready, projected, v_projected, v_copied, qk_ready, high, rested, mid, low, slot_free, out0, out1, scored, raised) = k.sems(
            "loaded dv xs_ready turned xT_ready projected v_projected v_copied qk_ready high rested mid low slot_free out0 out1 scored raised")
        out = (out0, out1)
        block = ctx.enter_context(nc.Block())

        @block.sync
        def _(sp):
            sp.dma_start(w[:, :, :], d["w_qkv"]).then_inc(loaded, 16)
            sp.dma_start(cos[:, :], d["rope_cos"]).then_inc(loaded, 16)
            sp.dma_start(sin[:, :], d["rope_sin"]).then_inc(loaded, 16)
            sp.dma_start(sel_w[:, :], d["sel_w"]).then_inc(loaded, 16)
            sp.dma_start(s.number[:, :], d["number1"]).then_inc(loaded, 16)
            with sp.Fori(0, B // 2) as n:
                for r in range(2):
                    b = n * 2 + r
                    sp.wait_ge(low, b * 2 + 2)
                    for i in range(3):
                        for m, rows in ((0, slice(3 * i, 3 * i + 3)), (1, slice(i, 9, 3))):
                            src = parts[:, r, m, i, :].unsqueeze(1).to_broadcast([P, 3, L])
                            sp.dma_start(d["qk9"][m, bass.ds(b, 1), rows].rearrange("a c k h t -> (a k h) c t"), src).then_inc(out[r], 16)
                    sp.wait_ge(out[r], (n + 1) * 96)
                    sp.sem_inc(slot_free, 1)

        @block.vector
        def _(dve):
            v = nc.vector
            dve.wait_ge(loaded, 80)

            def bring(b, r):
                if at_least(b, 2):
                    dve.wait_ge(turned, b - 1)
                v.tensor_copy(xs[:, r, :, :], s.xc[:, bass.ds(b * TQ, TQ), :]).then_inc(xs_ready, 1)

            def rotate(b, r, step):
                if at_least(b, 2):
                    dve.wait_ge(low, b * 2 - 2)
                for m in range(2):
                    dve.wait_ge(projected, b * 2 + m + 1)
                    if at_least(b, 1):
                        dve.wait_ge(qk_ready, b * 2 + m - 1)
                    step.mark(v.tensor_tensor(qk[:, r, m, :], psP[:, 2 * m, :], cos[:, :], ALU.mult))
                    step(v.tensor_tensor(prod[:, m, :], psP[:, 2 * m + 1, :], sin[:, :], ALU.mult))
                    v.tensor_tensor(qk[:, r, m, :], qk[:, r, m, :], prod[:, m, :], ALU.add).then_inc(qk_ready, 1)
                if not isinstance(b, int) or b + 2 < B:
                    bring(b + 2, r)

            def choose(i, step):
                dve.wait_ge(raised, i * 2 + 2)
                rows = [bass.ds((i * 2 + r) * TQ, TQ) for r in range(2)]
                number = s.number[:, :].unsqueeze(1).to_broadcast([P, TQ, E1])
                for r in range(2):
                    step.alternate(v.tensor_scalar(low_no[:, r], sel[:, r], 1.0, None, ALU.add))
                for r in range(2):
                    step.alternate(v.reciprocal(sel[:, r], low_no[:, r]))
                for c in range(K1):
                    for r in range(2):
                        step.alternate(v.tensor_reduce(best[:, r, :], sel[:, r], AX.X, ALU.max))
                    for r in range(2):
                        step.alternate(v.tensor_copy(s.chosen[:, rows[r], c], best[:, r, :]))
                    for r in range(2):
                        step.alternate(v.tensor_tensor(low_no[:, r], sel[:, r], over(best[:, r, :], E1), ALU.is_lt))
                    for r in range(2):
                        step.alternate(v.scalar_tensor_tensor(low_no[:, r], low_no[:, r], float(E1), number, ALU.mult, ALU.add))
                    for r in range(2):
                        step.alternate(v.tensor_reduce(first[:, r, :], low_no[:, r], AX.X, ALU.min))
                    for r in range(2):
                        step.alternate(v.tensor_tensor(s.one[:, c, rows[r], :], number, over(first[:, r, :], E1), ALU.is_equal))
                    if c < K1 - 1:
                        for r in range(2):
                            step.alternate(v.scalar_tensor_tensor(sel[:, r], s.one[:, c, rows[r], :], -2.0, sel[:, r], ALU.mult, ALU.add))
                assert step.n == PER_PAIR

            def pair(i):
                step = Tally(dve, dv, i * PER_PAIR)
                for r in range(2):
                    rotate(i * 2 + r, r, step)
                choose(i, step)

            for r in range(2):
                bring(r, r)
            pair(0)
            with dve.Fori(1, HB - 1) as i:
                pair(i)
            pair(HB - 1)

        @block.tensor
        def _(pe):
            pe.wait_ge(loaded, 80)

            def turn(b, r):
                pe.wait_ge(xs_ready, b + 1)
                if at_least(b, 2):
                    pe.wait_ge(xT_ready, b - 1)
                for q in range(TQ):
                    ins = nc.tensor.transpose(psT[:, r, q, :], xs[:, r, q, :], s.ident[:, :])
                ins.then_inc(turned, 1)

            def project(b, r):
                pe.wait_ge(xT_ready, b + 1)
                if at_least(b, 1):
                    pe.wait_ge(raised, b)
                for q in range(TQ):
                    ins = nc.tensor.matmul(psL[:, q, :], xT[:, r, q * P:(q + 1) * P], sel_w[:, :], start=True, stop=True)
                ins.then_inc(scored, 1)
                for m in range(2):
                    if at_least(b, 1):
                        pe.wait_ge(qk_ready, b * 2 - 1 + m)
                    for n in range(2):
                        ins = nc.tensor.matmul(psP[:, 2 * m + n, :], w[:, 2 * m + n, :], xT[:, r, :], start=True, stop=True)
                    ins.then_inc(projected, 1)
                if at_least(b, 1):
                    pe.wait_ge(v_copied, b)
                for q in range(TQ):
                    ins = nc.tensor.matmul(psV[:, q, :], xT[:, r, q * P:(q + 1) * P], w[:, 4, :], start=True, stop=True)
                ins.then_inc(v_projected, 1)

            turn(0, 0)
            for r in range(2):
                turn(r + 1, 1 - r)
                project(r, r)
            with pe.Fori(1, HB - 1) as i:
                for r in range(2):
                    turn(i * 2 + r + 1, 1 - r)
                    project(i * 2 + r, r)
            turn(B - 1, 1)
            project(B - 2, 0)
            project(B - 1, 1)

        @block.scalar
        def _(act):
            def take(b, r):
                act.wait_ge(turned, b + 1)
                if at_least(b, 2):
                    act.wait_ge(v_projected, b - 1)
                nc.scalar.activation(xT[:, r, :], psT[:, r, :, :].rearrange("p q t -> p (q t)"), ACT.Copy).then_inc(xT_ready, 1)

            def parts_of(i, r):
                b = i * 2 + r
                act.wait_ge(scored, b + 1)
                if at_least(b, 2):
                    act.wait_ge(dv, i * PER_PAIR)
                nc.scalar.activation(sel[:, r], psL[:, :, 0:E1], ACT.Exp, scale=-1.0).then_inc(raised, 1)
                if at_least(b, 2):
                    act.wait_ge(slot_free, b - 1)
                for m in range(2):
                    act.wait_ge(qk_ready, b * 2 + m + 1)
                    nc.scalar.activation(parts[:, r, m, 0, :], qk[:, r, m, :], ACT.Copy).then_inc(high, 1)
                act.wait_ge(v_projected, b + 1)
                nc.scalar.activation(s.v[:, bass.ds(b * TQ, TQ), :], psV[:, :, :], ACT.Copy).then_inc(v_copied, 1)
                for m in range(2):
                    act.wait_ge(rested, b * 2 + m + 1)
                    nc.scalar.activation(parts[:, r, m, 1, :], rest[:, r, m, :], ACT.Copy).then_inc(mid, 1)

            take(0, 0)
            for r in range(2):
                take(r + 1, 1 - r)
                parts_of(0, r)
            with act.Fori(1, HB - 1) as i:
                for r in range(2):
                    take(i * 2 + r + 1, 1 - r)
                    parts_of(i, r)
            take(B - 1, 1)
            parts_of(HB - 1, 0)
            parts_of(HB - 1, 1)

        @block.gpsimd
        def _(pool):
            def lower(b, r):
                if at_least(b, 2):
                    pool.wait_ge(low, b * 2 - 2)
                for m in range(2):
                    pool.wait_ge(high, b * 2 + m + 1)
                    nc.gpsimd.tensor_tensor(rest[:, r, m, :], qk[:, r, m, :], parts[:, r, m, 0, :], ALU.subtract).then_inc(rested, 1)
                for m in range(2):
                    pool.wait_ge(mid, b * 2 + m + 1)
                    nc.gpsimd.tensor_tensor(parts[:, r, m, 2, :], rest[:, r, m, :], parts[:, r, m, 1, :], ALU.subtract).then_inc(low, 1)

            for r in range(2):
                lower(r, r)
            with pool.Fori(1, HB) as i:
                for r in range(2):
                    lower(i * 2 + r, r)

GROUPS = [(0, h, 1) for h in range(HG)] + [(1, h, 1) for h in range(HG)] + [(2, 0, 2), (2, 2, 2)] + [(3, 0, HG)]
NG = len(GROUPS)
ENDS = [4, 8, 10, 11]
HB = B // 2


def phase_attention(nc, d, s):
    with ExitStack() as ctx:
        k = Scope(nc, ctx, "a")
        q = k.sb("q", [KR + 1, 4, HG, L], BF16)
        key = k.sb("key", [KR + 1, 4, HG, L], BF16)
        mask_f, mask = k.sb("mask_f", [P, 2, P]), k.sb("mask", [P, 2, P], BF16)
        eye = k.sb("eye", [P, P], BF16)
        minus = k.sb("minus", [4 * HG, L], BF16)
        top = k.sb("top", [P, 2, HG, TQ])
        top_row = k.sb("top_row", [HG * TQ, 2, P], BF16)
        pt = k.sb("pt", [P, 2, HG, L])
        vaug = k.sb("vaug", [P, 2, TQ, HG, 32])
        ot = k.sb("ot", [P, 2, L])
        inv = k.sb("inv", [P, TQ, HG])
        xs = k.sb("xs", [P, 2, D])
        idx = k.sb("idx", [P, 2, K1, 1], U32)
        psA = k.ps("psA", [P, 2, 512])
        psB = k.ps("psB", [P, 2, 512])
        psO = k.ps("psO", [P, 512])
        psT = k.ps("psT", [P, TQ, HG, 32])
        psM = k.ps("psM", [P, 512])
        (loaded, dv, consts, minus_ready, minus_in, ld0, ld1, ld2, ld3, mr0, mr1, mr2, mr3, scored, maxed, top_turned, top_ready, rev_scored, raised, v_ready, summed,
         o_copied, o_turned, o_ready, wiped, sent0, sent1, brought, passed) = k.sems(
            "loaded dv consts minus_ready minus_in ld0 ld1 ld2 ld3 mr0 mr1 mr2 mr3 scored maxed top_turned top_ready rev_scored raised v_ready summed "
            "o_copied o_turned o_ready wiped sent0 sent1 brought passed")
        sent = (sent0, sent1)
        ld, row_in = (ld0, ld1, ld2, ld3), (mr0, mr1, mr2, mr3)
        block = ctx.enter_context(nc.Block())

        def run(eng, unit, finish):
            for hg in range(4):
                unit(0, hg, True, False)
            with eng.Fori(1, B - 1) as i:
                for hg in range(4):
                    unit(i, hg, False, False)
            for hg in range(4):
                unit(B - 1, hg, False, True)
            finish()

        @block.sync
        def _(sp):
            sp.dma_start(mask_f[:, :, :], d["mask"]).then_inc(loaded, 16)

            def load(i, hg):
                for m, dst in ((0, q), (1, key)):
                    sp.dma_start(dst[0:KR, hg, :, :], d["qk9"][m, bass.ds(i, 1), :, :, hg * HG:(hg + 1) * HG].rearrange("a c k h t -> (a c k) h t")).then_inc(ld[hg], 16)

            def row(n, hg):
                sp.wait_ge(top_ready, n + 1)
                sp.dma_start(q[KR:KR + 1, hg, :, :], top_row[:, (hg % 2), :]).then_inc(row_in[hg], 16)

            def unit(i, hg, first, last):
                if not (first and hg == 0) and not (last and hg == 3):
                    row(i * 4 + hg + 1, (hg + 1) % 4)
                if not last:
                    sp.wait_ge(rev_scored, (i * 4 + hg + 1) * NG)
                    load(i + 1, hg)

            for hg in range(4):
                load(0, hg)
            sp.wait_ge(minus_ready, 1)
            sp.dma_start(key[KR:KR + 1, :, :, :], minus[:, :]).then_inc(minus_in, 16)
            for n in range(2):
                row(n, n)
            run(sp, unit, lambda: None)

        def max_groups(g):
            far, h0, hn = GROUPS[g]
            return TQ - 1 - far, h0, hn, (TQ - far) * P

        @block.tensor
        def _(pe):
            pe.wait_ge(consts, 1)

            def scores(n, slot, g):
                qt, h0, hn, w = max_groups(g)
                bank = (slot * NG + g) % 2
                if at_least(n * NG + g, 2):
                    pe.wait_ge(maxed, n * NG + g - 1)
                for j in range(hn):
                    h, lo = h0 + j, j * w
                    nc.tensor.matmul(psA[:, bank, lo:lo + w], q[0:KR, slot, h, qt * P:(qt + 1) * P], key[0:KR, slot, h, 0:w], start=True, stop=False)
                    ins = nc.tensor.matmul(psA[:, bank, lo + w - P:lo + w], eye[:, :], mask[:, 0, :], start=False, stop=True)
                ins.then_inc(scored, 1)

            def reversed_scores(n, slot, g):
                kt, h0, hn = GROUPS[g]
                w = (TQ - kt) * P
                bank = (slot * NG + g) % 2
                if at_least(n * NG + g, 2):
                    pe.wait_ge(raised, n * NG + g - 1)
                for j in range(hn):
                    h, lo = h0 + j, j * w
                    nc.tensor.matmul(psB[:, bank, lo:lo + w], key[:, slot, h, kt * P:(kt + 1) * P], q[:, slot, h, kt * P:L], start=True, stop=False)
                    ins = nc.tensor.matmul(psB[:, bank, lo:lo + P], eye[:, :], mask[:, 1, :], start=False, stop=True)
                ins.then_inc(rev_scored, 1)

            def turn_top(n, r):
                pe.wait_ge(maxed, (n + 1) * NG)
                if at_least(n, 1):
                    pe.wait_ge(top_ready, n)
                nc.tensor.transpose(psM[0:HG * TQ, 0:P], flat(top[:, r, :, :]), s.ident[:, :]).then_inc(top_turned, 1)

            def sum_v(n, slot, kt):
                pe.wait_ge(raised, n * NG + ENDS[kt])
                if kt == 0:
                    pe.wait_ge(v_ready, n + 1)
                    if at_least(n, 1):
                        pe.wait_ge(o_copied, n)
                for h in range(HG):
                    ins = nc.tensor.matmul(psO[32 * h:32 * h + 32, kt * P:L], vaug[:, slot % 2, kt, h, :], pt[:, kt % 2, h, 0:L - kt * P], start=kt == 0, stop=kt == TQ - 1)
                ins.then_inc(summed, 1)

            def turn_o(n, r):
                pe.wait_ge(o_copied, n + 1)
                if at_least(n, 1):
                    pe.wait_ge(o_ready, n)
                for qt in range(TQ):
                    ins = nc.tensor.transpose(flat(psT[:, qt, :, :]), ot[:, r, qt * P:(qt + 1) * P], s.ident[:, :])
                ins.then_inc(o_turned, 1)

            def unit(i, hg, first, last):
                n = i * 4 + hg
                ahead = not (last and hg >= 2)
                for g in range(NG):
                    if g == 0:
                        if ahead:
                            pe.wait_ge(ld[(hg + 2) % 4], (i + 1 + (hg >= 2)) * 32)
                        pe.wait_ge(row_in[hg], (i + 1) * 16)
                    if ahead:
                        scores(n + 2, (hg + 2) % 4, g)
                    reversed_scores(n, hg, g)
                    if g == 2 and not (first and hg == 0) and not (last and hg == 3):
                        turn_top(n + 1, (hg + 1) % 2)
                    if g == 4 and not (first and hg == 0):
                        turn_o(n - 1, (hg + 1) % 2)
                    if g == 5:
                        sum_v(n, hg, 0)
                    if g == 9:
                        sum_v(n, hg, 1)
                sum_v(n, hg, 2)
                sum_v(n, hg, 3)

            for n in range(2):
                pe.wait_ge(ld[n], 32)
                for g in range(NG):
                    scores(n, n, g)
            for n in range(2):
                turn_top(n, n)
            pe.wait_ge(minus_in, 16)
            run(pe, unit, lambda: turn_o(UN - 1, 1))

        @block.vector
        def _(dve):
            v = nc.vector
            step = Tally(dve, dv)
            nc.vector.memset(minus[:, :], -1.0).then_inc(minus_ready, 1)
            dve.wait_ge(loaded, 16)
            step.mark(v.tensor_copy(mask[:, :, :], mask_f[:, :, :]))
            v.tensor_copy(eye[:, :], s.ident[:, :]).then_inc(consts, 1)

            def maxima(n, slot, g):
                qt, h0, hn, w = max_groups(g)
                dve.wait_ge(scored, n * NG + g + 1)
                if g == 0 and at_least(n, 2):
                    dve.wait_ge(top_turned, n - 1)
                v.tensor_reduce(top[:, slot % 2, h0:h0 + hn, qt], psA[:, (slot * NG + g) % 2, 0:hn * w].rearrange("p (h w) -> p h w", w=w),
                                AX.X, ALU.max).then_inc(maxed, 1)

            def copy_top(i, n, hg):
                dve.wait_ge(top_turned, n + 1)
                before = (hg + 2) % 4
                if at_least(n, 2):
                    dve.wait_ge(row_in[before], (i if hg < 2 else i + 1) * 16)
                v.tensor_copy(top_row[:, hg % 2, :], psM[0:HG * TQ, 0:P]).then_inc(top_ready, 1)

            def divide(i, n, hg):
                dve.wait_ge(o_turned, n + 1)
                if at_least(n, 1):
                    dve.wait_ge(o_ready, n)
                v.reciprocal(inv[:, :, :], psT[:, :, :, DK]).then_inc(dv, 1)
                dve.wait_ge(dv, n + 2)
                v.tensor_tensor(s.o[:, bass.ds(i * TQ, TQ), hg * 32:hg * 32 + 32].rearrange("p q (h c) -> p q h c", c=DK), psT[:, :, :, 0:DK],
                                inv[:, :, :].unsqueeze(3).to_broadcast([P, TQ, HG, DK]), ALU.mult).then_inc(o_ready, 1)

            def unit(i, hg, first, last):
                n = i * 4 + hg
                for g in range(NG):
                    if not (last and hg >= 2):
                        maxima(n + 2, (hg + 2) % 4, g)
                    if g == 3 and not (first and hg == 0) and not (last and hg == 3):
                        copy_top(i if hg < 3 else i + 1, n + 1, (hg + 1) % 4)
                    if g == 5 and not (first and hg == 0):
                        divide(i if hg else i - 1, n - 1, (hg + 3) % 4)

            for n in range(2):
                for g in range(NG):
                    maxima(n, n, g)
            for n in range(2):
                copy_top(0, n, n)
            run(dve, unit, lambda: divide(B - 1, UN - 1, 3))

        @block.scalar
        def _(act):
            def copy_o(n, r):
                act.wait_ge(summed, (n + 1) * TQ)
                if at_least(n, 2):
                    act.wait_ge(o_turned, n - 1)
                nc.scalar.activation(ot[:, r, :], psO[:, :], ACT.Copy).then_inc(o_copied, 1)

            def unit(i, hg, first, last):
                n = i * 4 + hg
                for g in range(NG):
                    kt, h0, hn = GROUPS[g]
                    w = (TQ - kt) * P
                    act.wait_ge(rev_scored, n * NG + g + 1)
                    if g in (0, 4, 8, 10) and not (first and hg == 0 and kt < 2):
                        act.wait_ge(summed, n * TQ + kt - 1)
                    nc.scalar.activation(pt[:, kt % 2, h0:h0 + hn, 0:w], psB[:, (hg * NG + g) % 2, 0:hn * w].rearrange("p (h w) -> p h w", w=w),
                                         ACT.Exp, scale=INV_SQRT_DK).then_inc(raised, 1)
                    if g == 1 and not (first and hg == 0):
                        copy_o(n - 1, (hg + 1) % 2)

            run(act, unit, lambda: copy_o(UN - 1, 1))

        @block.gpsimd
        def _(pool):
            nc.gpsimd.memset(vaug[:, :, :, :, :], 0.0).then_inc(wiped, 1)
            pool.wait_ge(wiped, 1)
            nc.gpsimd.memset(vaug[:, :, :, :, DK:DK + 1], 1.0).then_inc(wiped, 1)
            pool.wait_ge(wiped, 2)

            def send(i, hg, first):
                n, r = i * 4 + hg, hg % 2
                if not (first and hg < 2):
                    pool.wait_ge(sent[r], i * (2 * K1 * 16) + hg // 2 * (K1 * 16))
                nc.gpsimd.tensor_copy(idx[:, r, :, :].rearrange("p c a -> p (c a)"), flat(s.place[:, bass.ds(n, 1), :])).then_inc(brought, 1)
                nc.gpsimd.tensor_copy(xs[:, r, :], flat(s.xc[:, bass.ds(n, 1), :])).then_inc(brought, 1)
                pool.wait_ge(brought, n * 2 + 2)
                pool.sem_inc(passed, 1)
                for c in range(K1):
                    nc.gpsimd.indirect_dma_start(
                        out=d["rows1"], out_offset=bass.IndirectOffsetOnAxis(ap=idx[:, r, c, :], axis=0),
                        in_=xs[:, r, :], in_offset=None, bounds_check=SLOTS1 - 1, oob_is_err=False).then_inc(sent[r], 16)

            def unit(i, hg, first, last):
                n = i * 4 + hg
                if not (first and hg < 2):
                    pool.wait_ge(summed, (n - 1) * TQ)
                nc.gpsimd.tensor_copy(vaug[:, hg % 2, :, :, 0:DK], s.v[:, bass.ds(i * TQ, TQ), hg * 32:hg * 32 + 32].rearrange("p q (h c) -> p q h c", c=DK)).then_inc(v_ready, 1)
                send(i, hg, first)

            run(pool, unit, lambda: None)
            for r in range(2):
                pool.wait_ge(sent[r], NT // 2 * K1 * 16)


def phase_attention_out(nc, d, s):
    with ExitStack() as ctx:
        k = Scope(nc, ctx, "ao")
        w = k.sb("w", [P, D])
        oT = k.sb("oT", [P, 2, TQ, P])
        psT = k.ps("psT", [P, 2, TQ, P])
        psS = k.ps("psS", [P, 2, TQ, D])
        o = k.sb("o", [P, 2, TQ, D])
        loaded, o_ready, turned, oT_ready, projected, copied = k.sems("loaded o_ready turned oT_ready projected copied")
        block = ctx.enter_context(nc.Block())

        @block.sync
        def _(sp):
            sp.dma_start(w[:, :], d["w_o"]).then_inc(loaded, 16)

        @block.tensor
        def _(pe):
            def turn(b, r):
                pe.wait_ge(o_ready, b + 1)
                for q in range(TQ):
                    ins = nc.tensor.transpose(psT[:, r, q, :], o[:, r, q, :], s.ident[:, :])
                ins.then_inc(turned, 1)

            def project(b, r):
                pe.wait_ge(oT_ready, b + 1)
                for q in range(TQ):
                    ins = nc.tensor.matmul(psS[:, r, q, :], oT[:, r, q, :], w[:, :], start=True, stop=True)
                ins.then_inc(projected, 1)

            pe.wait_ge(loaded, 16)
            for r in range(2):
                turn(r, r)
            for r in range(2):
                project(r, r)
                turn(r + 2, r)
            with pe.Fori(1, HB - 1) as i:
                for r in range(2):
                    b = i * 2 + r
                    pe.wait_ge(copied, i * 2)
                    project(b, r)
                    turn(b + 2, r)
            for r in range(2):
                pe.wait_ge(copied, (HB - 1) * 2)
                project(B - 2 + r, r)

        @block.vector
        def _(dve):
            def take(b, r):
                dve.wait_ge(turned, b + 1)
                if at_least(b, 2):
                    dve.wait_ge(projected, b - 1)
                nc.vector.tensor_copy(oT[:, r, :, :], psT[:, r, :, :]).then_inc(oT_ready, 1)

            for r in range(2):
                take(r, r)
            with dve.Fori(1, HB) as i:
                for r in range(2):
                    take(i * 2 + r, r)

        @block.scalar
        def _(act):
            with act.Fori(0, HB) as i:
                for r in range(2):
                    b = i * 2 + r
                    act.wait_ge(projected, b + 1)
                    nc.scalar.activation(s.s1[:, bass.ds(b * TQ, TQ), :], psS[:, r, :, :], ACT.Copy).then_inc(copied, 1)

        @block.gpsimd
        def _(pool):
            def bring(b, r):
                nc.gpsimd.tensor_copy(o[:, r, :, :], s.o[:, bass.ds(b * TQ, TQ), :]).then_inc(o_ready, 1)

            for r in range(2):
                bring(r, r)
            with pool.Fori(0, HB - 1) as i:
                for r in range(2):
                    pool.wait_ge(turned, i * 2 + r + 1)
                    bring(i * 2 + r + 2, r)

def phase_route1(nc, d, s):
    with ExitStack() as ctx:
        k = Scope(nc, ctx, "u")
        tri_f, tri = k.sb("tri_f", [P, P]), k.sb("tri", [P, P], BF16)
        ones = k.sb("ones", [P, P], BF16)
        tile_no = k.sb("tile_no", [P, 2])
        sel, low = (k.sb(n, [P, NT, E1]) for n in ("sel", "low"))
        picks = k.sb("picks", [P, NT, E1], BF16)
        first = k.sb("first", [P, NT])
        tiles, grown = k.sb("tiles", [P, E1]), k.sb("grown", [P, 2, E1])
        done = k.sb("done", [P, 2, E1])
        expert, expert_i = k.sb("expert", [P, 2]), k.sb("expert_i", [P, 2], I32)
        ps = k.ps("ps", [P, 8, 512])
        per_bank = 512 // E1
        loaded, dv, picked, counted, named, written = k.sems("loaded dv picked counted named written")
        block = ctx.enter_context(nc.Block())

        @block.sync
        def _(sp):
            sp.dma_start(tri_f[:, :], d["tri"]).then_inc(loaded, 16)
            sp.dma_start(tile_no[:, :], d["tile_no"]).then_inc(loaded, 16)
            sp.wait_ge(named, 1)
            sp.dma_start(d["expert_of"].rearrange("(p a) -> p a", p=P), expert_i[:, :]).then_inc(written, 16)
            sp.wait_ge(written, 16)
            sp.dma_start(s.tile_expert[:, :], d["expert_of"].rearrange("(o t) -> o t", o=1)).then_inc(written, 16)
            sp.wait_ge(written, 32)

        @block.vector
        def _(dve):
            v = nc.vector
            step = Tally(dve, dv)
            step.mark(v.memset(ones[:, :], 1.0))

            wide = [P, NT, E1]
            one = s.one
            dve.wait_ge(loaded, 32)
            step.mark(v.tensor_copy(tri[:, :], tri_f[:, :]))
            step(v.tensor_tensor(picks[:, :, :], one[:, 0], one[:, 1], ALU.add))
            step(v.tensor_tensor(picks[:, :, :], picks[:, :, :], one[:, 2], ALU.add))
            v.tensor_tensor(picks[:, :, :], picks[:, :, :], one[:, 3], ALU.add).then_inc(picked, 1)
            dve.wait_ge(counted, 1)

            def in_tile(t):
                lo = t % per_bank * E1
                return ps[:, 4 + t // per_bank, lo:lo + E1]

            step(v.memset(low[:, 0, :], 0.0))
            for t in range(1, NT):
                step(v.tensor_tensor(low[:, t, :], low[:, t - 1, :], in_tile(t - 1), ALU.add))
            step(v.tensor_tensor(tiles[:, :], low[:, NT - 1, :], in_tile(NT - 1), ALU.add))
            step(v.tensor_scalar(tiles[:, :], tiles[:, :], 1.0 / P, (P / 2 - 0.5) / P, ALU.mult, ALU.add))
            step(v.tensor_scalar(tiles[:, :], tiles[:, :], ROUND, -ROUND, ALU.add, ALU.add))
            step(v.tensor_copy(grown[:, 0, :], tiles[:, :]))
            at, by = 0, 1
            while by < E1:
                step.mark(v.tensor_copy(grown[:, 1 - at, 0:by], grown[:, at, 0:by]))
                step(v.tensor_tensor(grown[:, 1 - at, by:E1], grown[:, at, by:E1], grown[:, at, 0:E1 - by], ALU.add))
                at, by = 1 - at, by * 2
            end, start = grown[:, at, :], grown[:, 1 - at, :]
            step(v.tensor_tensor(done[:, :, :], end.unsqueeze(1).to_broadcast([P, 2, E1]), over(tile_no[:, :], E1), ALU.is_le))
            step(v.tensor_reduce(expert[:, :], done[:, :, :], AX.X, ALU.add))
            step(v.tensor_scalar(expert[:, :], expert[:, :], float(E1 - 1), None, ALU.min))
            v.tensor_copy(expert_i[:, :], expert[:, :]).then_inc(named, 1)
            step(v.tensor_tensor(start, end, tiles[:, :], ALU.subtract))
            step(v.tensor_scalar(start, start, float(P), -1.0, ALU.mult, ALU.add))
            for n in range(4):
                rows = slice(n * per_bank, (n + 1) * per_bank)
                step.mark(v.tensor_tensor(low[:, rows, :], low[:, rows, :], ps[:, n, :].rearrange("p (t e) -> p t e", e=E1), ALU.add))
            step.settle()
            step(v.tensor_tensor(low[:, :, :], low[:, :, :], start.unsqueeze(1).to_broadcast(wide), ALU.add))
            for c in range(K1):
                step(v.tensor_tensor(sel[:, :, :], low[:, :, :], one[:, c], ALU.mult))
                step(v.tensor_reduce(first[:, :], sel[:, :, :], AX.X, ALU.add))
                step(v.tensor_copy(s.place[:, :, c], first[:, :]))

        @block.tensor
        def _(pe):
            pe.wait_ge(picked, 1)
            flat_picks = flat(picks[:, :, :])
            for n in range(4):
                nc.tensor.matmul(ps[:, n, :], tri[:, :], flat_picks[:, n * 512:(n + 1) * 512], start=True, stop=True)
            for n in range(4):
                ins = nc.tensor.matmul(ps[:, 4 + n, :], ones[:, :], flat_picks[:, n * 512:(n + 1) * 512], start=True, stop=True)
            ins.then_inc(counted, 1)


def phase_experts1(nc, d, s):
    with ExitStack() as ctx:
        k = Scope(nc, ctx, "x")
        x, o = (k.sb(n, [P, 4, 4, D]) for n in ("x", "o"))
        w = k.sb("w", [P, 4, 4, 2 * P])
        xT, hT = (k.sb(n, [P, 2, 4, P]) for n in ("xT", "hT"))
        psX, psH, psO = (k.ps(n, [P, 2, 4, P]) for n in ("psX", "psH", "psO"))
        x_turned, xT_ready, hidden, hT_ready, outed, o_ready = k.sems("x_turned xT_ready hidden hT_ready outed o_ready")
        x_in, w_in, o_out = k.sems("x_in0 x_in1 x_in2 x_in3"), k.sems("w_in0 w_in1 w_in2 w_in3"), k.sems("o_out0 o_out1 o_out2 o_out3")
        block = ctx.enter_context(nc.Block())
        rows_in = d["rows1"].rearrange("(g t p) e -> g p t e", t=4, p=P)
        rows_out = d["rows1o"].rearrange("(g t p) e -> g p t e", t=4, p=P)
        QG = GR // 4

        def run(eng, stage):
            for r in range(4):
                stage(0, r)
            with eng.Fori(1, QG) as i:
                for r in range(4):
                    stage(i, r)

        def weights(eng, g, r, tiles):
            for t in tiles:
                e = eng.value_load(s.tile_expert[0:1, bass.ds(g * 4 + t, 1)], min_val=0, max_val=E1 - 1)
                eng.dma_start(w[:, r, t, :], d["keys_values"][bass.ds(e, 1)].rearrange("a p h -> (a p) h")).then_inc(w_in[r], 16)

        @block.sync
        def _(sp):
            def load(i, r):
                g = i * 4 + r
                if at_least(i, 1):
                    sp.wait_ge(outed, g - 3)
                weights(sp, g, r, (0, 1))

            run(sp, load)

        @block.gpsimd
        def _(pool):
            def load(i, r):
                if at_least(i, 1):
                    pool.wait_ge(x_turned, i * 4 + r - 3)
                pool.dma_start(x[:, r, :, :], rows_in[bass.ds(i * 4 + r, 1)].rearrange("a p t e -> (a p) t e")).then_inc(x_in[r], 16)

            def store(i, r):
                pool.wait_ge(o_ready, i * 4 + r + 1)
                pool.dma_start(rows_out[bass.ds(i * 4 + r, 1)].rearrange("a p t e -> (a p) t e"), o[:, r, :, :]).then_inc(o_out[r], 16)

            for r in range(4):
                load(0, r)
            with pool.Fori(1, QG) as i:
                for r in range(4):
                    load(i, r)
                    store(i - 1, r)
            for r in range(4):
                store(QG - 1, r)
            for r in range(4):
                pool.wait_ge(o_out[r], QG * 16)

        @block.tensor
        def _(pe):
            def turn(i, r):
                g = i * 4 + r
                pe.wait_ge(x_in[r], i * 16 + 16)
                if at_least(g, 2):
                    pe.wait_ge(xT_ready, g - 1)
                for t in range(4):
                    ins = nc.tensor.transpose(psX[:, r % 2, t, :], x[:, r, t, :], s.ident[:, :])
                ins.then_inc(x_turned, 1)

            def first(i, r):
                g = i * 4 + r
                pe.wait_ge(xT_ready, g + 1)
                pe.wait_ge(w_in[r], i * 64 + 64)
                if at_least(g, 2):
                    pe.wait_ge(hT_ready, g - 1)
                for t in range(4):
                    ins = nc.tensor.matmul(psH[:, r % 2, t, :], w[:, r, t, 0:P], xT[:, r % 2, t, :], start=True, stop=True)
                ins.then_inc(hidden, 1)

            def second(i, r):
                g = i * 4 + r
                pe.wait_ge(hT_ready, g + 1)
                if at_least(g, 2):
                    pe.wait_ge(o_ready, g - 1)
                for t in range(4):
                    ins = nc.tensor.matmul(psO[:, r % 2, t, :], hT[:, r % 2, t, :], w[:, r, t, P:2 * P], start=True, stop=True)
                ins.then_inc(outed, 1)

            def stage(i, r):
                if not isinstance(i, int) or i < QG - 1 or r < 3:
                    turn(i + (r + 1) // 4, (r + 1) % 4)
                first(i, r)
                if r or at_least(i, 1):
                    second(i if r else i - 1, (r + 3) % 4)

            turn(0, 0)
            for r in range(4):
                stage(0, r)
            with pe.Fori(1, QG - 1) as i:
                for r in range(4):
                    stage(i, r)
            for r in range(4):
                stage(QG - 1, r)
            second(QG - 1, 3)

        @block.scalar
        def _(act):
            def turned(i, r):
                g = i * 4 + r
                act.wait_ge(x_turned, g + 1)
                if at_least(g, 2):
                    act.wait_ge(hidden, g - 1)
                nc.scalar.activation(xT[:, r % 2, :, :], psX[:, r % 2, :, :], ACT.Copy).then_inc(xT_ready, 1)

            def out(i, r):
                g = i * 4 + r
                act.wait_ge(outed, g + 1)
                if at_least(g, 4):
                    act.wait_ge(o_out[r], i * 16)
                nc.scalar.activation(o[:, r, :, :], psO[:, r % 2, :, :], ACT.Copy).then_inc(o_ready, 1)

            def stage(i, r):
                if not isinstance(i, int) or i < QG - 1 or r < 3:
                    turned(i + (r + 1) // 4, (r + 1) % 4)
                if r or at_least(i, 1):
                    out(i if r else i - 1, (r + 3) % 4)
                    if not isinstance(i, int) or i * 4 + r + 3 < GR:
                        weights(act, i * 4 + r + 3, (r + 3) % 4, (2, 3))

            for r in range(4):
                weights(act, r, r, (2, 3))
            turned(0, 0)
            for r in range(4):
                stage(0, r)
            for r in range(4):
                stage(1, r)
            with act.Fori(2, QG - 1) as i:
                for r in range(4):
                    stage(i, r)
            for r in range(4):
                stage(QG - 1, r)
            out(QG - 1, 3)

        @block.vector
        def _(dve):
            def hide(i, r):
                g = i * 4 + r
                dve.wait_ge(hidden, g + 1)
                if at_least(g, 2):
                    dve.wait_ge(outed, g - 1)
                nc.vector.tensor_scalar(hT[:, r % 2, :, :], psH[:, r % 2, :, :], 0.0, None, ALU.max).then_inc(hT_ready, 1)

            run(dve, hide)


def phase_combine1(nc, d, s):
    with ExitStack() as ctx:
        k = Scope(nc, ctx, "h1")
        x = k.sb("x", [P, NT, D])
        got = k.sb("got", [P, 4, K1, D])
        idx = k.sb("idx", [P, 4, K1, 1], U32)
        acc, g = k.sb("acc", [P, 4, D]), k.sb("g", [P, 4, D])
        idx_ready, passed, dv, summed, gated, x_in, finished, stored = k.sems("idx_ready passed dv summed gated x_in finished stored")
        arrived = k.sems("got0 got1 got2 got3")
        block = ctx.enter_context(nc.Block())
        QT = NT // 4
        per_tile = K1

        @block.sync
        def _(sp):
            sp.dma_start(x[:, :, :], d["x1"].rearrange("b (q p) e -> p (b q) e", p=P)).then_inc(x_in, 16)
            with sp.Fori(0, B) as b:
                sp.wait_ge(finished, b * TQ + TQ)
                sp.dma_start(d["out"][bass.ds(b, 1)].rearrange("a (q p) e -> p (a q) e", p=P), x[:, bass.ds(b * TQ, TQ), :]).then_inc(stored, 16)
            sp.wait_ge(stored, 16 * B)

        @block.vector
        def _(dve):
            def index(i, r):
                nc.vector.tensor_copy(idx[:, r, :, :].rearrange("p c a -> p (c a)"), flat(s.place[:, bass.ds(i * 4 + r, 1), :])).then_inc(idx_ready, 1)

            def combine(i, r):
                t = i * 4 + r
                step = Tally(dve, dv, t * per_tile - (r > 0 or at_least(i, 1)))
                dve.wait_ge(arrived[r], (i + 1) * (16 * K1))
                if at_least(t, 4):
                    dve.wait_ge(gated, t - 3)
                w = flat(s.chosen[:, bass.ds(t, 1), :])
                step(nc.vector.tensor_scalar(acc[:, r, :], got[:, r, 0, :], w[:, 0:1], None, ALU.mult))
                for c in range(1, K1):
                    ins = nc.vector.scalar_tensor_tensor(acc[:, r, :], got[:, r, c, :], w[:, c:c + 1], acc[:, r, :], ALU.mult, ALU.add)
                    if c < K1 - 1:
                        step(ins)
                ins.then_inc(summed, 1)
                if r or at_least(i, 1):
                    finish(i if r else i - 1, (r + 3) % 4, step)

            def finish(i, r, step):
                t = i * 4 + r
                one = bass.ds(t, 1)
                dve.wait_ge(gated, t + 1)
                step(nc.vector.tensor_tensor(g[:, r:r + 1, :], g[:, r:r + 1, :], s.s1[:, one, :], ALU.mult))
                nc.vector.tensor_tensor(x[:, one, :], x[:, one, :], g[:, r:r + 1, :], ALU.add).then_inc(finished, 1)

            dve.wait_ge(x_in, 16)
            for r in range(4):
                index(0, r)
            for r in range(4):
                combine(0, r)
                index(1, r)
            with dve.Fori(1, QT - 1) as i:
                for r in range(4):
                    combine(i, r)
                    index(i + 1, r)
            for r in range(4):
                combine(QT - 1, r)
            finish(QT - 1, 3, Tally(dve, dv, NT * per_tile - 1))

        @block.gpsimd
        def _(pool):
            def fetch(i, r):
                t = i * 4 + r
                pool.wait_ge(idx_ready, t + 1)
                if at_least(t, 4):
                    pool.wait_ge(summed, t - 3)
                    pool.sem_inc(passed, 1)
                for c in range(K1):
                    nc.gpsimd.indirect_dma_start(
                        out=got[:, r, c, :], out_offset=None, in_=d["rows1o"],
                        in_offset=bass.IndirectOffsetOnAxis(ap=idx[:, r, c, :], axis=0)).then_inc(arrived[r], 16)

            for r in range(4):
                fetch(0, r)
            with pool.Fori(1, QT) as i:
                for r in range(4):
                    fetch(i, r)

        @block.scalar
        def _(act):
            def gate(i, r):
                t = i * 4 + r
                act.wait_ge(summed, t + 1)
                if at_least(t, 4):
                    act.wait_ge(finished, t - 3)
                nc.scalar.activation(g[:, r, :], acc[:, r, :], ACT.Silu).then_inc(gated, 1)

            for r in range(4):
                gate(0, r)
            with act.Fori(1, QT) as i:
                for r in range(4):
                    gate(i, r)


class Shared:
    pass


def phase_start(nc, d, s, k):
    loaded, = k.sems("ident_loaded")
    with nc.Block() as block:
        @block.sync
        def _(sp):
            sp.dma_start(s.ident[:, :], d["ident"]).then_inc(loaded, 16)
            sp.wait_ge(loaded, 16)


def program(nc, d):
    def dram(name, shape, dt=F32):
        d[name] = nc.dram_tensor(name, shape, dt).ap()

    dram("lnp", (2, 3, 4, L, DI), BF16)
    dram("hdp", (2, 6, 4, L + 1, DI), BF16)
    dram("st0", (B, L + 1, 6 * NS), BF16)
    dram("st1", (B, L, 6 * NS), BF16)
    dram("y", (B, L, DI))
    dram("hdx", (B, L, DI))
    dram("z", (B, L, DI))
    dram("xin", (SLOTS, D))
    dram("eout", (SLOTS, D))
    dram("x1", (B, L, D))
    dram("qk9", (2, B, 9, DK, NH, L), BF16)
    dram("rows1", (SLOTS1, D))
    dram("rows1o", (SLOTS1, D))
    dram("expert_of", (2 * P,), I32)
    s = Shared()
    Scope.taken = []
    with ExitStack() as whole:
        k = Scope(nc, whole, "s")
        s.ident, s.eps, s.rstd = k.sb("ident", [P, P]), k.sb("eps", [P, 1]), k.sb("rstd", [P, NT])
        s.xc = k.sb("xc", [P, NT, D])
        phase_start(nc, d, s, k)
        with ExitStack() as layer0:
            k0 = Scope(nc, layer0, "s0")
            s.kappa = k0.sb("kappa", [P, TQ, B])
            s.cos_c, s.sin_c = k0.sb("cos_c", [P, L]), k0.sb("sin_c", [P, L])
            s.cos_t, s.sin_t = (k0.sb(n, [P, TQ, HALF]) for n in ("cos_t", "sin_t"))
            s.bcr = k0.sb("bcr", [P, NT, WC - 3 * DI])
            s.place, s.fetch = k0.sb("place", [P, NT, 2], U32), k0.sb("fetch", [P, NT, 2], U32)
            s.gate = k0.sb("gate", [P, NT, 2])
            with ExitStack() as projections:
                k1 = Scope(nc, projections, "s1")
                s.xi, s.pre, s.zp = (k1.sb(n, [P, NT, DI]) for n in ("xi", "pre", "zp"))
                phase_norm(nc, d, s, "n0", d["x"], False)
                with ExitStack() as both, nc.Block() as block:
                    phase_project(nc, d, s, both, block)
                    phase_angles(nc, d, s, both, block)
                phase_route0(nc, d, s)
                phase_steps(nc, d, s)
            s.g0 = k0.sb("g0", [P, NT, D])
            with ExitStack() as recurrence:
                k2 = Scope(nc, recurrence, "s2")
                s.c_col = k2.sb("c_col", [P, 2, L])
                s.marg = k2.sb("marg", [108, 2, CH, 2, DI], BF16)
                s.mv, s.st = k2.sb("mv", [96, 2, CH, 2, DI], BF16), k2.sb("st", [96, 2, CH, P], BF16)
                s.zeros = k2.sb("zeros", [P, FILL, D])
                with ExitStack() as both, nc.Block() as block:
                    columns = phase_rotation(nc, d, s, both, block)
                    phase_experts0(nc, d, s, both, block)
                    block.tensor(columns)
                phase_scan(nc, d, s)
            phase_output0(nc, d, s)
        Scope.clear_all(nc)
        s.s1 = k.sb("s1", [P, NT, D])
        s.place, s.chosen = k.sb("place1", [P, NT, K1], U32), k.sb("chosen", [P, NT, K1])
        s.tile_expert = k.sb("tile_expert", [1, 2 * P], I32)
        phase_norm(nc, d, s, "n1", None, True)
        with ExitStack() as attention:
            k6 = Scope(nc, attention, "s6")
            s.v, s.o = k6.sb("v", [P, NT, D]), k6.sb("o", [P, NT, D])
            with ExitStack() as routing:
                k7 = Scope(nc, routing, "s7")
                s.one, s.number = k7.sb("one", [P, K1, NT, E1], BF16), k7.sb("number", [P, E1])
                phase_qkv(nc, d, s)
                phase_route1(nc, d, s)
            phase_attention(nc, d, s)
            phase_attention_out(nc, d, s)
        phase_experts1(nc, d, s)
        phase_combine1(nc, d, s)


def lay_out(inputs):
    w = {name: np.asarray(a) for name, a in inputs.items()}
    state = np.arange(P) % NS
    rows = lambda a: np.tile(a, (P, 1))
    f = {"x": w["L0_attn_x"], "ident": np.eye(P, dtype=np.float32)}
    f["wcat"] = np.concatenate([w["L0_attn_W_in"].T, w["L0_attn_W_dt"].T, w["L0_attn_W_B"].T, w["L0_attn_W_C"].T, w["L0_ffn_w_router"]], 1)
    f["b_dt"], f["dt_bias"] = rows(w["L0_attn_b_dt"]), rows(w["L0_attn_dt_bias"])
    freq = w["L0_attn_rope_freq"]
    f["freq"], f["freq_col"] = rows(freq), np.tile(freq, 2 * 4)[:, None]
    f["sign_col"] = np.where(state < HALF, 1.0, -1.0)[:, None]
    f["steps"] = np.arange(L).reshape(TQ, P).T
    f["steps_row"] = rows(np.arange(L))
    f["alog"] = np.tile(w["L0_attn_A_log"].T, (3, 1))
    at = np.arange(P)
    group = at // NS
    same = group[:, None] == group[None]
    f["eye_j"] = np.stack([np.eye(P), same & ((at[:, None] + HALF) % NS == state[None])], 1)
    f["mask4"] = group[:, None] == np.arange(4)[None]
    r = np.arange(3 * NS + 12)
    f["sel"] = np.where(r[:, None] < 3 * NS, r[:, None] % NS == state[None], (r[:, None] - 3 * NS) % 4 == group[None])
    f["tri"] = at[:, None] <= at[None]
    f["number"] = np.tile(np.arange(E0), (P, NT, 1))
    f["offset"] = np.broadcast_to((np.arange(NT) // (NT // G0) * E0 * C0)[None, :, None, None] + (np.arange(E0) * C0), (P, NT, 2, E0))
    f["wi"], f["wo"] = w["L0_ffn_wi"], w["L0_ffn_wo"]
    f["ln_w"], f["ln_b"] = rows(w["L0_attn_ln_w"]), rows(w["L0_attn_ln_b"])
    f["wout"] = w["L0_attn_W_out"].T
    q, key, v, o = (w["L1_attn_W_" + c].T for c in "qkvo")
    order = at % NH * DK + at // NH
    f["w_qkv"], f["w_o"] = np.stack([q[:, order], q[:, order ^ 1], key[:, order], key[:, order ^ 1], v], 1), o
    theta = np.float32(10000.0) ** (-2.0 * np.arange(DK // 2, dtype=np.float32) / np.float32(DK))
    angle = np.minimum(np.arange(L), 255).astype(np.float32)[:, None] * theta[None].astype(np.float32)
    pair = at // NH // 2
    f["rope_cos"] = np.cos(angle)[:, pair].T
    f["rope_sin"] = (np.sin(angle)[:, pair] * np.where(at // NH % 2 == 0, -1, 1)).T
    f["mask"] = np.stack([np.where(at[None] > at[:, None], NEG, 0), np.where(at[None] < at[:, None], NEG, 0)], 1)
    f["sel_w"] = np.tile(w["L1_ffn_expert_sel"].T, (1, 2))
    f["number1"] = rows(np.arange(E1))
    f["tile_no"] = 2 * at[:, None] + np.arange(2)
    f["keys_values"] = np.concatenate([w["L1_ffn_keys"], w["L1_ffn_values"]], 2)
    return {name: np.ascontiguousarray(a, dtype=np.float32) for name, a in f.items()}


def kernel(**inputs):
    import concourse.bacc as bacc
    from concourse.bass_utils import run_bass_kernel_spmd

    arrays = lay_out(inputs)
    nc = bacc.Bacc("TRN2", target_bir_lowering=False, num_devices=1)
    d = {name: nc.dram_tensor(name, a.shape, F32, kind="ExternalInput").ap() for name, a in arrays.items()}
    d["out"] = nc.dram_tensor("out", (B, L, D), F32, kind="ExternalOutput").ap()
    program(nc, d)
    r = run_bass_kernel_spmd(nc, [arrays], core_ids=[0])
    return r.results[0]["out"]
```
